# Optimizing a Trainium2 kernel written in Bass

```python
import numpy as np
import jax
import jax.numpy as jnp

def _softmax(x, axis=-1):
    return jax.nn.softmax(x, axis=axis)

def _gelu(x):
    return jax.nn.gelu(x, approximate=True)

def _silu(x):
    return jax.nn.silu(x)

def _sigmoid(x):
    return jax.nn.sigmoid(x)

def _layernorm(x, axis=-1, eps=1e-05):
    m = jnp.mean(x, axis=axis, keepdims=True)
    v = jnp.var(x, axis=axis, keepdims=True)
    return (x - m) / jnp.sqrt(v + eps)

def _scatter_add(tgt, idx, src, axis=0):
    return tgt.at[idx].add(src)

def _segment_sum(src, seg, n):
    return jax.ops.segment_sum(src, seg, n)
kernel_name = 'mk_decoder_preln_d1_seqx_r4_006ba0'

def setup_inputs(seed: int=0):
    np.random.seed(seed)
    _w = jnp.asarray

    def _rec_inputs():
        import jax
        import jax.numpy as jnp
        _rk = jax.random.key(seed)
        x = 7.22e-05 + 1 * jax.random.normal(jax.random.fold_in(_rk, 1), (32, 128, 512), jnp.float32)
        _lenS = 128 - jax.random.randint(jax.random.fold_in(_rk, 7), (32,), 0, max(1, 128 // 4) + 1, jnp.int32)
        _lenS2 = 128 - jax.random.randint(jax.random.fold_in(_rk, 8), (32,), 0, max(1, 128 // 4) + 1, jnp.int32)
        _ctx_512P = jax.random.normal(jax.random.fold_in(_rk, 11), (32, 16, 128), jnp.float32)
        _ctx_512c = jax.random.dirichlet(jax.random.fold_in(_rk, 511), 0.3 * jnp.ones((16,), jnp.float32), (32, 128))
        _ctx_512t = jnp.einsum('bsk,bkd->bsd', _ctx_512c, _ctx_512P)
        _ctx_512t = _ctx_512t * jax.lax.rsqrt(jnp.mean(jnp.square(_ctx_512t)) + 1e-12) * 0.953939
        ctx_512 = -0.000514642 + 1.00011 * (_ctx_512t + 0.3 * jax.random.normal(jax.random.fold_in(_rk, 611), (32, 128, 128), jnp.float32))
        return (x, ctx_512)
    x, ctx_512 = _rec_inputs()

    def _L0_attn_setup():
        import jax, jax.numpy as jnp
        import numpy as np
        B, S, D = (4, 1024, 512)
        IDENTITY_WEIGHT = 0.5
        ROT_DIM = D // 2

        def _layernorm(x, gamma, beta, eps=1e-05):
            mu = jnp.mean(x, axis=-1, keepdims=True)
            var = jnp.var(x, axis=-1, keepdims=True)
            return (x - mu) * jax.lax.rsqrt(var + eps) * gamma + beta

        def _rotary(t, rot_dim, theta=10000.0):
            seq = t.shape[-2]
            inv_freq = 1.0 / theta ** (jnp.arange(0, rot_dim, 2, dtype=jnp.float32) / rot_dim)
            freqs = jnp.arange(seq, dtype=jnp.float32)[:, None] * inv_freq[None, :]
            freqs = jnp.repeat(freqs, 2, axis=-1)
            cos, sin = (jnp.cos(freqs), jnp.sin(freqs))
            t_rot, t_pass = (t[..., :rot_dim], t[..., rot_dim:])
            x1, x2 = (t_rot[..., 0::2], t_rot[..., 1::2])
            rot_half = jnp.stack([-x2, x1], axis=-1).reshape(t_rot.shape)
            return jnp.concatenate([t_rot * cos + rot_half * sin, t_pass], axis=-1)

        def _cos_sim(x):
            return x / jnp.linalg.norm(x, axis=-1, keepdims=True)
        key = jax.random.key(seed)
        ks = jax.random.split(key, 3)
        scale = 0.02
        return {'X': jax.random.normal(ks[0], (B, S, D), jnp.float32), 'W_in': jax.random.normal(ks[1], (D, 3 * D), jnp.float32) * scale, 'b_in': jnp.zeros((3 * D,), jnp.float32), 'W_out': jax.random.normal(ks[2], (D, D), jnp.float32) * scale, 'b_out': jnp.zeros((D,), jnp.float32), 'gamma': jnp.ones((D,), jnp.float32), 'beta': jnp.zeros((D,), jnp.float32)}
    _L0_attn_all = _L0_attn_setup()
    _L0_attn_in = {k: v for k, v in _L0_attn_all.items() if k in ('W_in', 'b_in', 'W_out', 'b_out', 'gamma', 'beta')}
    del _L0_attn_all

    def _L0_xattn_setup():
        import jax, jax.numpy as jnp
        import numpy as np
        B, S, E = (2, 512, 512)
        QH, KVH = (32, 8)
        D = E // QH
        G = QH // KVH
        DROPOUT = 1.0
        key = jax.random.key(seed)
        k1, k2, k3 = jax.random.split(key, 3)
        q = jax.random.normal(k1, (B, S, E), dtype=jnp.float32)
        k = jax.random.normal(k2, (B, S, E // G), dtype=jnp.float32)
        v = jax.random.normal(k3, (B, S, E // G), dtype=jnp.float32)
        return {'q': q, 'k': k, 'v': v}
    _L0_xattn_all = _L0_xattn_setup()
    _L0_xattn_in = {k: v for k, v in _L0_xattn_all.items() if k in ()}
    del _L0_xattn_all

    def _L0_ffn_setup():
        import jax, jax.numpy as jnp
        import numpy as np
        E, R, K = (8, 8, 2)
        D, F = (512, 2048)
        B, S = (2, 512)
        SCALING = 16.0 / 8.0

        def act(x):
            return jax.nn.gelu(x, approximate=True)
        key = jax.random.key(seed)
        ks = jax.random.split(key, 12)
        return {'hidden_states': jax.random.normal(ks[0], (B, S, D), jnp.float32), 'W_r': jax.random.normal(ks[1], (E, D), jnp.float32) * 0.02, 'b_r': jnp.zeros((E,), jnp.float32), 'W1': jax.random.normal(ks[2], (F, D), jnp.float32) * 0.02, 'b1': jnp.zeros((F,), jnp.float32), 'W2': jax.random.normal(ks[3], (D, F), jnp.float32) * 0.02, 'b2': jnp.zeros((D,), jnp.float32), 'A1': jax.random.normal(ks[4], (E, R, D), jnp.float32) * 0.02, 'B1': jax.random.normal(ks[5], (F, R) * 1 + ()).reshape(1, F, R).repeat(1, 0) * 0.0 + jax.random.normal(ks[5], (E, F, R), jnp.float32) * 0.02, 'A2': jax.random.normal(ks[6], (E, R, F), jnp.float32) * 0.02, 'B2': jax.random.normal(ks[7], (E, D, R), jnp.float32) * 0.02}
    _L0_ffn_all = _L0_ffn_setup()
    _L0_ffn_in = {k: v for k, v in _L0_ffn_all.items() if k in ('W_r', 'b_r', 'W1', 'b1', 'W2', 'b2', 'A1', 'B1', 'A2', 'B2')}
    del _L0_ffn_all
    return {'x': x, 'ctx_512': ctx_512, 'L0_attn_W_in': _L0_attn_in['W_in'], 'L0_attn_b_in': _L0_attn_in['b_in'], 'L0_attn_W_out': _L0_attn_in['W_out'], 'L0_attn_b_out': _L0_attn_in['b_out'], 'L0_attn_gamma': _L0_attn_in['gamma'], 'L0_attn_beta': _L0_attn_in['beta'], 'L0_ffn_W_r': _L0_ffn_in['W_r'], 'L0_ffn_b_r': _L0_ffn_in['b_r'], 'L0_ffn_W1': _L0_ffn_in['W1'], 'L0_ffn_b1': _L0_ffn_in['b1'], 'L0_ffn_W2': _L0_ffn_in['W2'], 'L0_ffn_b2': _L0_ffn_in['b2'], 'L0_ffn_A1': _L0_ffn_in['A1'], 'L0_ffn_B1': _L0_ffn_in['B1'], 'L0_ffn_A2': _L0_ffn_in['A2'], 'L0_ffn_B2': _L0_ffn_in['B2']}

def reference(x, ctx_512, L0_attn_W_in, L0_attn_b_in, L0_attn_W_out, L0_attn_b_out, L0_attn_gamma, L0_attn_beta, L0_ffn_W_r, L0_ffn_b_r, L0_ffn_W1, L0_ffn_b1, L0_ffn_W2, L0_ffn_b2, L0_ffn_A1, L0_ffn_B1, L0_ffn_A2, L0_ffn_B2):
    import jax
    import jax.numpy as jnp

    def _L0_attn_ref(X, W_in, b_in, W_out, b_out, gamma, beta):
        import jax, jax.numpy as jnp
        import numpy as np
        B, S, D = (4, 1024, 512)
        IDENTITY_WEIGHT = 0.5
        ROT_DIM = D // 2

        def _layernorm(x, gamma, beta, eps=1e-05):
            mu = jnp.mean(x, axis=-1, keepdims=True)
            var = jnp.var(x, axis=-1, keepdims=True)
            return (x - mu) * jax.lax.rsqrt(var + eps) * gamma + beta

        def _rotary(t, rot_dim, theta=10000.0):
            seq = t.shape[-2]
            inv_freq = 1.0 / theta ** (jnp.arange(0, rot_dim, 2, dtype=jnp.float32) / rot_dim)
            freqs = jnp.arange(seq, dtype=jnp.float32)[:, None] * inv_freq[None, :]
            freqs = jnp.repeat(freqs, 2, axis=-1)
            cos, sin = (jnp.cos(freqs), jnp.sin(freqs))
            t_rot, t_pass = (t[..., :rot_dim], t[..., rot_dim:])
            x1, x2 = (t_rot[..., 0::2], t_rot[..., 1::2])
            rot_half = jnp.stack([-x2, x1], axis=-1).reshape(t_rot.shape)
            return jnp.concatenate([t_rot * cos + rot_half * sin, t_pass], axis=-1)

        def _cos_sim(x):
            return x / jnp.linalg.norm(x, axis=-1, keepdims=True)
        Xn = _layernorm(X, gamma, beta)
        QKV = Xn @ W_in + b_in
        Q, K, V = jnp.split(QKV, 3, axis=-1)
        K = _rotary(K, ROT_DIM)
        V = _rotary(V, ROT_DIM)
        A = jnp.sum(_cos_sim(K) * _cos_sim(V), axis=-2)
        A = (1.0 - IDENTITY_WEIGHT) * A + IDENTITY_WEIGHT
        Y = A[:, None, :] * Q
        Y = Y @ W_out + b_out
        return Y + X

    def _L0_xattn_ref(q, k, v):
        import jax, jax.numpy as jnp
        import numpy as np
        B, S, E = (2, 512, 512)
        QH, KVH = (32, 8)
        D = E // QH
        G = QH // KVH
        DROPOUT = 1.0
        b, s, _ = q.shape
        qh = q.reshape(b, s, KVH, G, D).transpose(0, 2, 3, 1, 4)
        kh = k.reshape(b, s, KVH, D).transpose(0, 2, 1, 3)
        vh = v.reshape(b, s, KVH, D).transpose(0, 2, 1, 3)
        scale = 1.0 / jnp.sqrt(jnp.float32(D))
        scores = jnp.einsum('bkgsd,bktd->bkgst', qh, kh) * scale
        attn = jax.nn.softmax(scores, axis=-1) / DROPOUT
        out = jnp.einsum('bkgst,bktd->bkgsd', attn, vh)
        return out.transpose(0, 3, 1, 2, 4).reshape(b, s, E)

    def _L0_ffn_ref(hidden_states, W_r, b_r, W1, b1, W2, b2, A1, B1, A2, B2):
        import jax, jax.numpy as jnp
        import numpy as np
        E, R, K = (8, 8, 2)
        D, F = (512, 2048)
        B, S = (2, 512)
        SCALING = 16.0 / 8.0

        def act(x):
            return jax.nn.gelu(x, approximate=True)
        b, s, d = hidden_states.shape
        N = b * s
        x = hidden_states.reshape(N, d)
        probs = jax.nn.softmax(x @ W_r.T + b_r, axis=-1)
        w_topk, idx_topk = jax.lax.top_k(probs, K)
        base1 = x @ W1.T + b1
        u1 = jnp.einsum('nd,erd->ner', x, A1)
        B1_rf = B1.transpose(0, 2, 1).reshape(E * R, F)
        B2_rf = B2.transpose(0, 2, 1).reshape(E * R, d)
        res = jnp.zeros((N, d), hidden_states.dtype)
        for k in range(K):
            oh = jax.nn.one_hot(idx_topk[:, k], E, dtype=x.dtype)
            z1 = (u1 * oh[:, :, None]).reshape(N, E * R)
            h = act(base1 + z1 @ B1_rf * SCALING)
            u2 = jnp.einsum('nf,erf->ner', h, A2)
            z2 = (u2 * oh[:, :, None]).reshape(N, E * R)
            y = h @ W2.T + b2 + z2 @ B2_rf * SCALING
            res = res + w_topk[:, k:k + 1] * y
        return res.reshape(b, s, d)
    x = x + _L0_attn_ref(_layernorm(x, axis=-1), L0_attn_W_in, L0_attn_b_in, L0_attn_W_out, L0_attn_b_out, L0_attn_gamma, L0_attn_beta)
    x = x + _L0_xattn_ref(_layernorm(x, axis=-1), ctx_512, ctx_512)
    x = x + _L0_ffn_ref(_layernorm(x, axis=-1), L0_ffn_W_r, L0_ffn_b_r, L0_ffn_W1, L0_ffn_b1, L0_ffn_W2, L0_ffn_b2, L0_ffn_A1, L0_ffn_B1, L0_ffn_A2, L0_ffn_B2)
    return x

_drawn_inputs = setup_inputs


def setup_inputs(seed=0):
    import zlib

    import numpy as np

    out = dict(_drawn_inputs(seed))
    spreads = {'L0_attn_b_in': (0.0, 0.711),
     'L0_attn_b_out': (0.0, 0.1),
     'L0_attn_gamma': (1.0, 0.6),
     'L0_attn_beta': (0.0, 0.8),
     'L0_ffn_b_r': (0.0, 0.8),
     'L0_ffn_b1': (0.0, 0.8),
     'L0_ffn_b2': (0.0, 0.466)}
    factors = {'L0_ffn_W_r': 7.525,
     'L0_ffn_A1': 8.0,
     'L0_ffn_B1': 8.0,
     'L0_ffn_A2': 8.0,
     'L0_ffn_B2': 8.0}
    for name, (base, spread) in spreads.items():
        noise = np.random.default_rng([zlib.crc32(name.encode()), seed]).standard_normal(out[name].shape)
        drawn = base * np.exp(spread * noise) if base else spread * noise
        out[name] = jnp.asarray(drawn.astype(out[name].dtype))
    for name, factor in factors.items():
        out[name] = (out[name] * factor).astype(out[name].dtype)
    return out
```

```python
from contextlib import ExitStack

import numpy as np
import concourse.bass as bass
from concourse import mybir

F32 = mybir.dt.float32
F16 = mybir.dt.float16
ALU = mybir.AluOpType
ACT = mybir.ActivationFunctionType
AX = mybir.AxisListType

P = 128
BATCH, S, D = 32, 128, 512
GB = 2
NG = BATCH // GB
T = GB * S
KC = D // P
F = 2048
FC = F // P
NH, KVH, DH = 32, 8, 16
HPG = NH // KVH
PAIRS = NH // 2
SLOT = 64
NE, R = 8, 8
ER = NE * R
U1W = ER + NE
ROT = D // 2
EPS = 1e-5
SCORE_SCALE = DH ** -0.5
IDENTITY_WEIGHT = 0.5
LORA_SCALE = 2.0
HUGE = 3.0e38
SX = 2.0 ** 6
SW = 2.0 ** 10
SQ = 2.0 ** 4
SA = 2.0 ** 10
SM = 2.0 ** 6
SH = 2.0 ** 4


class Signal:

    def __init__(self, sem, per_group, by=1):
        self.sem, self.per_group, self.by = sem, per_group, by

    def count(self, g, k=None):
        k = self.per_group if k is None else k
        return g * (self.per_group * self.by) + k * self.by


class Chain:

    def __init__(self, eng, sig):
        self.eng, self.sig, self.g, self.n = eng, sig, 0, 0

    def begin(self, g):
        self.g, self.n = g, 0

    def link(self, instruction):
        self.n += 1
        instruction.then_inc(self.sig.sem, 1)
        self.eng.wait_ge(self.sig.sem, self.sig.count(self.g, self.n))

    def end(self):
        assert self.n == self.sig.per_group, (self.sig.sem, self.n)


def build(nc, x_d, ctxT_d, ctx_d, w_in_d, b_q_d, b_kv_d, w_out_d, b_out_d, gamma_d, beta_d,
          a1r_d, b_r_d, w1t_d, b1_d, w2t_d, b2_d, b1t_d, a2t_d, b2t_d, cos_d, sin_d, kform_d,
          out_d):
    ctx = ExitStack()
    with ctx:
        def sb(name, shape, dt=F32):
            return ctx.enter_context(nc.sbuf_tensor(name, shape, dt))

        def sem(name):
            return ctx.enter_context(nc.semaphore(name))

        def sig(name, per_group, by=1):
            return Signal(sem(name), per_group, by)

        w_in = sb("w_in", [P, 2, KC, 3 * D], F16)
        w_out = sb("w_out", [P, 2, KC, D], F16)
        w1 = sb("w1", [P, 2, KC, F], F16)
        w2 = sb("w2", [P, 2, FC, D], F16)
        a1r = sb("a1r", [P, KC, 2, U1W], F16)
        a2 = sb("a2", [P, FC, 2, ER], F16)
        lb1h = sb("lb1h", [P, F], F16)
        lb1l = sb("lb1l", [ER, F], F16)
        lb2h = sb("lb2h", [P, D], F16)
        lb2l = sb("lb2l", [ER, D], F16)
        bkv = sb("bkv", [P, 2 * D])
        bout = sb("bout", [P, D])
        b2b = sb("b2b", [P, D])
        brb = sb("brb", [P, NE])
        bq = sb("bq", [P, KC])
        b1c = sb("b1c", [P, FC])
        gamma = sb("gamma", [P, KC])
        beta = sb("beta", [P, KC])
        cos = sb("cos", [P, ROT])
        sin = sb("sin", [P, ROT])
        kform = sb("kform", [P, 3])
        idf = sb("idf", [P, P])
        idb = sb("idb", [P, P], F16)
        ones = sb("ones", [P, P])
        small = sb("small", [P, 4, GB])
        lnsa = sb("lnsa", [P, 1])
        gammaS = sb("gammaS", [P, KC])
        descend = sb("descend", [P, NE])
        X = sb("X", [P, GB, D])
        XF = sb("XF", [P, GB, D])
        stat = sb("stat", [P, GB, 6])
        mv = sb("mv", [P, 3, GB, 2])
        nrm = sb("nrm", [P, 10, GB])
        XN = sb("XN", [P, GB, D])
        beta_b = XN[:, 0, :].rearrange("p (k n) -> p k n", k=KC)
        junk = XN[:, 1, 0:D // 2].bitcast(F16)
        xnT = sb("xnT", [P, 2, KC, T], F16)
        kst = xnT[:, :, :, :].rearrange("p a k t -> p (a k t)").bitcast(F32)
        KV = sb("KV", [P, GB, 2, D])
        PR = KV[:, :, 0, :]
        QxT = KV[:, 0, :, :].rearrange("p h n -> p (h n)").bitcast(F16).rearrange("p (q t) -> p q t", t=P)
        khi = KV[:, 1, 0, :].bitcast(F16)
        ON = KV[:, 1, 1, :].rearrange("p (h n) -> p h n", h=2)
        kfm = sb("kfm", [P, KVH * P])
        rotc = kfm[:, 0:2 * ROT].rearrange("p (h n) -> p h n", h=2)
        rots = kfm[:, 2 * ROT:4 * ROT].rearrange("p (h n) -> p h n", h=2)
        EX = sb("EX", [P, 2, HPG * P])
        prs = EX[:, :, :].rearrange("p b n -> p (b n)").bitcast(F16).rearrange("p (b h n) -> p b h n", b=GB, h=2)
        ss = sb("ss", [P, GB, 2])
        wn = sb("wn", [P, GB])
        ones16 = sb("ones16", [P, 1], F16)
        asum = sb("asum", [P, GB, KC])
        acol = sb("acol", [P, GB, KC])
        bqa = sb("bqa", [P, GB, KC])
        QA = sb("QA", [P, KC, T])
        Q2 = QA[:, :, :].rearrange("p k t -> p (k t)").rearrange("p (b n) -> p b n", b=GB)
        qas = sb("qas", [P, 2, KC, T], F16)
        exh, exl = (qas[:, i].rearrange("p k t -> p (k t)").rearrange("p (b n) -> p b n", b=2) for i in range(2))
        kx = sb("kx", [P, KVH, 2, P], F16)
        vst = sb("vst", [P, GB, P])
        vx = sb("vx", [P, KVH, 2 * DH + 1], F16)
        Qx = sb("Qx", [P, NH, SLOT], F16)
        negm = sb("negm", [P, NH])
        mparts = sb("mparts", [P, 4, 2, PAIRS], F16)
        fence = sb("fence", [P, 1])
        mT = sb("mT", [2 * NH, P], F16)
        rl = sb("rl", [P, 2, NH // 2])
        h3T = sb("h3T", [P, 2, KC, T], F16)
        rt = sb("rt", [P, GB, U1W])
        lg = sb("lg", [P, GB, NE])
        top = sb("top", [P, 5, GB])
        sel = sb("sel", [P, 8, GB, NE])
        sume = sb("sume", [P, GB])
        rho = sb("rho", [P, GB])
        w1st = sb("w1st", [P, GB])
        rho1 = sb("rho1", [P, GB])
        zf = kfm[:, 0:2 * GB * ER].rearrange("p (b k e) -> p b k e", b=GB, k=2)
        zz = kfm[:, 2 * GB * ER:4 * GB * ER].bitcast(F16).rearrange("p (b k h e) -> p b k h e", b=GB, k=2, h=2)
        drho = kfm[:, 4 * GB * ER:4 * GB * ER + GB * P].rearrange("p (b n) -> p b n", b=GB)
        zT = sb("zT", [P, 2, T], F16)
        rhoB = sb("rhoB", [P, T])
        OUT = sb("OUT", [P, GB, D])
        H1, H2 = (OUT[:, i, :].rearrange("p (s t) -> p s t", s=2) for i in range(2))
        T2 = sb("T2", [P, 2, T])
        t2s = sb("t2s", [P, 2, 2, T], F16)
        HS = sb("HS", [P, 2, T])
        hs = sb("hs", [P, 2, FC, T], F16)
        u2, us, z2f, z2g = (T2[:, i // 2, (i % 2) * GB * ER:(i % 2 + 1) * GB * ER].rearrange("p (b e) -> p b e", b=GB)
                            for i in range(4))
        z2s = sb("z2s", [P, GB, 2, ER], F16)
        z2T = sb("z2T", [P, GB, P], F16)
        stage = hs[:, :, :, :].rearrange("p a c t -> p (a c t)").bitcast(F32)

        banks = [ctx.enter_context(nc.psum_tensor(f"bank{i}", [P, 512], F32)) for i in range(8)]
        FB, UB, AB = banks[0:2], banks[2], banks[3:8]
        UBv = UB[:, :].rearrange("p (b h e) -> p b h e", b=4, h=2)

        s_small = sem("small_loaded")
        s_const = sem("constants_made")
        s_stage = [sem(f"stage{i}_loaded") for i in range(2)]
        s_hi = sem("weight_high_made")
        s_lo = sem("weight_low_made")
        s_beta = sem("beta_product_done")
        s_bias = sem("bias_folded")
        s_pconst = sem("pool_constants_made")
        x_in = sig("x_loaded", 1, 16)
        k_in = sig("k_loaded", 8 * GB, 16)
        v_in = sig("v_loaded", 1, 16)
        stats1 = sig("stats1_ready", GB)
        norm1 = sig("norm1_ready", 1)
        xn_rdy = sig("xn_ready", GB)
        base_rdy = sig("base_ready", GB)
        bo_added = sig("bout_added", GB)
        xnT_ps = sig("xnT_in_psum", GB)
        xn_hi = sig("xnT_high_ready", GB)
        xn_lo = sig("xnT_low_ready", GB)
        kv_ps = sig("kv_in_psum", GB)
        kv_rdy = sig("kv_biased", 2 * GB)
        rot_done = sig("kv_rotated", GB)
        norms = sig("kv_norms_ready", 2 * GB)
        pr_rdy = sig("kv_product_ready", GB)
        pr_hi = sig("kv_product_high", GB)
        pr_lo = sig("kv_product_low", GB)
        wn_rdy = sig("weights_of_tokens_ready", GB)
        a_ps = sig("a_in_psum", GB)
        a_rdy = sig("a_ready", 1)
        q_ps = sig("q_in_psum", 2)
        qa_rdy = sig("qa_ready", KC * GB)
        qa_hi = sig("qa_high", 1)
        qa_lo = sig("qa_low", 1)
        y_ps = sig("y_in_psum", GB)
        x1_rdy = sig("x1_ready", GB)
        stats2 = sig("stats2_ready", GB)
        norm2 = sig("norm2_ready", GB)
        q2_rdy = sig("q_normed", GB)
        qx_hi = sig("qx_high", GB)
        qx_lo = sig("qx_low", GB)
        k_hi = sig("k_high", GB)
        k_fm = sig("k_formed", GB)
        kx_a = sig("kx_first_half", GB)
        kx_b = sig("kx_second_half", GB)
        v_hi = sig("v_high", GB)
        v_lo = sig("v_low", GB)
        qxT_ps = sig("qxT_in_psum", 2 * GB)
        qxT_rdy = sig("qxT_ready", 2 * GB)
        sc_ps = sig("scores_for_max_in_psum", KVH * GB)
        max_done = sig("max_taken", KVH * GB)
        mp_rdy = sig("max_parts_ready", GB)
        mT_ps = sig("maxT_in_psum", GB)
        mT_rdy = sig("maxT_ready", GB)
        m_in = sig("max_rows_placed", 4 * GB, 16)
        st_ps = sig("shifted_scores_in_psum", KVH * GB)
        ex_rdy = sig("exp_ready", KVH * GB)
        ex_hi = sig("exp_high", KVH * GB)
        ex_lo = sig("exp_low", KVH * GB)
        pv_done = sig("pv_done", KVH * GB)
        on_rdy = sig("attention_normed", 2 * GB)
        x2_rdy = sig("x2_ready", 2 * GB)
        stats3 = sig("stats3_ready", GB)
        norm3 = sig("norm3_ready", GB)
        h3_rdy = sig("h3_ready", GB)
        h3T_ps = sig("h3T_in_psum", GB)
        h3_hi = sig("h3T_high", GB)
        h3_lo = sig("h3T_low", GB)
        u1_ps = sig("u1_in_psum", GB)
        top_rdy = sig("top_logits_ready", 1)
        rho_rdy = sig("rho_ready", 2 * GB)
        zz_rdy = sig("z_parts_ready", 1)
        zT_ps = sig("zT_in_psum", 1)
        zT_rdy = sig("zT_ready", 1)
        drho_rdy = sig("rho_diagonal_ready", GB)
        rho_ps = sig("rho_rows_in_psum", 1)
        rhoB_rdy = sig("rho_rows_ready", 1)
        dve_at = sig("vector_step_attention", 37)
        pool_at = sig("pool_step_attention", 23)
        f1_ps = sig("hidden1_in_psum", FC)
        h1_rdy = sig("hidden1_ready", FC)
        f2_ps = sig("hidden2_in_psum", FC)
        h2_rdy = sig("hidden2_ready", FC)
        t2_rdy = sig("weighted2_ready", FC)
        t2_hi = sig("weighted2_high", FC)
        t2_lo = sig("weighted2_low", FC)
        hs_rdy = sig("hidden_sum_ready", FC)
        hs_hi = sig("hidden_sum_high", FC)
        hs_lo = sig("hidden_sum_low", FC)
        u2_used = sig("u2_product_done", FC)
        u2_ev = sig("u2_read", 1)
        us_ps = sig("us_in_psum", 1)
        us_ev = sig("us_read", 1)
        z2_rdy = sig("z2_parts_ready", 1)
        z2T_ps = sig("z2T_in_psum", 1)
        z2T_rdy = sig("z2T_ready", 1)
        yf_ps = sig("ffn_out_in_psum", GB)
        out_rdy = sig("out_ready", GB)
        out_st = sig("out_stored", GB, 16)
        dve_ff = sig("vector_step_ffn", 7)

        w_in_v = w_in_d.rearrange("(k p) n -> p k n", p=P)
        w1_v = w1t_d.rearrange("(k p) n -> p k n", p=P)
        w2_v = w2t_d.rearrange("(k p) n -> p k n", p=P)
        pieces = []
        for k in range(KC):
            pieces.append(([((0, P), w_in_v[:, k, :])], (3 * D,), w_in[:, 0, k, :], w_in[:, 1, k, :], gammaS[:, k:k + 1]))
        pieces.append(([((0, P), w_out_d.rearrange("(k p) n -> p k n", p=P))], (KC, D), w_out[:, 0], w_out[:, 1], SW))
        pieces.append(([((0, P), a1r_d.rearrange("(k p) n -> p k n", p=P))], (KC, U1W), a1r[:, :, 0, :], a1r[:, :, 1, :], SW))
        pieces.append(([((0, ER), b1t_d), ((ER, P), b1t_d)], (F,), lb1h[:, :], lb1l[:, :], LORA_SCALE * SW))
        pieces.append(([((0, ER), b2t_d), ((ER, P), b2t_d)], (D,), lb2h[:, :], lb2l[:, :], LORA_SCALE * SW))
        pieces.append(([((0, P), a2t_d.rearrange("(c p) n -> p c n", p=P))], (FC, ER), a2[:, :, 0, :], a2[:, :, 1, :], SW))
        for k in range(KC):
            pieces.append(([((0, P), w1_v[:, k, :])], (F,), w1[:, 0, k, :], w1[:, 1, k, :], SW))
        for k in range(KC):
            pieces.append(([((0, P), w2_v[:, 4 * k:4 * k + 4, :])], (4, D), w2[:, 0, 4 * k:4 * k + 4, :], w2[:, 1, 4 * k:4 * k + 4, :], SW))

        def staged(i, rows=P):
            shape = pieces[i][1]
            n = int(np.prod(shape))
            v = stage[0:rows, (i % 2) * 2048:(i % 2) * 2048 + n]
            return v.rearrange("p (a n) -> p a n", a=shape[0]) if len(shape) == 2 else v

        loads_of = [len(p[0]) for p in pieces]

        def stage_count(i):
            return 16 * sum(loads_of[j] for j in range(i % 2, i + 1, 2))

        block = ctx.enter_context(nc.Block())

        @block.sync
        def _(sp):
            for dst, src in ((gamma[:, :], gamma_d),
                             (beta[:, :], beta_d),
                             (bq[:, :], b_q_d),
                             (b1c[:, :], b1_d),
                             (bkv[:, :], b_kv_d.partition_broadcast(P)),
                             (bout[:, :], b_out_d.partition_broadcast(P)),
                             (b2b[:, :], b2_d.partition_broadcast(P)),
                             (brb[:, :], b_r_d.partition_broadcast(P)),
                             (cos[:, :], cos_d), (sin[:, :], sin_d), (kform[:, :], kform_d)):
                sp.dma_start(dst, src).then_inc(s_small, 16)

            def load_group(g):
                if not (isinstance(g, int) and g == 0):
                    sp.wait_ge(x2_rdy.sem, x2_rdy.count(g - 1))
                sp.dma_start(X[:, :, :], x_d[bass.ds(g * GB, GB)].rearrange("b s d -> s b d")).then_inc(x_in.sem, 16)
                if not (isinstance(g, int) and g == 0):
                    sp.wait_ge(v_lo.sem, v_lo.count(g - 1))
                sp.dma_start(vst[:, :, :], ctx_d[bass.ds(g * GB, GB)].rearrange("b t n -> t b n")).then_inc(v_in.sem, 16)

            def load_keys(g, b):
                if b == 0:
                    sp.wait_ge(q_ps.sem, q_ps.count(g))
                else:
                    sp.wait_ge(k_fm.sem, k_fm.count(g, b))
                    sp.wait_ge(k_hi.sem, k_hi.count(g, b))
                for r in range(8):
                    sp.dma_start(kst[16 * r:16 * r + 16, :].unsqueeze(1),
                                 ctxT_d[bass.ds(g * GB + b, 1)].rearrange("b d n -> d b n")).then_inc(k_in.sem, 16)

            def place_max(g, b):
                sp.wait_ge(mT_rdy.sem, mT_rdy.count(g, b + 1))
                for part in range(2):
                    for parity in range(2):
                        row = SLOT * parity + 3 * DH + part
                        src = mT[NH * part + PAIRS * parity:NH * part + PAIRS * (parity + 1), :]
                        sp.dma_start(QxT[row:row + 1, :, :], src).then_inc(m_in.sem, 16)

            def attention(g):
                load_group(g)
                for b in range(GB):
                    load_keys(g, b)
                    place_max(g, b)

            def ffn(g):
                for b in range(GB):
                    sp.wait_ge(out_rdy.sem, out_rdy.count(g, b + 1))
                    sp.dma_start(out_d[bass.ds(g * GB + b, 1)].rearrange("b s d -> s b d"), OUT[:, b:b + 1, :]).then_inc(out_st.sem, 16)

            for i, (loads, shape, hi, lo, scale) in enumerate(pieces):
                if i >= 2:
                    sp.wait_ge(s_lo, i - 1)
                    sp.wait_ge(s_hi, i - 1)
                    if i - 2 < KC:
                        sp.wait_ge(s_beta, i - 1)
                for (r0, r1), src in loads:
                    v = staged(i)
                    sp.dma_start(v[r0:r1], src).then_inc(s_stage[i % 2], 16)
            attention(0)
            with sp.Fori(0, NG - 1) as i:
                attention(i + 1)
                ffn(i)
            ffn(NG - 1)
            sp.wait_ge(out_st.sem, out_st.count(NG - 1))

        @block.gpsimd
        def _(pool):
            pool.memset(idf[:, :], 0.0).then_inc(s_pconst, 1)
            pool.memset(idb[:, :], 0.0).then_inc(s_pconst, 1)
            for i, v in enumerate((EPS, -0.5, -1.0, SA)):
                pool.memset(small[:, i, :], v).then_inc(s_pconst, 1)
            pool.wait_ge(s_pconst, N_PCONST - 2)
            for m in (idf, idb):
                pool.affine_select(out=m[:, :], in_=m[:, :], compare_op=ALU.not_equal, fill=1.0, base=0,
                                   pattern=[[-1, P]], channel_multiplier=1).then_inc(s_pconst, 1)
            pool.wait_ge(s_const, N_CONST)
            pool.wait_ge(s_small, 16 * N_SMALL)
            chain = Chain(pool, pool_at)
            link = chain.link

            def rsqrt(dst, src, n):
                link(pool.tensor_tensor(nrm[:, 7, 0:n], src, small[:, 0, 0:n], ALU.add))
                return pool.tensor_tensor(dst, nrm[:, 7, 0:n], small[:, 1, 0:n], ALU.pow)

            def norm_scales(g):
                chain.begin(g)
                pool.wait_ge(stats1.sem, stats1.count(g))
                mean, var = mv[:, 0, :, 0], mv[:, 0, :, 1]
                link(rsqrt(nrm[:, 0, :], var, GB))
                link(pool.tensor_tensor(nrm[:, 1, :], nrm[:, 0, :], nrm[:, 0, :], ALU.mult))
                link(pool.tensor_tensor(nrm[:, 2, :], nrm[:, 1, :], var, ALU.mult))
                link(rsqrt(nrm[:, 3, :], nrm[:, 2, :], GB))
                link(pool.tensor_tensor(nrm[:, 4, :], nrm[:, 3, :], nrm[:, 0, :], ALU.mult))
                link(pool.tensor_tensor(nrm[:, 1, :], nrm[:, 0, :], mean, ALU.mult))
                link(pool.tensor_tensor(nrm[:, 5, :], nrm[:, 1, :], small[:, 2, :], ALU.mult))
                pool.tensor_tensor(nrm[:, 6, :], nrm[:, 0, :], ones[:, 0:GB], ALU.add).then_inc(norm1.sem, 1)

            def add_bout(g, b):
                pool.wait_ge(base_rdy.sem, base_rdy.count(g, b + 1))
                pool.tensor_tensor(X[:, b, :], X[:, b, :], bout[:, :], ALU.add).then_inc(bo_added.sem, 1)

            def rotate(g, b):
                pool.wait_ge(kv_rdy.sem, kv_rdy.count(g, 2 * (b + 1)))
                rot = KV[:, b, :, 0:ROT]
                link(pool.tensor_tensor(rotc[:, :, :], rot, cos[:, :].unsqueeze(1).to_broadcast([P, 2, ROT]), ALU.mult))
                for o in range(2):
                    link(pool.tensor_tensor(rots[:, :, o::2], KV[:, b, :, 1 - o:ROT:2],
                                            sin[:, o::2].unsqueeze(1).to_broadcast([P, 2, ROT // 2]), ALU.mult))
                pool.tensor_tensor(rot, rotc[:, :, :], rots[:, :, :], ALU.add).then_inc(rot_done.sem, 1)
                pool.wait_ge(rot_done.sem, rot_done.count(g, b + 1))
                pool.wait_ge(norms.sem, norms.count(g, 2 * (b + 1)))
                pool.tensor_tensor(PR[:, b, :], KV[:, b, 0, :], KV[:, b, 1, :], ALU.mult).then_inc(pr_rdy.sem, 1)

            def token_weights(g, b):
                pool.wait_ge(norms.sem, norms.count(g, 2 * (b + 1)))
                link(pool.tensor_tensor(wn[:, b:b + 1], ss[:, b, 0:1], ss[:, b, 1:2], ALU.mult))
                link(pool.tensor_tensor(wn[:, b:b + 1], wn[:, b:b + 1], small[:, 1, 0:1], ALU.pow))
                pool.tensor_tensor(wn[:, b:b + 1], wn[:, b:b + 1], small[:, 3, 0:1], ALU.mult).then_inc(wn_rdy.sem, 1)

            def form_keys(g, b):
                pool.wait_ge(k_fm.sem, k_fm.count(g, b + 1))
                pool.wait_ge(k_hi.sem, k_hi.count(g, b + 1))
                if b >= 1:
                    pool.wait_ge(pv_done.sem, pv_done.count(g, KVH * b))
                pool.tensor_tensor(kx[0:SLOT, :, 0, :], kfm[0:SLOT, :].rearrange("p (g t) -> p g t", g=KVH),
                                          khi[0:SLOT, :].rearrange("p (g t) -> p g t", g=KVH), ALU.subtract).then_inc(kx_a.sem, 1)

            def query_norm(g, b):
                pool.wait_ge(stats2.sem, stats2.count(g, b + 1))
                rsqrt(nrm[:, 8, b:b + 1], mv[:, 1, b, 1:2], 1).then_inc(norm2.sem, 1)

            def low_exp(g, b, u):
                n = KVH * b + u
                pool.wait_ge(ex_hi.sem, ex_hi.count(g, n + 1))
                if n >= 2:
                    pool.wait_ge(pv_done.sem, pv_done.count(g, n - 1))
                pool.tensor_tensor(exl[:, n % 2, :], EX[:, n % 2, :], exh[:, n % 2, :], ALU.subtract).then_inc(ex_lo.sem, 1)

            def ffn_norm(g, b):
                pool.wait_ge(stats3.sem, stats3.count(g, b + 1))
                rsqrt(nrm[:, 9, b:b + 1], mv[:, 2, b, 1:2], 1).then_inc(norm3.sem, 1)

            def attention(g):
                norm_scales(g)
                for b in range(GB):
                    add_bout(g, b)
                for b in range(GB):
                    rotate(g, b)
                    token_weights(g, b)
                for b in range(GB):
                    query_norm(g, b)
                for b in range(GB):
                    form_keys(g, b)
                    for u in range(KVH):
                        low_exp(g, b, u)
                    ffn_norm(g, b)
                chain.end()

            def ffn(g):
                for c in range(FC):
                    pool.wait_ge(hs_hi.sem, hs_hi.count(g, c + 1))
                    pool.tensor_tensor(hs[:, 1, c, :], HS[:, c % 2, :], hs[:, 0, c, :], ALU.subtract).then_inc(hs_lo.sem, 1)

            attention(0)
            with pool.Fori(0, NG - 1) as i:
                ffn(i)
                attention(i + 1)
            ffn(NG - 1)

        @block.scalar
        def _(act):
            act.wait_ge(s_small, 16 * N_SMALL)
            act.wait_ge(s_const, N_CONST)
            act.wait_ge(s_pconst, N_PCONST)
            for i, (loads, shape, hi, lo, scale) in enumerate(pieces):
                act.wait_ge(s_stage[i % 2], stage_count(i))
                act.activation(hi, staged(i), ACT.Copy, scale=scale).then_inc(s_hi, 1)

            def high_xn(g, b):
                act.wait_ge(xnT_ps.sem, xnT_ps.count(g, b + 1))
                act.activation(xnT[:, 0, :, b * S:(b + 1) * S], AB[b][:, :].rearrange("p (k t) -> p k t", k=KC), ACT.Copy, scale=SX).then_inc(xn_hi.sem, 1)

            def kv_norms(g, b):
                act.wait_ge(rot_done.sem, rot_done.count(g, b + 1))
                for o in range(2):
                    act.activation(junk[:, :], KV[:, b, o, :], ACT.Square, accum_out=ss[:, b, o:o + 1]).then_inc(norms.sem, 1)
                    act.wait_ge(norms.sem, norms.count(g, 2 * b + o + 1))
                act.wait_ge(pr_rdy.sem, pr_rdy.count(g, b + 1))
                act.wait_ge(wn_rdy.sem, wn_rdy.count(g, b + 1))
                act.activation(prs[:, b, 0, :], PR[:, b, :], ACT.Copy, scale=wn[:, b:b + 1]).then_inc(pr_hi.sem, 1)

            def scale_q(g):
                act.wait_ge(a_rdy.sem, a_rdy.count(g))
                for c in range(KC):
                    act.wait_ge(q_ps.sem, q_ps.count(g, c // 2 + 1))
                    for b in range(GB):
                        src = AB[1 + c // 2][:, (c % 2) * T + b * S:(c % 2) * T + (b + 1) * S]
                        act.activation(QA[:, c, b * S:(b + 1) * S], src, ACT.Identity,
                                              scale=acol[:, b, c:c + 1], bias=bqa[:, b, c:c + 1]).then_inc(qa_rdy.sem, 1)
                act.wait_ge(qa_rdy.sem, qa_rdy.count(g))
                act.activation(qas[:, 0], QA[:, :, :], ACT.Copy).then_inc(qa_hi.sem, 1)

            def high_kv(g, b):
                act.wait_ge(k_in.sem, k_in.count(g, 8 * (b + 1)))
                act.wait_ge(v_in.sem, v_in.count(g))
                if b >= 1:
                    act.wait_ge(kx_a.sem, kx_a.count(g, b))
                    act.wait_ge(kx_b.sem, kx_b.count(g, b))
                    act.wait_ge(pv_done.sem, pv_done.count(g, KVH * b))
                act.activation(khi[:, :], kst[:, :], ACT.Copy, scale=kform[:, 0:1]).then_inc(k_hi.sem, 1)
                act.activation(kfm[:, :], kst[:, :], ACT.Identity, scale=kform[:, 1:2], bias=kform[:, 2:3]).then_inc(k_fm.sem, 1)
                act.activation(vx[:, :, 0:DH], vst[:, b, :].rearrange("p (g e) -> p g e", g=KVH), ACT.Copy, scale=SQ).then_inc(v_hi.sem, 1)

            def high_query(g, b):
                act.wait_ge(q2_rdy.sem, q2_rdy.count(g, b + 1))
                if b >= 1:
                    act.wait_ge(qxT_ps.sem, qxT_ps.count(g, 2 * b))
                act.activation(Qx[:, :, :].rearrange("p h (s e) -> p h s e", e=DH)[:, :, 0:3:2, :],
                                      Q2[:, b, :].rearrange("p (h e) -> p h e", h=NH).unsqueeze(2).to_broadcast([P, NH, 2, DH]), ACT.Copy, scale=SQ).then_inc(qx_hi.sem, 1)

            def exps(g, b, u):
                n = KVH * b + u
                act.wait_ge(st_ps.sem, st_ps.count(g, n + 1))
                if n >= 2:
                    act.wait_ge(ex_lo.sem, ex_lo.count(g, n - 1))
                act.activation(EX[:, n % 2, :], AB[1 + u % 2][:, :], ACT.Exp, scale=SCORE_SCALE / (SQ * SQ), bias=lnsa[:, :]).then_inc(ex_rdy.sem, 1)
                act.wait_ge(ex_rdy.sem, ex_rdy.count(g, n + 1))
                if n >= 2:
                    act.wait_ge(pv_done.sem, pv_done.count(g, n - 1))
                act.activation(exh[:, n % 2, :], EX[:, n % 2, :], ACT.Copy).then_inc(ex_hi.sem, 1)

            def high_h3(g, b):
                act.wait_ge(h3T_ps.sem, h3T_ps.count(g, b + 1))
                act.activation(h3T[:, 0, :, b * S:(b + 1) * S], AB[b][:, :].rearrange("p (k t) -> p k t", k=KC), ACT.Copy, scale=SX).then_inc(h3_hi.sem, 1)

            def router_exps(g):
                act.wait_ge(top_rdy.sem, top_rdy.count(g))
                for b in range(GB):
                    act.activation(sel[:, 7, b, :], lg[:, b, :], ACT.Exp, bias=top[:, 1, b:b + 1], accum_out=sume[:, b:b + 1]).then_inc(rho_rdy.sem, 1)
                    act.activation(rho[:, b:b + 1], top[:, 2, b:b + 1], ACT.Exp, bias=top[:, 1, b:b + 1]).then_inc(rho_rdy.sem, 1)

            def attention(g):
                for b in range(GB):
                    high_xn(g, b)
                for b in range(GB):
                    kv_norms(g, b)
                scale_q(g)
                for b in range(GB):
                    high_kv(g, b)
                    high_query(g, b)
                    for u in range(KVH):
                        exps(g, b, u)
                for b in range(GB):
                    high_h3(g, b)
                router_exps(g)
                if not (isinstance(g, int) and g == 0):
                    act.wait_ge(out_st.sem, out_st.count(g - 1))

            def gelus(g, c):
                act.wait_ge(f1_ps.sem, f1_ps.count(g, c + 1))
                if c >= 2:
                    act.wait_ge(hs_rdy.sem, hs_rdy.count(g, c - 1))
                act.activation(H1[:, c % 2, :], FB[c % 2][:, 0:T], ACT.Gelu_apprx_tanh, bias=b1c[:, c:c + 1], scale=1.0 / (SX * SW)).then_inc(h1_rdy.sem, 1)
                act.wait_ge(f2_ps.sem, f2_ps.count(g, c + 1))
                if c >= 2:
                    act.wait_ge(t2_rdy.sem, t2_rdy.count(g, c - 1))
                act.activation(H2[:, c % 2, :], FB[c % 2][:, 0:T], ACT.Gelu_apprx_tanh, bias=b1c[:, c:c + 1], scale=1.0 / (SX * SW)).then_inc(h2_rdy.sem, 1)

            def high_hidden(g, c):
                act.wait_ge(t2_rdy.sem, t2_rdy.count(g, c + 1))
                if c >= 2:
                    act.wait_ge(u2_used.sem, u2_used.count(g, c - 1))
                act.activation(t2s[:, c % 2, 0, :], T2[:, c % 2, :], ACT.Copy).then_inc(t2_hi.sem, 1)
                act.wait_ge(hs_rdy.sem, hs_rdy.count(g, c + 1))
                act.activation(hs[:, 0, c, :], HS[:, c % 2, :], ACT.Copy).then_inc(hs_hi.sem, 1)

            def ffn(g):
                for c in range(FC + 1):
                    if c < FC:
                        gelus(g, c)
                    if c >= 1:
                        high_hidden(g, c - 1)

            attention(0)
            with act.Fori(0, NG - 1) as i:
                ffn(i)
                attention(i + 1)
            ffn(NG - 1)

        @block.vector
        def _(dve):
            dve.memset(ones[:, :], 1.0).then_inc(s_const, 1)
            dve.memset(Qx[:, :, :], 0.0).then_inc(s_const, 1)
            dve.memset(kx[:, :, :, :], 0.0).then_inc(s_const, 1)
            dve.memset(vx[:, :, DH:DH + 1], SQ).then_inc(s_const, 1)
            dve.memset(ones16[:, :], 1.0).then_inc(s_const, 1)
            dve.memset(lnsa[:, :], float(np.log(SA))).then_inc(s_const, 1)
            dve.memset(mparts[:, :, :, :], 0.0).then_inc(s_const, 1)
            for e in range(NE):
                dve.memset(descend[:, e:e + 1], float(NE - e)).then_inc(s_const, 1)
            dve.wait_ge(s_small, 16 * N_SMALL)
            dve.tensor_scalar(gammaS[:, :], gamma[:, :], SW, None, ALU.mult).then_inc(s_const, 1)
            dve.tensor_copy(beta_b[:, :, :], beta[:, :].unsqueeze(2).to_broadcast([P, KC, P])).then_inc(s_const, 1)
            dve.wait_ge(s_const, N_CONST)
            dve.wait_ge(s_pconst, N_PCONST)
            for i, (loads, shape, hi, lo, scale) in enumerate(pieces):
                rows = lo.shape[0]
                dve.wait_ge(s_hi, i + 1)
                dve.scalar_tensor_tensor(lo, staged(i, rows), scale, hi[0:rows], ALU.mult, ALU.subtract).then_inc(s_lo, 1)
                if i == KC - 1:
                    dve.wait_ge(s_beta, KC)
                    for h in range(2):
                        dve.tensor_tensor(bkv[:, h * D:(h + 1) * D], AB[h][:, :], bkv[:, h * D:(h + 1) * D], ALU.add).then_inc(s_bias, 1)
                    dve.tensor_tensor(bq[:, :], AB[2][:, 0:KC], bq[:, :], ALU.add).then_inc(s_bias, 1)
            dve.wait_ge(s_bias, 3)
            dve.wait_ge(s_lo, len(pieces))
            chain = Chain(dve, dve_at)
            link = chain.link

            def stats(src, norm, b, sig_):
                link(dve.bn_stats(stat[:, b, :], src))
                dve.memset(fence[:, 0:1], 0.0)
                dve.bn_aggr(mv[:, norm, b, :], stat[:, b, :]).then_inc(sig_.sem, 1)

            def norm_x(g):
                chain.begin(g)
                dve.wait_ge(x_in.sem, x_in.count(g))
                for b in range(GB):
                    stats(X[:, b, :], 0, b, stats1)
                dve.wait_ge(norm1.sem, norm1.count(g))
                for b in range(GB):
                    dve.tensor_scalar(XN[:, b, :], X[:, b, :], mv[:, 0, b, 0:1], nrm[:, 4, b:b + 1], ALU.subtract, ALU.mult).then_inc(xn_rdy.sem, 1)
                for b in range(GB):
                    dve.wait_ge(xn_rdy.sem, xn_rdy.count(g, b + 1))
                    dve.tensor_scalar(X[:, b, :], X[:, b, :], nrm[:, 6, b:b + 1], nrm[:, 5, b:b + 1], ALU.mult, ALU.add).then_inc(base_rdy.sem, 1)

            def low_xn(g, b):
                dve.wait_ge(xn_hi.sem, xn_hi.count(g, b + 1))
                bs = slice(b * S, (b + 1) * S)
                dve.scalar_tensor_tensor(xnT[:, 1, :, bs], AB[b][:, :].rearrange("p (k t) -> p k t", k=KC), SX, xnT[:, 0, :, bs], ALU.mult, ALU.subtract).then_inc(xn_lo.sem, 1)

            def bias_kv(g, b):
                dve.wait_ge(kv_ps.sem, kv_ps.count(g, b + 1))
                for h in range(2):
                    bank = AB[(2 + 2 * b + h) % 5]
                    dve.scalar_tensor_tensor(KV[:, b, h, :], bank[:, :], 1.0 / (SX * SW), bkv[:, h * D:(h + 1) * D], ALU.mult, ALU.add).then_inc(kv_rdy.sem, 1)

            def low_product(g, b):
                dve.wait_ge(pr_hi.sem, pr_hi.count(g, b + 1))
                dve.scalar_tensor_tensor(prs[:, b, 1, :], PR[:, b, :], wn[:, b:b + 1], prs[:, b, 0, :], ALU.mult, ALU.subtract).then_inc(pr_lo.sem, 1)

            def make_a(g):
                dve.wait_ge(a_ps.sem, a_ps.count(g))
                link(dve.tensor_scalar(asum[:, :, :], AB[3][:, 0:GB * KC].rearrange("p (b c) -> p b c", b=GB),
                                       (1.0 - IDENTITY_WEIGHT) / SA, IDENTITY_WEIGHT, ALU.mult, ALU.add))
                link(dve.tensor_scalar(acol[:, :, :], asum[:, :, :], SQ / (SX * SW), None, ALU.mult))
                link(dve.tensor_scalar(asum[:, :, :], asum[:, :, :], SQ, None, ALU.mult))
                dve.tensor_tensor(bqa[:, :, :], asum[:, :, :], bq[:, :].unsqueeze(1).to_broadcast([P, GB, KC]), ALU.mult).then_inc(a_rdy.sem, 1)

            def low_qa(g):
                dve.wait_ge(qa_hi.sem, qa_hi.count(g))
                dve.tensor_tensor(qas[:, 1], QA[:, :, :], qas[:, 0], ALU.subtract).then_inc(qa_lo.sem, 1)

            def make_x1(g, b):
                dve.wait_ge(y_ps.sem, y_ps.count(g, b + 1))
                dve.wait_ge(bo_added.sem, bo_added.count(g, b + 1))
                dve.scalar_tensor_tensor(X[:, b, :], AB[(4 + b) % 5][:, :], 1.0 / (SQ * SW), X[:, b, :], ALU.mult, ALU.add).then_inc(x1_rdy.sem, 1)
                dve.wait_ge(x1_rdy.sem, x1_rdy.count(g, b + 1))
                stats(X[:, b, :], 1, b, stats2)
                dve.wait_ge(norm2.sem, norm2.count(g, b + 1))
                dve.tensor_scalar(Q2[:, b, :], X[:, b, :], mv[:, 1, b, 0:1], nrm[:, 8, b:b + 1], ALU.subtract, ALU.mult).then_inc(q2_rdy.sem, 1)

            def second_keys(g, b):
                dve.wait_ge(k_hi.sem, k_hi.count(g, b + 1))
                dve.wait_ge(k_fm.sem, k_fm.count(g, b + 1))
                if b >= 1:
                    dve.wait_ge(pv_done.sem, pv_done.count(g, KVH * b))
                dve.tensor_tensor(kx[SLOT:P, :, 1, :], kfm[SLOT:P, :].rearrange("p (g t) -> p g t", g=KVH),
                                         khi[SLOT:P, :].rearrange("p (g t) -> p g t", g=KVH), ALU.subtract).then_inc(kx_b.sem, 1)

            def low_values(g, b):
                dve.wait_ge(v_hi.sem, v_hi.count(g, b + 1))
                dve.scalar_tensor_tensor(vx[:, :, DH + 1:], vst[:, b, :].rearrange("p (g e) -> p g e", g=KVH), SQ,
                                                vx[:, :, 0:DH], ALU.mult, ALU.subtract).then_inc(v_lo.sem, 1)

            def low_query(g, b):
                dve.wait_ge(qx_hi.sem, qx_hi.count(g, b + 1))
                dve.scalar_tensor_tensor(Qx[:, :, DH:2 * DH], Q2[:, b, :].rearrange("p (h e) -> p h e", h=NH), SQ, Qx[:, :, 0:DH], ALU.mult, ALU.subtract).then_inc(qx_lo.sem, 1)

            def take_max(g, b):
                for h in range(2):
                    dve.wait_ge(qxT_ps.sem, qxT_ps.count(g, 2 * b + h + 1))
                    src = AB[1 + h][:, :].bitcast(F16).rearrange("p (q t) -> p q t", t=P)
                    dve.tensor_copy(QxT[:, h * 8:(h + 1) * 8, :], src).then_inc(qxT_rdy.sem, 1)
                for u in range(KVH):
                    dve.wait_ge(sc_ps.sem, sc_ps.count(g, KVH * b + u + 1))
                    dve.tensor_reduce(negm[:, HPG * u:HPG * (u + 1)], AB[3 + u % 2][:, :].rearrange("p (h t) -> p h t", h=HPG),
                                             AX.X, ALU.max, negate=True).then_inc(max_done.sem, 1)
                dve.wait_ge(max_done.sem, max_done.count(g, KVH * (b + 1)))
                by_parity = negm[:, :].rearrange("p (q two) -> p two q", two=2)
                link(dve.tensor_scalar(mparts[:, 0], by_parity, 1.0 / SM, None, ALU.mult))
                dve.scalar_tensor_tensor(mparts[:, 1], by_parity, 1.0 / SM, mparts[:, 0], ALU.mult, ALU.subtract).then_inc(mp_rdy.sem, 1)
                dve.wait_ge(mT_ps.sem, mT_ps.count(g, b + 1))
                if b >= 1:
                    dve.wait_ge(m_in.sem, m_in.count(g, 4 * b))
                dve.tensor_copy(mT[:, :], AB[0][0:2 * NH, 0:S // 2].bitcast(F16)).then_inc(mT_rdy.sem, 1)

            def norm_attention(g, b):
                for h in range(2):
                    dve.wait_ge(pv_done.sem, pv_done.count(g, KVH * b + HPG * (h + 1)))
                    acc = AB[3 + h][:, 0:NH // 2 * (DH + 1)].rearrange("p (h e) -> p h e", e=DH + 1)
                    link(dve.reciprocal(rl[:, h, :].unsqueeze(2), acc[:, :, DH:DH + 1]))
                    dve.tensor_tensor(ON[:, h, :].rearrange("p (h e) -> p h e", e=DH), acc[:, :, 0:DH],
                                             rl[:, h, :].unsqueeze(2).to_broadcast([P, NH // 2, DH]), ALU.mult).then_inc(on_rdy.sem, 1)
                    dve.wait_ge(on_rdy.sem, on_rdy.count(g, 2 * b + h + 1))
                    half = slice(h * D // 2, (h + 1) * D // 2)
                    dve.tensor_tensor(XF[:, b, half], X[:, b, half], ON[:, h, :], ALU.add).then_inc(x2_rdy.sem, 1)
                dve.wait_ge(x2_rdy.sem, x2_rdy.count(g, 2 * (b + 1)))
                stats(XF[:, b, :], 2, b, stats3)
                dve.wait_ge(norm3.sem, norm3.count(g, b + 1))
                dve.tensor_scalar(XN[:, b, :], XF[:, b, :], mv[:, 2, b, 0:1], nrm[:, 9, b:b + 1], ALU.subtract, ALU.mult).then_inc(h3_rdy.sem, 1)

            def low_h3(g, b):
                dve.wait_ge(h3_hi.sem, h3_hi.count(g, b + 1))
                bs = slice(b * S, (b + 1) * S)
                dve.scalar_tensor_tensor(h3T[:, 1, :, bs], AB[b][:, :].rearrange("p (k t) -> p k t", k=KC), SX, h3T[:, 0, :, bs], ALU.mult, ALU.subtract).then_inc(h3_lo.sem, 1)

            def spread(v):
                return v.unsqueeze(2).to_broadcast([P, GB, NE])

            def first_of(logits, top_, mask):
                link(dve.tensor_tensor(sel[:, 0], logits, spread(top_), ALU.is_equal))
                link(dve.tensor_tensor(sel[:, 1], sel[:, 0], descend[:, :].unsqueeze(1).to_broadcast([P, GB, NE]), ALU.mult))
                link(dve.tensor_reduce(top[:, 3, :].unsqueeze(2), sel[:, 1], AX.X, ALU.max))
                link(dve.tensor_tensor(mask, sel[:, 1], spread(top[:, 3, :]), ALU.is_equal))

            def route(g):
                dve.wait_ge(u1_ps.sem, u1_ps.count(g))
                for b in range(GB):
                    link(dve.tensor_reduce(rt[:, b, :].unsqueeze(2), AB[2][:, b * 2 * U1W:(b + 1) * 2 * U1W].rearrange("p (h w) -> p w h", h=2), AX.X, ALU.add))
                link(dve.tensor_scalar(rt[:, :, :], rt[:, :, :], 1.0 / (SX * SW), None, ALU.mult))
                link(dve.tensor_tensor(lg[:, :, :], rt[:, :, ER:U1W], brb[:, :].unsqueeze(1).to_broadcast([P, GB, NE]), ALU.add))
                link(dve.tensor_reduce(top[:, 0, :].unsqueeze(2), lg[:, :, :], AX.X, ALU.max))
                link(dve.tensor_scalar(top[:, 1, :], top[:, 0, :], -1.0, None, ALU.mult))
                first_of(lg[:, :, :], top[:, 0, :], sel[:, 2])
                link(dve.scalar_tensor_tensor(sel[:, 3], sel[:, 2], -HUGE, lg[:, :, :], ALU.mult, ALU.add))
                dve.tensor_reduce(top[:, 2, :].unsqueeze(2), sel[:, 3], AX.X, ALU.max).then_inc(top_rdy.sem, 1)
                dve.wait_ge(top_rdy.sem, top_rdy.count(g))
                first_of(sel[:, 3], top[:, 2, :], sel[:, 4])
                link(dve.tensor_tensor(sel[:, 5], sel[:, 4], sel[:, 2], ALU.subtract))
                u1 = rt[:, :, 0:ER].rearrange("p b (e r) -> p b e r", r=R)
                for k, m in ((0, 2), (1, 5)):
                    link(dve.tensor_tensor(zf[:, :, k, :].rearrange("p b (e r) -> p b e r", r=R), u1,
                                           sel[:, m].unsqueeze(3).to_broadcast([P, GB, NE, R]), ALU.mult))
                link(dve.tensor_scalar(zz[:, :, :, 0, :], zf[:, :, :, :], SX, None, ALU.mult))
                dve.scalar_tensor_tensor(zz[:, :, :, 1, :].rearrange("p b k e -> p (b k) e"), zf[:, :, :, :].rearrange("p b k e -> p (b k) e"), SX,
                                                zz[:, :, :, 0, :].rearrange("p b k e -> p (b k) e"), ALU.mult, ALU.subtract).then_inc(zz_rdy.sem, 1)
                dve.wait_ge(rho_rdy.sem, rho_rdy.count(g))
                for b in range(GB):
                    dve.tensor_scalar(drho[:, b, :], idf[:, :], rho[:, b:b + 1], None, ALU.mult).then_inc(drho_rdy.sem, 1)
                link(dve.tensor_scalar(rho1[:, :], rho[:, :], SH * SW, SH * SW, ALU.mult, ALU.add))
                link(dve.reciprocal(w1st[:, :], sume[:, :]))
                link(dve.tensor_scalar(w1st[:, :], w1st[:, :], 1.0 / (SH * SW), None, ALU.mult))
                dve.wait_ge(zT_ps.sem, zT_ps.count(g))
                dve.tensor_copy(zT[:, :, :], AB[3][:, 0:T].bitcast(F16).rearrange("p (k t) -> p k t", k=2)).then_inc(zT_rdy.sem, 1)
                dve.wait_ge(rho_ps.sem, rho_ps.count(g))
                dve.tensor_scalar(rhoB[:, :], AB[4][:, 0:T], SH, None, ALU.mult).then_inc(rhoB_rdy.sem, 1)
                dve.wait_ge(rhoB_rdy.sem, rhoB_rdy.count(g))

            def attention(g):
                norm_x(g)
                for b in range(GB):
                    low_xn(g, b)
                for b in range(GB):
                    bias_kv(g, b)
                for b in range(GB):
                    low_product(g, b)
                make_a(g)
                low_qa(g)
                for b in range(GB):
                    make_x1(g, b)
                for b in range(GB):
                    second_keys(g, b)
                    low_values(g, b)
                    low_query(g, b)
                    take_max(g, b)
                    norm_attention(g, b)
                for b in range(GB):
                    low_h3(g, b)
                route(g)
                if not (isinstance(g, int) and g == 0):
                    dve.wait_ge(out_st.sem, out_st.count(g - 1))
                chain.end()

            ff = Chain(dve, dve_ff)

            def weigh_hidden(g, c):
                s = c % 2
                dve.wait_ge(h2_rdy.sem, h2_rdy.count(g, c + 1))
                if c >= 2:
                    dve.wait_ge(t2_hi.sem, t2_hi.count(g, c - 1))
                    dve.wait_ge(t2_lo.sem, t2_lo.count(g, c - 1))
                dve.tensor_tensor(T2[:, s, :], H2[:, s, :], rhoB[:, :], ALU.mult).then_inc(t2_rdy.sem, 1)
                dve.wait_ge(t2_rdy.sem, t2_rdy.count(g, c + 1))
                dve.wait_ge(h1_rdy.sem, h1_rdy.count(g, c + 1))
                if c >= 2:
                    dve.wait_ge(hs_lo.sem, hs_lo.count(g, c - 1))
                    dve.wait_ge(hs_hi.sem, hs_hi.count(g, c - 1))
                dve.scalar_tensor_tensor(HS[:, s, :], H1[:, s, :], SH, T2[:, s, :], ALU.mult, ALU.add).then_inc(hs_rdy.sem, 1)

            def low_weighted(g, c):
                s = c % 2
                dve.wait_ge(t2_hi.sem, t2_hi.count(g, c + 1))
                if c >= 2:
                    dve.wait_ge(u2_used.sem, u2_used.count(g, c - 1))
                dve.tensor_tensor(t2s[:, s, 1, :], T2[:, s, :], t2s[:, s, 0, :], ALU.subtract).then_inc(t2_lo.sem, 1)

            def adapter_out(g):
                dve.wait_ge(u2_used.sem, u2_used.count(g))
                dve.tensor_reduce(u2[:, :, :].unsqueeze(3), UBv[:, 0:GB].rearrange("p b h e -> p b e h"), AX.X, ALU.add).then_inc(u2_ev.sem, 1)
                dve.wait_ge(us_ps.sem, us_ps.count(g))
                ff.link(dve.tensor_reduce(us[:, :, :].unsqueeze(3), UBv[:, 2:2 + GB].rearrange("p b h e -> p b e h"), AX.X, ALU.add))
                dve.wait_ge(u2_ev.sem, u2_ev.count(g))

                def masked(dst, src, m):
                    return dve.tensor_tensor(dst.rearrange("p b (e r) -> p b e r", r=R), src.rearrange("p b (e r) -> p b e r", r=R),
                                             sel[:, m].unsqueeze(3).to_broadcast([P, GB, NE, R]), ALU.mult)
                ff.link(masked(z2f[:, :, :], us[:, :, :], 2))
                ff.link(masked(z2g[:, :, :], u2[:, :, :], 5))
                ff.link(dve.tensor_tensor(z2f[:, :, :], z2f[:, :, :], z2g[:, :, :], ALU.add))
                ff.link(dve.tensor_scalar(z2s[:, :, 0, :], z2f[:, :, :], 1.0 / SW, None, ALU.mult))
                dve.scalar_tensor_tensor(z2s[:, :, 1, :], z2f[:, :, :], 1.0 / SW, z2s[:, :, 0, :], ALU.mult, ALU.subtract).then_inc(z2_rdy.sem, 1)
                dve.wait_ge(z2T_ps.sem, z2T_ps.count(g))
                dve.tensor_copy(z2T[:, :, :], UB[:, 0:GB * S // 2].bitcast(F16).rearrange("p (b t) -> p b t", b=GB)).then_inc(z2T_rdy.sem, 1)

            def output(g, b):
                dve.wait_ge(yf_ps.sem, yf_ps.count(g, b + 1))
                ff.link(dve.scalar_tensor_tensor(OUT[:, b, :], b2b[:, :], rho1[:, b:b + 1], FB[b][:, :], ALU.mult, ALU.add))
                dve.scalar_tensor_tensor(OUT[:, b, :], OUT[:, b, :], w1st[:, b:b + 1], XF[:, b, :], ALU.mult, ALU.add).then_inc(out_rdy.sem, 1)

            def ffn(g):
                ff.begin(g)
                for c in range(FC + 1):
                    if c < FC:
                        weigh_hidden(g, c)
                    if c >= 1:
                        low_weighted(g, c - 1)
                adapter_out(g)
                for b in range(GB):
                    output(g, b)
                dve.wait_ge(out_rdy.sem, out_rdy.count(g))
                ff.end()

            attention(0)
            with dve.Fori(0, NG - 1) as i:
                ffn(i)
                attention(i + 1)
            ffn(NG - 1)

        @block.tensor
        def _(pe):
            PASSES = ((0, 0), (0, 1), (1, 0))
            pe.wait_ge(s_const, N_CONST)
            pe.wait_ge(s_pconst, N_PCONST)
            for k in range(KC):
                pe.wait_ge(s_stage[k % 2], stage_count(k))
                for h in range(2):
                    pe.matmul(AB[h][:, :], beta_b[:, k, :], staged(k)[:, (1 + h) * D:(2 + h) * D], start=(k == 0), stop=(k == KC - 1))
                for c in range(KC):
                    last = pe.matmul(AB[2][:, c:c + 1], staged(k)[:, c * P:(c + 1) * P], beta[:, k:k + 1],
                                     start=(k == 0 and c == 0), stop=(k == KC - 1), skip_group_check=True)
                last.then_inc(s_beta, 1)
            pe.wait_ge(s_bias, 3)
            pe.wait_ge(s_lo, len(pieces))

            def mm(*a, **k):
                return pe.matmul(*a, **k)

            def to_width(g, b, src_rdy, done):
                pe.wait_ge(src_rdy.sem, src_rdy.count(g, b + 1))
                for k in range(KC):
                    last = pe.transpose(AB[b][:, k * P:(k + 1) * P], XN[:, b, k * P:(k + 1) * P], idf[:, :])
                last.then_inc(done.sem, 1)

            def project_kv(g, b):
                pe.wait_ge(xn_lo.sem, xn_lo.count(g, b + 1))
                bs = slice(b * S, (b + 1) * S)
                out = [AB[(2 + 2 * b + h) % 5] for h in range(2)]
                for k in range(KC):
                    for xp in range(2):
                        for h in range(2):
                            for wp in range(2 - xp):
                                last = mm(out[h][:, :], xnT[:, xp, k, bs], w_in[:, wp, k, (1 + h) * D:(2 + h) * D],
                                          start=(k == 0 and xp == 0 and wp == 0), stop=(k == KC - 1 and xp == 1),
                                          skip_group_check=True)
                last.then_inc(kv_ps.sem, 1)

            def project_q(g, j):
                if j == 1:
                    pe.wait_ge(kv_rdy.sem, kv_rdy.count(g, 1))
                for c in range(2 * j, 2 * j + 2):
                    for k in range(KC):
                        for xp, wp in PASSES:
                            last = mm(AB[1 + j][:, (c % 2) * T:(c % 2 + 1) * T], w_in[:, wp, k, c * P:(c + 1) * P], xnT[:, xp, k, :],
                                      start=(k == 0 and (xp, wp) == PASSES[0]), stop=(k == KC - 1 and (xp, wp) == PASSES[-1]))
                last.then_inc(q_ps.sem, 1)

            def sum_tokens(g, b):
                pe.wait_ge(kv_rdy.sem, kv_rdy.count(g, 2))
                pe.wait_ge(pr_lo.sem, pr_lo.count(g, b + 1))
                pe.wait_ge(pr_hi.sem, pr_hi.count(g, b + 1))
                for c in range(KC):
                    col = b * KC + c
                    for part in range(2):
                        last = mm(AB[3][:, col:col + 1], prs[:, b, part, c * P:(c + 1) * P], ones16[:, :], start=(part == 0), stop=(part == 1))
                last.then_inc(a_ps.sem, 1)

            def project_y(g, b):
                pe.wait_ge(kv_rdy.sem, kv_rdy.count(g, 2 * GB))
                pe.wait_ge(qa_lo.sem, qa_lo.count(g))
                for c in range(KC):
                    for xp, wp in PASSES:
                        last = mm(AB[(4 + b) % 5][:, :], qas[:, xp, c, b * S:(b + 1) * S], w_out[:, wp, c, :],
                                  start=(c == 0 and (xp, wp) == PASSES[0]), stop=(c == KC - 1 and (xp, wp) == PASSES[-1]))
                last.then_inc(y_ps.sem, 1)

            def turn_queries(g, b):
                pe.wait_ge(qx_lo.sem, qx_lo.count(g, b + 1))
                pe.wait_ge(qx_hi.sem, qx_hi.count(g, b + 1))
                pe.wait_ge(qa_rdy.sem, qa_rdy.count(g))
                if b >= 1:
                    pe.wait_ge(ex_rdy.sem, ex_rdy.count(g, KVH * b))
                for q in range(PAIRS):
                    dst = AB[1 + q // 8][:, :].bitcast(F16)[:, (q % 8) * P:(q % 8 + 1) * P]
                    last = pe.transpose(dst, Qx[:, 2 * q:2 * q + 2, :].rearrange("p h e -> p (h e)"), idb[:, :])
                    if q % 8 == 7:
                        last.then_inc(qxT_ps.sem, 1)

            def scores_for_max(g, b, u):
                n = KVH * b + u
                pe.wait_ge(qxT_rdy.sem, qxT_rdy.count(g, 2 * b + u // 4 + 1))
                if u == 0:
                    pe.wait_ge(kx_a.sem, kx_a.count(g, b + 1))
                    pe.wait_ge(kx_b.sem, kx_b.count(g, b + 1))
                    pe.wait_ge(x1_rdy.sem, x1_rdy.count(g))
                if u >= 2:
                    pe.wait_ge(max_done.sem, max_done.count(g, n - 1))
                elif b >= 1:
                    pe.wait_ge(on_rdy.sem, on_rdy.count(g, 2 * b))
                for q in range(2):
                    last = mm(AB[3 + u % 2][:, q * 2 * P:(q + 1) * 2 * P], QxT[:, 2 * u + q, :],
                              kx[:, u, :, :].rearrange("p h t -> p (h t)"), start=True, stop=True)
                last.then_inc(sc_ps.sem, 1)

            def turn_max(g, b):
                pe.wait_ge(mp_rdy.sem, mp_rdy.count(g, b + 1))
                pe.wait_ge(x1_rdy.sem, x1_rdy.count(g))
                if b >= 1:
                    pe.wait_ge(mT_rdy.sem, mT_rdy.count(g, b))
                pe.transpose(AB[0][:, 0:S // 2].bitcast(F16), mparts[:, :, :, :].rearrange("p a b q -> p (a b q)"), idb[:, :]).then_inc(mT_ps.sem, 1)

            def shifted_scores(g, b, u):
                n = KVH * b + u
                if u == 0:
                    pe.wait_ge(m_in.sem, m_in.count(g, 4 * (b + 1)))
                    pe.wait_ge(qxT_rdy.sem, qxT_rdy.count(g, 2 * (b + 1)))
                if u >= 2:
                    pe.wait_ge(ex_rdy.sem, ex_rdy.count(g, n - 1))
                for a in range(2):
                    last = mm(AB[1 + u % 2][:, a * 2 * P:(a + 1) * 2 * P], kx[:, u, a, :],
                              QxT[:, 2 * u:2 * u + 2, :].rearrange("p q t -> p (q t)"), start=True, stop=True)
                last.then_inc(st_ps.sem, 1)

            def weigh_values(g, b, u):
                n = KVH * b + u
                if u == 0:
                    pe.wait_ge(v_lo.sem, v_lo.count(g, b + 1))
                    pe.wait_ge(max_done.sem, max_done.count(g, KVH * (b + 1)))
                pe.wait_ge(ex_lo.sem, ex_lo.count(g, n + 1))
                pe.wait_ge(ex_hi.sem, ex_hi.count(g, n + 1))
                for a in range(2):
                    for q in range(2):
                        at = (HPG * (u % 4) + 2 * q + a) * (DH + 1)
                        out = AB[3 + u // 4][:, at:at + DH + 1]
                        cols = slice((a * 2 + q) * P, (a * 2 + q + 1) * P)
                        mm(out, exh[:, n % 2, cols], vx[:, u, 0:DH + 1], start=True, stop=False, skip_group_check=True)
                        mm(out[:, 0:DH], exh[:, n % 2, cols], vx[:, u, DH + 1:], start=False, stop=False, skip_group_check=True)
                        last = mm(out, exl[:, n % 2, cols], vx[:, u, 0:DH + 1], start=False, stop=True, skip_group_check=True)
                last.then_inc(pv_done.sem, 1)

            def adapter_and_router(g, b):
                pe.wait_ge(h3_lo.sem, h3_lo.count(g, b + 1))
                at = b * 2 * U1W
                for k in range(KC):
                    bs = slice(b * S, (b + 1) * S)
                    mm(AB[2][:, at:at + 2 * U1W], h3T[:, 0, k, bs], a1r[:, k, :, :].rearrange("p h w -> p (h w)"),
                       start=(k == 0), stop=False, skip_group_check=True)
                    last = mm(AB[2][:, at:at + U1W], h3T[:, 1, k, bs], a1r[:, k, 0, :], start=False, stop=(k == KC - 1), skip_group_check=True)
                last.then_inc(u1_ps.sem, 1)

            def turn_routing(g):
                pe.wait_ge(x2_rdy.sem, x2_rdy.count(g))
                pe.wait_ge(zz_rdy.sem, zz_rdy.count(g))
                for k in range(2):
                    for b in range(GB):
                        dst = AB[3][:, 0:T].bitcast(F16)[:, (k * GB + b) * S:(k * GB + b + 1) * S]
                        last = pe.transpose(dst, zz[:, b, k].rearrange("p h e -> p (h e)"), idb[:, :])
                last.then_inc(zT_ps.sem, 1)
                pe.wait_ge(drho_rdy.sem, drho_rdy.count(g))
                for b in range(GB):
                    last = mm(AB[4][:, b * S:(b + 1) * S], ones[:, :], drho[:, b, :], start=True, stop=True)
                last.then_inc(rho_ps.sem, 1)

            def attention(g):
                for b in range(GB):
                    to_width(g, b, xn_rdy, xnT_ps)
                for b in range(GB):
                    project_kv(g, b)
                for j in range(2):
                    project_q(g, j)
                for b in range(GB):
                    sum_tokens(g, b)
                for b in range(GB):
                    project_y(g, b)
                for b in range(GB):
                    turn_queries(g, b)
                    for u in range(KVH):
                        scores_for_max(g, b, u)
                    turn_max(g, b)
                    for u in range(KVH + 1):
                        if u < KVH:
                            shifted_scores(g, b, u)
                        if u >= 1:
                            weigh_values(g, b, u - 1)
                for b in range(GB):
                    to_width(g, b, h3_rdy, h3T_ps)
                for b in range(GB):
                    adapter_and_router(g, b)
                turn_routing(g)

            def hidden(g, c):
                if c >= 2:
                    pe.wait_ge(h2_rdy.sem, h2_rdy.count(g, c - 1))
                cs = slice(c * P, (c + 1) * P)
                for k in range(KC):
                    for xp, wp in PASSES:
                        mm(FB[c % 2][:, 0:T], w1[:, wp, k, cs], h3T[:, xp, k, :], start=(k == 0 and (xp, wp) == PASSES[0]), stop=False,
                           skip_group_check=True)
                adapter_in(c, 0).then_inc(f1_ps.sem, 1)

            def adapter_in(c, k):
                cs = slice(c * P, (c + 1) * P)
                mm(FB[c % 2][:, 0:T], lb1h[:, cs], zT[:, k, :], start=False, stop=False, skip_group_check=True)
                return mm(FB[c % 2][:, 0:T], lb1l[:, cs], zT[0:ER, k, :], start=False, stop=True, skip_group_check=True)

            def second_hidden(g, c):
                pe.wait_ge(h1_rdy.sem, h1_rdy.count(g, c + 1))
                adapter_in(c, 1).then_inc(f2_ps.sem, 1)

            def down(c, at, hi, lo, first):
                mm(UB[:, at:at + 2 * ER], hi, a2[:, c, :, :].rearrange("p h e -> p (h e)"), start=first, stop=False, skip_group_check=True)
                return mm(UB[:, at:at + ER], lo, a2[:, c, 0, :], start=False, stop=(c == FC - 1), skip_group_check=True)

            def second_down(g, c):
                pe.wait_ge(t2_lo.sem, t2_lo.count(g, c + 1))
                pe.wait_ge(t2_hi.sem, t2_hi.count(g, c + 1))
                for b in range(GB):
                    bs = slice(b * S, (b + 1) * S)
                    last = down(c, b * 2 * ER, t2s[:, c % 2, 0, bs], t2s[:, c % 2, 1, bs], c == 0 and b == 0)
                last.then_inc(u2_used.sem, 1)

            def sum_down(g):
                pe.wait_ge(u2_ev.sem, u2_ev.count(g))
                pe.wait_ge(hs_lo.sem, hs_lo.count(g))
                pe.wait_ge(hs_hi.sem, hs_hi.count(g))
                for c in range(FC):
                    for b in range(GB):
                        bs = slice(b * S, (b + 1) * S)
                        last = down(c, (2 + b) * 2 * ER, hs[:, 0, c, bs], hs[:, 1, c, bs], c == 0 and b == 0)
                last.then_inc(us_ps.sem, 1)

            def width_out(g, b):
                pe.wait_ge(h2_rdy.sem, h2_rdy.count(g))
                bs = slice(b * S, (b + 1) * S)
                for c in range(FC):
                    for xp, wp in PASSES:
                        mm(FB[b][:, :], hs[:, xp, c, bs], w2[:, wp, c, :], start=(c == 0 and (xp, wp) == PASSES[0]), stop=False, skip_group_check=True)

            def turn_z2(g):
                pe.wait_ge(z2_rdy.sem, z2_rdy.count(g))
                for b in range(GB):
                    dst = UB[:, 0:GB * S // 2].bitcast(F16)[:, b * S:(b + 1) * S]
                    last = pe.transpose(dst, z2s[:, b].rearrange("p h e -> p (h e)"), idb[:, :])
                last.then_inc(z2T_ps.sem, 1)

            def adapter_up(g, b):
                pe.wait_ge(z2T_rdy.sem, z2T_rdy.count(g))
                mm(FB[b][:, :], z2T[:, b, :], lb2h[:, :], start=False, stop=False, skip_group_check=True)
                mm(FB[b][:, :], z2T[0:ER, b, :], lb2l[:, :], start=False, stop=True, skip_group_check=True).then_inc(yf_ps.sem, 1)

            def ffn(g):
                pe.wait_ge(zT_rdy.sem, zT_rdy.count(g))
                pe.wait_ge(rhoB_rdy.sem, rhoB_rdy.count(g))
                for c in range(FC + 2):
                    if c < FC:
                        hidden(g, c)
                    if 1 <= c <= FC:
                        second_hidden(g, c - 1)
                    if c >= 2:
                        second_down(g, c - 2)
                sum_down(g)
                width_out(g, 0)
                turn_z2(g)
                adapter_up(g, 0)
                width_out(g, 1)
                adapter_up(g, 1)

            attention(0)
            with pe.Fori(0, NG - 1) as i:
                ffn(i)
                pe.wait_ge(out_rdy.sem, out_rdy.count(i))
                attention(i + 1)
            ffn(NG - 1)


N_SMALL = 11
N_PCONST = 8
N_CONST = 7 + NE + 2


def kernel(**inputs):
    import concourse.bacc as _bacc
    from concourse.bass_utils import run_bass_kernel_spmd as _run

    a = {k: np.asarray(v) for k, v in inputs.items()}
    inv = 1.0 / 10000.0 ** (np.arange(0, ROT, 2, dtype=np.float32) / np.float32(ROT))
    freqs = np.repeat(np.arange(S, dtype=np.float32)[:, None] * inv[None, :].astype(np.float32), 2, axis=-1)
    sign = np.where(np.arange(ROT) % 2 == 0, -1.0, 1.0).astype(np.float32)
    rep = (np.arange(P) // DH) % 4
    dim = np.arange(P) % DH
    kform = np.stack([SQ * (rep == 2), SQ * (rep < 3), SM * ((rep == 3) & (dim < 2))], axis=1).astype(np.float32)

    def columns(v):
        return v.reshape(-1, P).T

    feeds = [
        ("x", a["x"]),
        ("ctxT", a["ctx_512"].reshape(BATCH, S, KVH, DH).transpose(0, 3, 2, 1).reshape(BATCH, DH, KVH * S)),
        ("ctx", a["ctx_512"]),
        ("w_in", a["L0_attn_W_in"]), ("b_q", columns(a["L0_attn_b_in"][:D])), ("b_kv", a["L0_attn_b_in"][D:]),
        ("w_out", a["L0_attn_W_out"]), ("b_out", a["L0_attn_b_out"]),
        ("gamma", columns(a["L0_attn_gamma"])), ("beta", columns(a["L0_attn_beta"])),
        ("a1r", np.concatenate([a["L0_ffn_A1"].reshape(ER, D), a["L0_ffn_W_r"]], axis=0).T),
        ("b_r", a["L0_ffn_b_r"]),
        ("w1t", a["L0_ffn_W1"].T), ("b1", columns(a["L0_ffn_b1"])),
        ("w2t", a["L0_ffn_W2"].T), ("b2", a["L0_ffn_b2"]),
        ("b1t", a["L0_ffn_B1"].transpose(0, 2, 1).reshape(ER, F)),
        ("a2t", a["L0_ffn_A2"].reshape(ER, F).T),
        ("b2t", a["L0_ffn_B2"].transpose(0, 2, 1).reshape(ER, D)),
        ("cos", np.cos(freqs).astype(np.float32)), ("sin", (np.sin(freqs) * sign).astype(np.float32)),
        ("kform", kform),
    ]
    nc = _bacc.Bacc("TRN2", target_bir_lowering=False, num_devices=1)
    arrays, args = {}, []
    for name, v in feeds:
        v = np.ascontiguousarray(v)
        arrays[f"in_{name}"] = v
        args.append(nc.dram_tensor(f"in_{name}", v.shape, mybir.dt.from_np(v.dtype), kind="ExternalInput").ap())
    args.append(nc.dram_tensor("out_x", (BATCH, S, D), F32, kind="ExternalOutput").ap())
    build(nc, *args)
    return _run(nc, [arrays], core_ids=[0]).results[0]["out_x"]
```

```python
from contextlib import ExitStack

import numpy as np
import concourse.bass as bass
from concourse import mybir

F32 = mybir.dt.float32
F16 = mybir.dt.float16
ALU = mybir.AluOpType
ACT = mybir.ActivationFunctionType
AX = mybir.AxisListType

P = 128
BATCH, S, D = 32, 128, 512
GB = 2
NG = BATCH // GB
T = GB * S
KC = D // P
F = 2048
FC = F // P
NH, KVH, DH = 32, 8, 16
HPG = NH // KVH
PAIRS = NH // 2
SLOT = 64
NE, R = 8, 8
ER = NE * R
U1W = ER + NE
ROT = D // 2
EPS = 1e-5
SCORE_SCALE = DH ** -0.5
IDENTITY_WEIGHT = 0.5
LORA_SCALE = 2.0
HUGE = 3.0e38
SX = 2.0 ** 6
SW = 2.0 ** 10
SQ = 2.0 ** 4
SA = 2.0 ** 10
SM = 2.0 ** 6
SH = 2.0 ** 4


class Signal:

    def __init__(self, sem, per_group, by=1):
        self.sem, self.per_group, self.by = sem, per_group, by

    def count(self, g, k=None):
        k = self.per_group if k is None else k
        return g * (self.per_group * self.by) + k * self.by


class Chain:

    def __init__(self, eng, sig):
        self.eng, self.sig, self.g, self.n = eng, sig, 0, 0

    def begin(self, g):
        self.g, self.n = g, 0

    def link(self, instruction):
        self.n += 1
        instruction.then_inc(self.sig.sem, 1)
        self.eng.wait_ge(self.sig.sem, self.sig.count(self.g, self.n))

    def end(self):
        assert self.n == self.sig.per_group, (self.sig.sem, self.n)


def build(nc, x_d, ctxT_d, ctx_d, w_in_d, b_q_d, b_kv_d, w_out_d, b_out_d, gamma_d, beta_d,
          a1r_d, b_r_d, w1t_d, b1_d, w2t_d, b2_d, b1t_d, a2t_d, b2t_d, cos_d, sin_d, kform_d,
          out_d):
    ctx = ExitStack()
    with ctx:
        def sb(name, shape, dt=F32):
            return ctx.enter_context(nc.sbuf_tensor(name, shape, dt))

        def sem(name):
            return ctx.enter_context(nc.semaphore(name))

        def sig(name, per_group, by=1):
            return Signal(sem(name), per_group, by)

        w_in = sb("w_in", [P, 2, KC, 3 * D], F16)
        w_out = sb("w_out", [P, 2, KC, D], F16)
        w1 = sb("w1", [P, 2, KC, F], F16)
        w2 = sb("w2", [P, 2, FC, D], F16)
        a1r = sb("a1r", [P, KC, 2, U1W], F16)
        a2 = sb("a2", [P, FC, 2, ER], F16)
        lb1h = sb("lb1h", [P, F], F16)
        lb1l = sb("lb1l", [ER, F], F16)
        lb2h = sb("lb2h", [P, D], F16)
        lb2l = sb("lb2l", [ER, D], F16)
        bkv = sb("bkv", [P, 2 * D])
        bout = sb("bout", [P, D])
        b2b = sb("b2b", [P, D])
        brb = sb("brb", [P, NE])
        bq = sb("bq", [P, KC])
        b1c = sb("b1c", [P, FC])
        gamma = sb("gamma", [P, KC])
        beta = sb("beta", [P, KC])
        cos = sb("cos", [P, ROT])
        sin = sb("sin", [P, ROT])
        kform = sb("kform", [P, 3])
        idf = sb("idf", [P, P])
        idb = sb("idb", [P, P], F16)
        ones = sb("ones", [P, P])
        small = sb("small", [P, 4, GB])
        lnsa = sb("lnsa", [P, 1])
        gammaS = sb("gammaS", [P, KC])
        descend = sb("descend", [P, NE])
        X = sb("X", [P, GB, D])
        XF = sb("XF", [P, GB, D])
        stat = sb("stat", [P, GB, 6])
        mv = sb("mv", [P, 3, GB, 2])
        nrm = sb("nrm", [P, 10, GB])
        XN = sb("XN", [P, GB, D])
        beta_b = XN[:, 0, :].rearrange("p (k n) -> p k n", k=KC)
        junk = XN[:, 1, 0:D // 2].bitcast(F16)
        xnT = sb("xnT", [P, 2, KC, T], F16)
        kst = xnT[:, :, :, :].rearrange("p a k t -> p (a k t)").bitcast(F32)
        KV = sb("KV", [P, GB, 2, D])
        PR = KV[:, :, 0, :]
        QxT = KV[:, 0, :, :].rearrange("p h n -> p (h n)").bitcast(F16).rearrange("p (q t) -> p q t", t=P)
        khi = KV[:, 1, 0, :].bitcast(F16)
        ON = KV[:, 1, 1, :].rearrange("p (h n) -> p h n", h=2)
        kfm = sb("kfm", [P, KVH * P])
        rotc = kfm[:, 0:2 * ROT].rearrange("p (h n) -> p h n", h=2)
        rots = kfm[:, 2 * ROT:4 * ROT].rearrange("p (h n) -> p h n", h=2)
        EX = sb("EX", [P, 2, HPG * P])
        prs = EX[:, :, :].rearrange("p b n -> p (b n)").bitcast(F16).rearrange("p (b h n) -> p b h n", b=GB, h=2)
        ss = sb("ss", [P, GB, 2])
        wn = sb("wn", [P, GB])
        ones16 = sb("ones16", [P, 1], F16)
        asum = sb("asum", [P, GB, KC])
        acol = sb("acol", [P, GB, KC])
        bqa = sb("bqa", [P, GB, KC])
        QA = sb("QA", [P, GB, KC, S])
        Q2 = QA[:, :, :, :].rearrange("p b k t -> p b (k t)")
        qas = sb("qas", [P, 2, KC, T], F16)
        exh, exl = (qas[:, i].rearrange("p k t -> p (k t)").rearrange("p (b n) -> p b n", b=2) for i in range(2))
        kx = sb("kx", [P, KVH, 2, P], F16)
        vst = sb("vst", [P, GB, P])
        vx = sb("vx", [P, KVH, 2 * DH + 1], F16)
        Qx = sb("Qx", [P, NH, SLOT], F16)
        negm = sb("negm", [P, NH])
        fence = sb("fence", [P, 1])
        rl = sb("rl", [P, 2, NH // 2])
        h3T = sb("h3T", [P, 2, KC, T], F16)
        rt = sb("rt", [P, GB, U1W])
        lg = sb("lg", [P, GB, NE])
        top = sb("top", [P, 5, GB])
        sel = sb("sel", [P, 8, GB, NE])
        sume = sb("sume", [P, GB])
        rho = sb("rho", [P, GB])
        w1st = sb("w1st", [P, GB])
        rho1 = sb("rho1", [P, GB])
        zf = kfm[:, 0:2 * GB * ER].rearrange("p (b k e) -> p b k e", b=GB, k=2)
        zz = kfm[:, 2 * GB * ER:4 * GB * ER].bitcast(F16).rearrange("p (b k h e) -> p b k h e", b=GB, k=2, h=2)
        drho = kfm[:, 4 * GB * ER:4 * GB * ER + GB * P].rearrange("p (b n) -> p b n", b=GB)
        zT = sb("zT", [P, 2, T], F16)
        rhoB = sb("rhoB", [P, T])
        OUT = sb("OUT", [P, GB, D])
        H1, H2 = (OUT[:, i, :].rearrange("p (s t) -> p s t", s=2) for i in range(2))
        T2 = sb("T2", [P, 2, T])
        t2s = sb("t2s", [P, 2, 2, T], F16)
        HS = sb("HS", [P, 2, T])
        hs = sb("hs", [P, 2, FC, T], F16)
        u2, us, z2f, z2g = (T2[:, i // 2, (i % 2) * GB * ER:(i % 2 + 1) * GB * ER].rearrange("p (b e) -> p b e", b=GB)
                            for i in range(4))
        z2s = sb("z2s", [P, GB, 2, ER], F16)
        z2T = sb("z2T", [P, GB, P], F16)
        stage = hs[:, :, :, :].rearrange("p a c t -> p (a c t)").bitcast(F32)

        banks = [ctx.enter_context(nc.psum_tensor(f"bank{i}", [P, 512], F32)) for i in range(8)]
        FB, UB, AB = banks[0:2], banks[2], banks[3:8]
        HB = [FB[0], AB[3], AB[4], FB[1]] + [FB[c % 2] for c in range(4, FC)]
        UBv = UB[:, :].rearrange("p (b h e) -> p b h e", b=4, h=2)

        s_small = sem("small_loaded")
        s_const = sem("constants_made")
        s_stage = [sem(f"stage{i}_loaded") for i in range(2)]
        s_hi = sem("weight_high_made")
        s_lo = sem("weight_low_made")
        s_beta = sem("beta_product_done")
        s_bias = sem("bias_folded")
        s_pconst = sem("pool_constants_made")
        x_in = sig("x_loaded", 1, 16)
        k_in = sig("k_loaded", 8 * GB, 16)
        v_in = sig("v_loaded", 1, 16)
        stats1 = sig("stats1_ready", GB)
        norm1 = sig("norm1_ready", 1)
        xn_rdy = sig("xn_ready", GB)
        base_rdy = sig("base_ready", GB)
        bo_added = sig("bout_added", GB)
        xnT_ps = sig("xnT_in_psum", GB)
        xn_hi = sig("xnT_high_ready", GB)
        xn_lo = sig("xnT_low_ready", GB)
        kv_ps = sig("kv_in_psum", GB)
        kv_rdy = sig("kv_biased", 2 * GB)
        rot_done = sig("kv_rotated", GB)
        norms = sig("kv_norms_ready", 2 * GB)
        pr_rdy = sig("kv_product_ready", GB)
        pr_hi = sig("kv_product_high", GB)
        pr_lo = sig("kv_product_low", GB)
        wn_rdy = sig("weights_of_tokens_ready", GB)
        a_ps = sig("a_in_psum", GB)
        a_rdy = sig("a_ready", GB)
        q_ps = sig("q_in_psum", 2)
        qa_rdy = sig("qa_ready", KC * GB)
        qa_hi = sig("qa_high", GB)
        qa_lo = sig("qa_low", GB)
        y_ps = sig("y_in_psum", GB)
        x1_rdy = sig("x1_ready", GB)
        stats2 = sig("stats2_ready", GB)
        norm2 = sig("norm2_ready", GB)
        q2_rdy = sig("q_normed", GB)
        qx_hi = sig("qx_high", GB)
        qx_lo = sig("qx_low", GB)
        k_hi = sig("k_high", GB)
        k_fm = sig("k_formed", GB)
        kx_a = sig("kx_even_heads", 2 * GB)
        kx_b = sig("kx_odd_heads", GB)
        v_hi = sig("v_high", GB)
        v_lo = sig("v_low", GB)
        qxT_ps = sig("qxT_in_psum", 4 * GB)
        qxT_a = sig("qxT_first_half", 2 * GB)
        qxT_b = sig("qxT_second_half", 2 * GB)
        sc_ps = sig("scores_for_max_in_psum", KVH * GB)
        max_done = sig("max_taken", KVH * GB)
        mp_rdy = sig("max_parts_ready", GB)
        st_ps = sig("shifted_scores_in_psum", KVH * GB)
        ex_rdy = sig("exp_ready", KVH * GB)
        ex_hi = sig("exp_high", KVH * GB)
        ex_lo_v = sig("exp_low_by_vector", KVH * GB // 2)
        ex_lo_p = sig("exp_low_by_pool", KVH * GB // 2)
        pv_done = sig("pv_done", KVH * GB)
        on_rdy = sig("attention_normed", 2 * GB)
        x2_rdy = sig("x2_ready", 2 * GB)
        xf_rdy = sig("x2_kept", GB)
        stats3 = sig("stats3_ready", GB)
        norm3 = sig("norm3_ready", GB)
        h3_rdy = sig("h3_ready", GB)
        h3T_ps = sig("h3T_in_psum", GB)
        h3_hi = sig("h3T_high", GB)
        h3_lo = sig("h3T_low", GB)
        u1_ps = sig("u1_in_psum", GB)
        top_rdy = sig("top_logits_ready", 1)
        rho_rdy = sig("rho_ready", 2 * GB)
        zz_rdy = sig("z_parts_ready", 1)
        zT_ps = sig("zT_in_psum", 1)
        zT_rdy = sig("zT_ready", 1)
        drho_rdy = sig("rho_diagonal_ready", GB)
        rho_ps = sig("rho_rows_in_psum", 1)
        rhoB_rdy = sig("rho_rows_ready", 1)
        dve_at = sig("vector_step_attention", 40)
        pool_at = sig("pool_step_attention", 23)
        f1_ps = sig("hidden1_in_psum", FC)
        h1_rdy = sig("hidden1_ready", FC)
        f2_ps = sig("hidden2_in_psum", FC)
        h2_rdy = sig("hidden2_ready", FC)
        t2_rdy = sig("weighted2_ready", FC)
        t2_hi = sig("weighted2_high", FC)
        t2_lo = sig("weighted2_low", FC)
        hs_rdy = sig("hidden_sum_ready", FC)
        hs_hi = sig("hidden_sum_high", FC)
        hs_lo = sig("hidden_sum_low", FC)
        u2_used = sig("u2_product_done", FC)
        u2_ev = sig("u2_read", 1)
        us_ps = sig("us_in_psum", 1)
        us_ev = sig("us_read", 1)
        z2_rdy = sig("z2_parts_ready", 1)
        z2T_ps = sig("z2T_in_psum", 1)
        z2T_rdy = sig("z2T_ready", 1)
        yf_ps = sig("ffn_out_in_psum", GB)
        out_rdy = sig("out_ready", GB)
        out_st = sig("out_stored", GB, 16)
        dve_ff = sig("vector_step_ffn", 7)

        w_in_v = w_in_d.rearrange("(k p) n -> p k n", p=P)
        w1_v = w1t_d.rearrange("(k p) n -> p k n", p=P)
        w2_v = w2t_d.rearrange("(k p) n -> p k n", p=P)
        pieces = []
        for k in range(KC):
            pieces.append(([((0, P), w_in_v[:, k, :])], (3 * D,), w_in[:, 0, k, :], w_in[:, 1, k, :], gammaS[:, k:k + 1]))
        pieces.append(([((0, P), w_out_d.rearrange("(k p) n -> p k n", p=P))], (KC, D), w_out[:, 0], w_out[:, 1], SW))
        pieces.append(([((0, P), a1r_d.rearrange("(k p) n -> p k n", p=P))], (KC, U1W), a1r[:, :, 0, :], a1r[:, :, 1, :], SW))
        pieces.append(([((0, ER), b1t_d), ((ER, P), b1t_d)], (F,), lb1h[:, :], lb1l[:, :], LORA_SCALE * SW))
        pieces.append(([((0, ER), b2t_d), ((ER, P), b2t_d)], (D,), lb2h[:, :], lb2l[:, :], LORA_SCALE * SW))
        pieces.append(([((0, P), a2t_d.rearrange("(c p) n -> p c n", p=P))], (FC, ER), a2[:, :, 0, :], a2[:, :, 1, :], SW))
        for k in range(KC):
            pieces.append(([((0, P), w1_v[:, k, :])], (F,), w1[:, 0, k, :], w1[:, 1, k, :], SW))
        for k in range(KC):
            pieces.append(([((0, P), w2_v[:, 4 * k:4 * k + 4, :])], (4, D), w2[:, 0, 4 * k:4 * k + 4, :], w2[:, 1, 4 * k:4 * k + 4, :], SW))

        def staged(i, rows=P):
            shape = pieces[i][1]
            n = int(np.prod(shape))
            v = stage[0:rows, (i % 2) * 2048:(i % 2) * 2048 + n]
            return v.rearrange("p (a n) -> p a n", a=shape[0]) if len(shape) == 2 else v

        loads_of = [len(p[0]) for p in pieces]

        def stage_count(i):
            return 16 * sum(loads_of[j] for j in range(i % 2, i + 1, 2))

        block = ctx.enter_context(nc.Block())

        @block.sync
        def _(sp):
            for dst, src in ((gamma[:, :], gamma_d),
                             (beta[:, :], beta_d),
                             (bq[:, :], b_q_d),
                             (b1c[:, :], b1_d),
                             (bkv[:, :], b_kv_d.partition_broadcast(P)),
                             (bout[:, :], b_out_d.partition_broadcast(P)),
                             (b2b[:, :], b2_d.partition_broadcast(P)),
                             (brb[:, :], b_r_d.partition_broadcast(P)),
                             (cos[:, :], cos_d), (sin[:, :], sin_d), (kform[:, :], kform_d)):
                sp.dma_start(dst, src).then_inc(s_small, 16)

            def load_group(g):
                if not (isinstance(g, int) and g == 0):
                    sp.wait_ge(xf_rdy.sem, xf_rdy.count(g - 1))
                    sp.wait_ge(h3_rdy.sem, h3_rdy.count(g - 1))
                sp.dma_start(X[:, :, :], x_d[bass.ds(g * GB, GB)].rearrange("b s d -> s b d")).then_inc(x_in.sem, 16)
                if not (isinstance(g, int) and g == 0):
                    sp.wait_ge(v_lo.sem, v_lo.count(g - 1))
                sp.dma_start(vst[:, :, :], ctx_d[bass.ds(g * GB, GB)].rearrange("b t n -> t b n")).then_inc(v_in.sem, 16)

            def load_keys(g, b):
                if b == 0:
                    sp.wait_ge(q_ps.sem, q_ps.count(g))
                else:
                    sp.wait_ge(k_fm.sem, k_fm.count(g, b))
                    sp.wait_ge(k_hi.sem, k_hi.count(g, b))
                for r in range(8):
                    sp.dma_start(kst[16 * r:16 * r + 16, :].unsqueeze(1),
                                 ctxT_d[bass.ds(g * GB + b, 1)].rearrange("b d n -> d b n")).then_inc(k_in.sem, 16)

            def attention(g):
                load_group(g)
                for b in range(GB):
                    load_keys(g, b)

            def ffn(g):
                for b in range(GB):
                    sp.wait_ge(out_rdy.sem, out_rdy.count(g, b + 1))
                    sp.dma_start(out_d[bass.ds(g * GB + b, 1)].rearrange("b s d -> s b d"), OUT[:, b:b + 1, :]).then_inc(out_st.sem, 16)

            for i, (loads, shape, hi, lo, scale) in enumerate(pieces):
                if i >= 2:
                    sp.wait_ge(s_lo, i - 1)
                    sp.wait_ge(s_hi, i - 1)
                    if i - 2 < KC:
                        sp.wait_ge(s_beta, i - 1)
                for (r0, r1), src in loads:
                    v = staged(i)
                    sp.dma_start(v[r0:r1], src).then_inc(s_stage[i % 2], 16)
            attention(0)
            with sp.Fori(0, NG - 1) as i:
                attention(i + 1)
                ffn(i)
            ffn(NG - 1)
            sp.wait_ge(out_st.sem, out_st.count(NG - 1))

        @block.gpsimd
        def _(pool):
            pool.memset(idf[:, :], 0.0).then_inc(s_pconst, 1)
            pool.memset(idb[:, :], 0.0).then_inc(s_pconst, 1)
            for i, v in enumerate((EPS, -0.5, -1.0, SA)):
                pool.memset(small[:, i, :], v).then_inc(s_pconst, 1)
            pool.wait_ge(s_pconst, N_PCONST - 2)
            for m in (idf, idb):
                pool.affine_select(out=m[:, :], in_=m[:, :], compare_op=ALU.not_equal, fill=1.0, base=0,
                                   pattern=[[-1, P]], channel_multiplier=1).then_inc(s_pconst, 1)
            pool.wait_ge(s_const, N_CONST)
            pool.wait_ge(s_small, 16 * N_SMALL)
            chain = Chain(pool, pool_at)
            link = chain.link

            def rsqrt(dst, src, n):
                link(pool.tensor_tensor(nrm[:, 7, 0:n], src, small[:, 0, 0:n], ALU.add))
                return pool.tensor_tensor(dst, nrm[:, 7, 0:n], small[:, 1, 0:n], ALU.pow)

            def norm_scales(g):
                chain.begin(g)
                pool.wait_ge(stats1.sem, stats1.count(g))
                mean, var = mv[:, 0, :, 0], mv[:, 0, :, 1]
                link(rsqrt(nrm[:, 0, :], var, GB))
                link(pool.tensor_tensor(nrm[:, 1, :], nrm[:, 0, :], nrm[:, 0, :], ALU.mult))
                link(pool.tensor_tensor(nrm[:, 2, :], nrm[:, 1, :], var, ALU.mult))
                link(rsqrt(nrm[:, 3, :], nrm[:, 2, :], GB))
                link(pool.tensor_tensor(nrm[:, 4, :], nrm[:, 3, :], nrm[:, 0, :], ALU.mult))
                link(pool.tensor_tensor(nrm[:, 1, :], nrm[:, 0, :], mean, ALU.mult))
                link(pool.tensor_tensor(nrm[:, 5, :], nrm[:, 1, :], small[:, 2, :], ALU.mult))
                pool.tensor_tensor(nrm[:, 6, :], nrm[:, 0, :], ones[:, 0:GB], ALU.add).then_inc(norm1.sem, 1)

            def add_bout(g, b):
                pool.wait_ge(base_rdy.sem, base_rdy.count(g, b + 1))
                pool.tensor_tensor(X[:, b, :], X[:, b, :], bout[:, :], ALU.add).then_inc(bo_added.sem, 1)

            def rotate(g, b):
                pool.wait_ge(kv_rdy.sem, kv_rdy.count(g, 2 * (b + 1)))
                rot = KV[:, b, :, 0:ROT]
                link(pool.tensor_tensor(rotc[:, :, :], rot, cos[:, :].unsqueeze(1).to_broadcast([P, 2, ROT]), ALU.mult))
                for o in range(2):
                    link(pool.tensor_tensor(rots[:, :, o::2], KV[:, b, :, 1 - o:ROT:2],
                                            sin[:, o::2].unsqueeze(1).to_broadcast([P, 2, ROT // 2]), ALU.mult))
                pool.tensor_tensor(rot, rotc[:, :, :], rots[:, :, :], ALU.add).then_inc(rot_done.sem, 1)
                pool.wait_ge(rot_done.sem, rot_done.count(g, b + 1))
                pool.wait_ge(norms.sem, norms.count(g, 2 * (b + 1)))
                pool.tensor_tensor(PR[:, b, :], KV[:, b, 0, :], KV[:, b, 1, :], ALU.mult).then_inc(pr_rdy.sem, 1)

            def token_weights(g, b):
                pool.wait_ge(norms.sem, norms.count(g, 2 * (b + 1)))
                link(pool.tensor_tensor(wn[:, b:b + 1], ss[:, b, 0:1], ss[:, b, 1:2], ALU.mult))
                link(pool.tensor_tensor(wn[:, b:b + 1], wn[:, b:b + 1], small[:, 1, 0:1], ALU.pow))
                pool.tensor_tensor(wn[:, b:b + 1], wn[:, b:b + 1], small[:, 3, 0:1], ALU.mult).then_inc(wn_rdy.sem, 1)

            def form_keys(g, b):
                pool.wait_ge(k_fm.sem, k_fm.count(g, b + 1))
                pool.wait_ge(k_hi.sem, k_hi.count(g, b + 1))
                if b >= 1:
                    pool.wait_ge(st_ps.sem, st_ps.count(g, KVH * b))
                for h in range(2):
                    gs, cs = slice(h * KVH // 2, (h + 1) * KVH // 2), slice(h * KVH * S // 2, (h + 1) * KVH * S // 2)
                    pool.tensor_tensor(kx[0:SLOT, gs, 0, :], kfm[0:SLOT, cs].rearrange("p (g t) -> p g t", t=S),
                                       khi[0:SLOT, cs].rearrange("p (g t) -> p g t", t=S), ALU.subtract).then_inc(kx_a.sem, 1)

            def query_norm(g, b):
                pool.wait_ge(stats2.sem, stats2.count(g, b + 1))
                rsqrt(nrm[:, 8, b:b + 1], mv[:, 1, b, 1:2], 1).then_inc(norm2.sem, 1)

            def low_exp(g, b, u):
                n = KVH * b + u
                pool.wait_ge(ex_hi.sem, ex_hi.count(g, n + 1))
                if n >= 2:
                    pool.wait_ge(pv_done.sem, pv_done.count(g, n - 1))
                pool.tensor_tensor(exl[:, n % 2, :], EX[:, n % 2, :], exh[:, n % 2, :], ALU.subtract).then_inc(ex_lo_p.sem, 1)

            def ffn_norm(g, b):
                pool.wait_ge(stats3.sem, stats3.count(g, b + 1))
                rsqrt(nrm[:, 9, b:b + 1], mv[:, 2, b, 1:2], 1).then_inc(norm3.sem, 1)

            def attention(g):
                norm_scales(g)
                for b in range(GB):
                    add_bout(g, b)
                for b in range(GB):
                    rotate(g, b)
                    token_weights(g, b)
                query_norm(g, 0)
                form_keys(g, 0)
                query_norm(g, 1)
                for u in range(1, KVH, 2):
                    low_exp(g, 0, u)
                form_keys(g, 1)
                ffn_norm(g, 0)
                for u in range(1, KVH, 2):
                    low_exp(g, 1, u)
                ffn_norm(g, 1)
                chain.end()

            attention(0)
            with pool.Fori(0, NG - 1) as i:
                attention(i + 1)

        @block.scalar
        def _(act):
            act.wait_ge(s_small, 16 * N_SMALL)
            act.wait_ge(s_const, N_CONST)
            act.wait_ge(s_pconst, N_PCONST)
            for i, (loads, shape, hi, lo, scale) in enumerate(pieces):
                act.wait_ge(s_stage[i % 2], stage_count(i))
                act.activation(hi, staged(i), ACT.Copy, scale=scale).then_inc(s_hi, 1)

            def high_xn(g, b):
                act.wait_ge(xnT_ps.sem, xnT_ps.count(g, b + 1))
                act.activation(xnT[:, 0, :, b * S:(b + 1) * S], AB[b][:, :].rearrange("p (k t) -> p k t", k=KC), ACT.Copy, scale=SX).then_inc(xn_hi.sem, 1)

            def kv_norms(g, b):
                act.wait_ge(rot_done.sem, rot_done.count(g, b + 1))
                for o in range(2):
                    act.activation(junk[:, :], KV[:, b, o, :], ACT.Square, accum_out=ss[:, b, o:o + 1]).then_inc(norms.sem, 1)
                    act.wait_ge(norms.sem, norms.count(g, 2 * b + o + 1))

            def high_product(g, b):
                act.wait_ge(pr_rdy.sem, pr_rdy.count(g, b + 1))
                act.wait_ge(wn_rdy.sem, wn_rdy.count(g, b + 1))
                act.activation(prs[:, b, 0, :], PR[:, b, :], ACT.Copy, scale=wn[:, b:b + 1]).then_inc(pr_hi.sem, 1)

            def scale_q(g, b):
                act.wait_ge(a_rdy.sem, a_rdy.count(g, b + 1))
                act.wait_ge(q_ps.sem, q_ps.count(g))
                for c in range(KC):
                    src = AB[1 + c // 2][:, (c % 2) * T + b * S:(c % 2) * T + (b + 1) * S]
                    act.activation(QA[:, b, c, :], src, ACT.Identity,
                                   scale=acol[:, b, c:c + 1], bias=bqa[:, b, c:c + 1]).then_inc(qa_rdy.sem, 1)
                act.wait_ge(qa_rdy.sem, qa_rdy.count(g, KC * (b + 1)))
                act.activation(qas[:, 0, :, b * S:(b + 1) * S], QA[:, b], ACT.Copy).then_inc(qa_hi.sem, 1)

            def high_keys(g, b):
                act.wait_ge(k_in.sem, k_in.count(g, 8 * (b + 1)))
                if b >= 1:
                    act.wait_ge(kx_a.sem, kx_a.count(g, 2 * b))
                    act.wait_ge(kx_b.sem, kx_b.count(g, b))
                act.activation(khi[:, :], kst[:, :], ACT.Copy, scale=kform[:, 0:1]).then_inc(k_hi.sem, 1)
                act.activation(kfm[:, :], kst[:, :], ACT.Identity, scale=kform[:, 1:2], bias=kform[:, 2:3]).then_inc(k_fm.sem, 1)

            def high_values(g, b):
                act.wait_ge(v_in.sem, v_in.count(g))
                if b >= 1:
                    act.wait_ge(pv_done.sem, pv_done.count(g, KVH * b))
                act.activation(vx[:, :, 0:DH], vst[:, b, :].rearrange("p (g e) -> p g e", g=KVH), ACT.Copy, scale=SQ).then_inc(v_hi.sem, 1)

            def high_query(g, b):
                act.wait_ge(q2_rdy.sem, q2_rdy.count(g, b + 1))
                if b >= 1:
                    act.wait_ge(qxT_ps.sem, qxT_ps.count(g, 4 * b))
                act.activation(Qx[:, :, :].rearrange("p h (s e) -> p h s e", e=DH)[:, :, 0:3:2, :],
                                      Q2[:, b, :].rearrange("p (h e) -> p h e", h=NH).unsqueeze(2).to_broadcast([P, NH, 2, DH]), ACT.Copy, scale=SQ).then_inc(qx_hi.sem, 1)

            def second_queries(g, b, turn):
                act.wait_ge(qxT_ps.sem, qxT_ps.count(g, 4 * b + 2 * turn + 2))
                src = AB[2][:, :].bitcast(F16).rearrange("p (q t) -> p q t", t=P)
                act.activation(QxT[:, PAIRS // 2:, :], src, ACT.Copy).then_inc(qxT_b.sem, 1)

            def exps(g, b, u):
                n = KVH * b + u
                act.wait_ge(st_ps.sem, st_ps.count(g, n + 1))
                if n >= 2:
                    low = ex_lo_p if n % 2 else ex_lo_v
                    act.wait_ge(low.sem, low.count(g, n // 2))
                act.activation(EX[:, n % 2, :], AB[1 + u % 2][:, :], ACT.Exp, scale=SCORE_SCALE / (SQ * SQ), bias=lnsa[:, :]).then_inc(ex_rdy.sem, 1)

            def keep_x2(g, b):
                act.wait_ge(x2_rdy.sem, x2_rdy.count(g, 2 * (b + 1)))
                if not (isinstance(g, int) and g == 0):
                    act.wait_ge(out_rdy.sem, out_rdy.count(g - 1, b + 1))
                act.activation(XF[:, b, :], X[:, b, :], ACT.Copy).then_inc(xf_rdy.sem, 1)

            def high_h3(g, b):
                act.wait_ge(h3T_ps.sem, h3T_ps.count(g, b + 1))
                act.activation(h3T[:, 0, :, b * S:(b + 1) * S], AB[b][:, :].rearrange("p (k t) -> p k t", k=KC), ACT.Copy, scale=SX).then_inc(h3_hi.sem, 1)

            def router_exps(g):
                act.wait_ge(top_rdy.sem, top_rdy.count(g))
                for b in range(GB):
                    act.activation(sel[:, 7, b, :], lg[:, b, :], ACT.Exp, bias=top[:, 1, b:b + 1], accum_out=sume[:, b:b + 1]).then_inc(rho_rdy.sem, 1)
                    act.activation(rho[:, b:b + 1], top[:, 2, b:b + 1], ACT.Exp, bias=top[:, 1, b:b + 1]).then_inc(rho_rdy.sem, 1)

            def first_gelu(g, c):
                act.wait_ge(f1_ps.sem, f1_ps.count(g, c + 1))
                if c >= 2:
                    act.wait_ge(hs_rdy.sem, hs_rdy.count(g, c - 1))
                act.activation(H1[:, c % 2, :], HB[c][:, 0:T], ACT.Gelu_apprx_tanh, bias=b1c[:, c:c + 1], scale=1.0 / (SX * SW)).then_inc(h1_rdy.sem, 1)

            def second_gelu(g, c):
                act.wait_ge(f2_ps.sem, f2_ps.count(g, c + 1))
                if c >= 2:
                    act.wait_ge(t2_rdy.sem, t2_rdy.count(g, c - 1))
                act.activation(H2[:, c % 2, :], HB[c][:, 0:T], ACT.Gelu_apprx_tanh, bias=b1c[:, c:c + 1], scale=1.0 / (SX * SW)).then_inc(h2_rdy.sem, 1)

            def high_hidden(g, c):
                act.wait_ge(t2_rdy.sem, t2_rdy.count(g, c + 1))
                if c >= 2:
                    act.wait_ge(u2_used.sem, u2_used.count(g, c - 1))
                act.activation(t2s[:, c % 2, 0, :], T2[:, c % 2, :], ACT.Copy).then_inc(t2_hi.sem, 1)
                act.wait_ge(hs_rdy.sem, hs_rdy.count(g, c + 1))
                act.activation(hs[:, 0, c, :], HS[:, c % 2, :], ACT.Copy).then_inc(hs_hi.sem, 1)

            def body(f, n):
                for c in range(FC + 1):
                    if f is not None:
                        if c < FC:
                            first_gelu(f, c)
                        if c >= 1:
                            high_hidden(f, c - 1)
                    if n is not None:
                        if c == 3:
                            high_xn(n, 0)
                            high_xn(n, 1)
                    if f is not None and c < FC:
                        second_gelu(f, c)
                    if n is None:
                        continue
                    if c in (8, 10):
                        kv_norms(n, (c - 8) // 2)
                    if c in (9, 11):
                        high_product(n, (c - 9) // 2)
                    if c in (11, 13):
                        scale_q(n, (c - 11) // 2)
                    if c == 14:
                        high_keys(n, 0)
                    if c == 15:
                        high_values(n, 0)
                        high_query(n, 0)
                if n is None:
                    return
                second_queries(n, 0, 0)
                high_keys(n, 1)
                second_queries(n, 0, 1)
                for u in range(KVH):
                    exps(n, 0, u)
                    if u == 3:
                        high_query(n, 1)
                high_values(n, 1)
                second_queries(n, 1, 0)
                second_queries(n, 1, 1)
                for u in range(KVH):
                    exps(n, 1, u)
                    if u == 3:
                        high_h3(n, 0)
                    if u == 6:
                        keep_x2(n, 0)
                high_h3(n, 1)
                keep_x2(n, 1)
                router_exps(n)
                if f is not None:
                    act.wait_ge(out_st.sem, out_st.count(f))

            body(None, 0)
            with act.Fori(0, NG - 1) as i:
                body(i, i + 1)
            body(NG - 1, None)

        @block.vector
        def _(dve):
            dve.memset(ones[:, :], 1.0).then_inc(s_const, 1)
            dve.memset(Qx[:, :, :], 0.0).then_inc(s_const, 1)
            dve.memset(kx[:, :, :, :], 0.0).then_inc(s_const, 1)
            dve.memset(vx[:, :, DH:DH + 1], SQ).then_inc(s_const, 1)
            dve.memset(ones16[:, :], 1.0).then_inc(s_const, 1)
            dve.memset(lnsa[:, :], float(np.log(SA))).then_inc(s_const, 1)
            for e in range(NE):
                dve.memset(descend[:, e:e + 1], float(NE - e)).then_inc(s_const, 1)
            dve.wait_ge(s_small, 16 * N_SMALL)
            dve.tensor_scalar(gammaS[:, :], gamma[:, :], SW, None, ALU.mult).then_inc(s_const, 1)
            dve.tensor_copy(beta_b[:, :, :], beta[:, :].unsqueeze(2).to_broadcast([P, KC, P])).then_inc(s_const, 1)
            dve.wait_ge(s_const, N_CONST)
            dve.wait_ge(s_pconst, N_PCONST)
            for i, (loads, shape, hi, lo, scale) in enumerate(pieces):
                rows = lo.shape[0]
                dve.wait_ge(s_hi, i + 1)
                dve.scalar_tensor_tensor(lo, staged(i, rows), scale, hi[0:rows], ALU.mult, ALU.subtract).then_inc(s_lo, 1)
                if i == KC - 1:
                    dve.wait_ge(s_beta, KC)
                    for h in range(2):
                        dve.tensor_tensor(bkv[:, h * D:(h + 1) * D], AB[h][:, :], bkv[:, h * D:(h + 1) * D], ALU.add).then_inc(s_bias, 1)
                    dve.tensor_tensor(bq[:, :], AB[2][:, 0:KC], bq[:, :], ALU.add).then_inc(s_bias, 1)
            dve.wait_ge(s_bias, 3)
            dve.wait_ge(s_lo, len(pieces))
            chain = Chain(dve, dve_at)
            link = chain.link

            def stats(src, norm, b, sig_):
                link(dve.bn_stats(stat[:, b, :], src))
                dve.memset(fence[:, 0:1], 0.0)
                dve.bn_aggr(mv[:, norm, b, :], stat[:, b, :]).then_inc(sig_.sem, 1)

            def stats_x(g):
                chain.begin(g)
                dve.wait_ge(x_in.sem, x_in.count(g))
                for b in range(GB):
                    stats(X[:, b, :], 0, b, stats1)

            def norm_x(g):
                dve.wait_ge(norm1.sem, norm1.count(g))
                for b in range(GB):
                    dve.tensor_scalar(XN[:, b, :], X[:, b, :], mv[:, 0, b, 0:1], nrm[:, 4, b:b + 1], ALU.subtract, ALU.mult).then_inc(xn_rdy.sem, 1)
                for b in range(GB):
                    dve.wait_ge(xn_rdy.sem, xn_rdy.count(g, b + 1))
                    dve.tensor_scalar(X[:, b, :], X[:, b, :], nrm[:, 6, b:b + 1], nrm[:, 5, b:b + 1], ALU.mult, ALU.add).then_inc(base_rdy.sem, 1)

            def low_xn(g, b):
                dve.wait_ge(xn_hi.sem, xn_hi.count(g, b + 1))
                bs = slice(b * S, (b + 1) * S)
                dve.scalar_tensor_tensor(xnT[:, 1, :, bs], AB[b][:, :].rearrange("p (k t) -> p k t", k=KC), SX, xnT[:, 0, :, bs], ALU.mult, ALU.subtract).then_inc(xn_lo.sem, 1)

            def bias_kv(g, b):
                dve.wait_ge(kv_ps.sem, kv_ps.count(g, b + 1))
                for h in range(2):
                    bank = AB[(2 + 2 * b + h) % 5]
                    dve.scalar_tensor_tensor(KV[:, b, h, :], bank[:, :], 1.0 / (SX * SW), bkv[:, h * D:(h + 1) * D], ALU.mult, ALU.add).then_inc(kv_rdy.sem, 1)

            def low_product(g, b):
                dve.wait_ge(pr_hi.sem, pr_hi.count(g, b + 1))
                dve.scalar_tensor_tensor(prs[:, b, 1, :], PR[:, b, :], wn[:, b:b + 1], prs[:, b, 0, :], ALU.mult, ALU.subtract).then_inc(pr_lo.sem, 1)

            def make_a(g, b):
                dve.wait_ge(a_ps.sem, a_ps.count(g, b + 1))
                link(dve.tensor_scalar(asum[:, b, :], AB[3][:, b * KC:(b + 1) * KC],
                                       (1.0 - IDENTITY_WEIGHT) / SA, IDENTITY_WEIGHT, ALU.mult, ALU.add))
                link(dve.tensor_scalar(acol[:, b, :], asum[:, b, :], SQ / (SX * SW), None, ALU.mult))
                dve.scalar_tensor_tensor(bqa[:, b, :], asum[:, b, :], SQ, bq[:, :], ALU.mult, ALU.mult).then_inc(a_rdy.sem, 1)

            def low_qa(g, b):
                dve.wait_ge(qa_hi.sem, qa_hi.count(g, b + 1))
                bs = slice(b * S, (b + 1) * S)
                dve.tensor_tensor(qas[:, 1, :, bs], QA[:, b], qas[:, 0, :, bs], ALU.subtract).then_inc(qa_lo.sem, 1)

            def make_x1(g, b):
                dve.wait_ge(y_ps.sem, y_ps.count(g, b + 1))
                dve.wait_ge(bo_added.sem, bo_added.count(g, b + 1))
                dve.scalar_tensor_tensor(X[:, b, :], AB[(4 + b) % 5][:, :], 1.0 / (SQ * SW), X[:, b, :], ALU.mult, ALU.add).then_inc(x1_rdy.sem, 1)
                dve.wait_ge(x1_rdy.sem, x1_rdy.count(g, b + 1))
                stats(X[:, b, :], 1, b, stats2)

            def make_query(g, b):
                dve.wait_ge(norm2.sem, norm2.count(g, b + 1))
                dve.tensor_scalar(Q2[:, b, :], X[:, b, :], mv[:, 1, b, 0:1], nrm[:, 8, b:b + 1], ALU.subtract, ALU.mult).then_inc(q2_rdy.sem, 1)

            def second_keys(g, b):
                dve.wait_ge(k_hi.sem, k_hi.count(g, b + 1))
                dve.wait_ge(k_fm.sem, k_fm.count(g, b + 1))
                if b >= 1:
                    dve.wait_ge(st_ps.sem, st_ps.count(g, KVH * b))
                dve.tensor_tensor(kx[SLOT:P, :, 1, :], kfm[SLOT:P, :].rearrange("p (g t) -> p g t", g=KVH),
                                         khi[SLOT:P, :].rearrange("p (g t) -> p g t", g=KVH), ALU.subtract).then_inc(kx_b.sem, 1)

            def low_values(g, b):
                dve.wait_ge(v_hi.sem, v_hi.count(g, b + 1))
                dve.scalar_tensor_tensor(vx[:, :, DH + 1:], vst[:, b, :].rearrange("p (g e) -> p g e", g=KVH), SQ,
                                                vx[:, :, 0:DH], ALU.mult, ALU.subtract).then_inc(v_lo.sem, 1)

            def low_query(g, b):
                if b >= 1:
                    dve.wait_ge(qxT_ps.sem, qxT_ps.count(g, 4 * b))
                link(dve.memset(Qx[:, :, 3 * DH:3 * DH + 2], 0.0))
                dve.wait_ge(qx_hi.sem, qx_hi.count(g, b + 1))
                dve.scalar_tensor_tensor(Qx[:, :, DH:2 * DH], Q2[:, b, :].rearrange("p (h e) -> p h e", h=NH), SQ, Qx[:, :, 0:DH], ALU.mult, ALU.subtract).then_inc(qx_lo.sem, 1)

            def first_queries(g, b, turn):
                dve.wait_ge(qxT_ps.sem, qxT_ps.count(g, 4 * b + 2 * turn + 1))
                src = AB[1][:, :].bitcast(F16).rearrange("p (q t) -> p q t", t=P)
                dve.tensor_copy(QxT[:, 0:PAIRS // 2, :], src).then_inc(qxT_a.sem, 1)

            def take_max(g, b, u):
                dve.wait_ge(sc_ps.sem, sc_ps.count(g, KVH * b + u + 1))
                dve.tensor_reduce(negm[:, HPG * u:HPG * (u + 1)], AB[3 + u % 2][:, :].rearrange("p (h t) -> p h t", h=HPG),
                                  AX.X, ALU.max, negate=True).then_inc(max_done.sem, 1)

            def split_max(g, b):
                dve.wait_ge(max_done.sem, max_done.count(g, KVH * (b + 1)))
                hi, lo = (Qx[:, :, 3 * DH + i] for i in range(2))
                link(dve.tensor_scalar(hi, negm[:, :], 1.0 / SM, None, ALU.mult))
                dve.scalar_tensor_tensor(lo, negm[:, :], 1.0 / SM, hi, ALU.mult, ALU.subtract).then_inc(mp_rdy.sem, 1)

            def split_exp(g, b, u):
                n = KVH * b + u
                dve.wait_ge(ex_rdy.sem, ex_rdy.count(g, n + 1))
                if n >= 2:
                    dve.wait_ge(pv_done.sem, pv_done.count(g, n - 1))
                dve.tensor_copy(exh[:, n % 2, :], EX[:, n % 2, :]).then_inc(ex_hi.sem, 1)
                if n % 2 == 0:
                    dve.wait_ge(ex_hi.sem, ex_hi.count(g, n + 1))
                    dve.tensor_tensor(exl[:, n % 2, :], EX[:, n % 2, :], exh[:, n % 2, :], ALU.subtract).then_inc(ex_lo_v.sem, 1)

            def add_attention(g, b, h):
                dve.wait_ge(pv_done.sem, pv_done.count(g, KVH * b + HPG * (h + 1)))
                acc = AB[3 + h][:, 0:NH // 2 * (DH + 1)].rearrange("p (h e) -> p h e", e=DH + 1)
                link(dve.reciprocal(rl[:, h, :].unsqueeze(2), acc[:, :, DH:DH + 1]))
                dve.tensor_tensor(ON[:, h, :].rearrange("p (h e) -> p h e", e=DH), acc[:, :, 0:DH],
                                  rl[:, h, :].unsqueeze(2).to_broadcast([P, NH // 2, DH]), ALU.mult).then_inc(on_rdy.sem, 1)
                dve.wait_ge(on_rdy.sem, on_rdy.count(g, 2 * b + h + 1))
                half = slice(h * D // 2, (h + 1) * D // 2)
                dve.tensor_tensor(X[:, b, half], X[:, b, half], ON[:, h, :], ALU.add).then_inc(x2_rdy.sem, 1)

            def stats_x2(g, b):
                dve.wait_ge(x2_rdy.sem, x2_rdy.count(g, 2 * (b + 1)))
                stats(X[:, b, :], 2, b, stats3)

            def make_h3(g, b):
                dve.wait_ge(norm3.sem, norm3.count(g, b + 1))
                dve.tensor_scalar(XN[:, b, :], X[:, b, :], mv[:, 2, b, 0:1], nrm[:, 9, b:b + 1], ALU.subtract, ALU.mult).then_inc(h3_rdy.sem, 1)

            def low_h3(g, b):
                dve.wait_ge(h3_hi.sem, h3_hi.count(g, b + 1))
                bs = slice(b * S, (b + 1) * S)
                dve.scalar_tensor_tensor(h3T[:, 1, :, bs], AB[b][:, :].rearrange("p (k t) -> p k t", k=KC), SX, h3T[:, 0, :, bs], ALU.mult, ALU.subtract).then_inc(h3_lo.sem, 1)

            def spread(v):
                return v.unsqueeze(2).to_broadcast([P, GB, NE])

            def first_of(logits, top_, mask):
                link(dve.tensor_tensor(sel[:, 0], logits, spread(top_), ALU.is_equal))
                link(dve.tensor_tensor(sel[:, 1], sel[:, 0], descend[:, :].unsqueeze(1).to_broadcast([P, GB, NE]), ALU.mult))
                link(dve.tensor_reduce(top[:, 3, :].unsqueeze(2), sel[:, 1], AX.X, ALU.max))
                link(dve.tensor_tensor(mask, sel[:, 1], spread(top[:, 3, :]), ALU.is_equal))

            def route(g):
                dve.wait_ge(u1_ps.sem, u1_ps.count(g))
                for b in range(GB):
                    link(dve.tensor_reduce(rt[:, b, :].unsqueeze(2), AB[0][:, b * 2 * U1W:(b + 1) * 2 * U1W].rearrange("p (h w) -> p w h", h=2), AX.X, ALU.add))
                link(dve.tensor_scalar(rt[:, :, :], rt[:, :, :], 1.0 / (SX * SW), None, ALU.mult))
                link(dve.tensor_tensor(lg[:, :, :], rt[:, :, ER:U1W], brb[:, :].unsqueeze(1).to_broadcast([P, GB, NE]), ALU.add))
                link(dve.tensor_reduce(top[:, 0, :].unsqueeze(2), lg[:, :, :], AX.X, ALU.max))
                link(dve.tensor_scalar(top[:, 1, :], top[:, 0, :], -1.0, None, ALU.mult))
                first_of(lg[:, :, :], top[:, 0, :], sel[:, 2])
                link(dve.scalar_tensor_tensor(sel[:, 3], sel[:, 2], -HUGE, lg[:, :, :], ALU.mult, ALU.add))
                dve.tensor_reduce(top[:, 2, :].unsqueeze(2), sel[:, 3], AX.X, ALU.max).then_inc(top_rdy.sem, 1)
                dve.wait_ge(top_rdy.sem, top_rdy.count(g))
                first_of(sel[:, 3], top[:, 2, :], sel[:, 4])
                link(dve.tensor_tensor(sel[:, 5], sel[:, 4], sel[:, 2], ALU.subtract))
                u1 = rt[:, :, 0:ER].rearrange("p b (e r) -> p b e r", r=R)
                for k, m in ((0, 2), (1, 5)):
                    link(dve.tensor_tensor(zf[:, :, k, :].rearrange("p b (e r) -> p b e r", r=R), u1,
                                           sel[:, m].unsqueeze(3).to_broadcast([P, GB, NE, R]), ALU.mult))
                link(dve.tensor_scalar(zz[:, :, :, 0, :], zf[:, :, :, :], SX, None, ALU.mult))
                dve.scalar_tensor_tensor(zz[:, :, :, 1, :].rearrange("p b k e -> p (b k) e"), zf[:, :, :, :].rearrange("p b k e -> p (b k) e"), SX,
                                                zz[:, :, :, 0, :].rearrange("p b k e -> p (b k) e"), ALU.mult, ALU.subtract).then_inc(zz_rdy.sem, 1)
                dve.wait_ge(rho_rdy.sem, rho_rdy.count(g))
                for b in range(GB):
                    dve.tensor_scalar(drho[:, b, :], idf[:, :], rho[:, b:b + 1], None, ALU.mult).then_inc(drho_rdy.sem, 1)
                link(dve.tensor_scalar(rho1[:, :], rho[:, :], SH * SW, SH * SW, ALU.mult, ALU.add))
                link(dve.reciprocal(w1st[:, :], sume[:, :]))
                link(dve.tensor_scalar(w1st[:, :], w1st[:, :], 1.0 / (SH * SW), None, ALU.mult))

            def finish_routing(g):
                dve.wait_ge(zT_ps.sem, zT_ps.count(g))
                dve.tensor_copy(zT[:, :, :], AB[0][:, 0:T].bitcast(F16).rearrange("p (k t) -> p k t", k=2)).then_inc(zT_rdy.sem, 1)
                dve.wait_ge(rho_ps.sem, rho_ps.count(g))
                dve.tensor_scalar(rhoB[:, :], AB[1][:, 0:T], SH, None, ALU.mult).then_inc(rhoB_rdy.sem, 1)
                dve.wait_ge(rhoB_rdy.sem, rhoB_rdy.count(g))

            ff = Chain(dve, dve_ff)

            def weigh_hidden(g, c):
                s = c % 2
                dve.wait_ge(h2_rdy.sem, h2_rdy.count(g, c + 1))
                if c >= 2:
                    dve.wait_ge(t2_hi.sem, t2_hi.count(g, c - 1))
                    dve.wait_ge(t2_lo.sem, t2_lo.count(g, c - 1))
                dve.tensor_tensor(T2[:, s, :], H2[:, s, :], rhoB[:, :], ALU.mult).then_inc(t2_rdy.sem, 1)
                dve.wait_ge(t2_rdy.sem, t2_rdy.count(g, c + 1))
                dve.wait_ge(h1_rdy.sem, h1_rdy.count(g, c + 1))
                if c >= 2:
                    dve.wait_ge(hs_lo.sem, hs_lo.count(g, c - 1))
                dve.scalar_tensor_tensor(HS[:, s, :], H1[:, s, :], SH, T2[:, s, :], ALU.mult, ALU.add).then_inc(hs_rdy.sem, 1)

            def low_weighted(g, c):
                s = c % 2
                dve.wait_ge(t2_hi.sem, t2_hi.count(g, c + 1))
                if c >= 2:
                    dve.wait_ge(u2_used.sem, u2_used.count(g, c - 1))
                dve.tensor_tensor(t2s[:, s, 1, :], T2[:, s, :], t2s[:, s, 0, :], ALU.subtract).then_inc(t2_lo.sem, 1)
                dve.wait_ge(hs_hi.sem, hs_hi.count(g, c + 1))
                dve.tensor_tensor(hs[:, 1, c, :], HS[:, s, :], hs[:, 0, c, :], ALU.subtract).then_inc(hs_lo.sem, 1)

            def read_second_down(g):
                ff.begin(g)
                dve.wait_ge(u2_used.sem, u2_used.count(g))
                dve.wait_ge(t2_lo.sem, t2_lo.count(g))
                dve.wait_ge(hs_rdy.sem, hs_rdy.count(g))
                dve.tensor_reduce(u2[:, :, :].unsqueeze(3), UBv[:, 0:GB].rearrange("p b h e -> p b e h"), AX.X, ALU.add).then_inc(u2_ev.sem, 1)

            def adapter_out(g):
                dve.wait_ge(us_ps.sem, us_ps.count(g))
                ff.link(dve.tensor_reduce(us[:, :, :].unsqueeze(3), UBv[:, 2:2 + GB].rearrange("p b h e -> p b e h"), AX.X, ALU.add))
                dve.wait_ge(u2_ev.sem, u2_ev.count(g))

                def masked(dst, src, m):
                    return dve.tensor_tensor(dst.rearrange("p b (e r) -> p b e r", r=R), src.rearrange("p b (e r) -> p b e r", r=R),
                                             sel[:, m].unsqueeze(3).to_broadcast([P, GB, NE, R]), ALU.mult)
                ff.link(masked(z2f[:, :, :], us[:, :, :], 2))
                ff.link(masked(z2g[:, :, :], u2[:, :, :], 5))
                ff.link(dve.tensor_tensor(z2f[:, :, :], z2f[:, :, :], z2g[:, :, :], ALU.add))
                ff.link(dve.tensor_scalar(z2s[:, :, 0, :], z2f[:, :, :], 1.0 / SW, None, ALU.mult))
                dve.scalar_tensor_tensor(z2s[:, :, 1, :], z2f[:, :, :], 1.0 / SW, z2s[:, :, 0, :], ALU.mult, ALU.subtract).then_inc(z2_rdy.sem, 1)

            def keep_z2(g):
                dve.wait_ge(z2T_ps.sem, z2T_ps.count(g))
                dve.tensor_copy(z2T[:, :, :], UB[:, 0:GB * S // 2].bitcast(F16).rearrange("p (b t) -> p b t", b=GB)).then_inc(z2T_rdy.sem, 1)

            def output(g, b):
                dve.wait_ge(yf_ps.sem, yf_ps.count(g, b + 1))
                dve.wait_ge(xf_rdy.sem, xf_rdy.count(g, b + 1))
                ff.link(dve.scalar_tensor_tensor(OUT[:, b, :], b2b[:, :], rho1[:, b:b + 1], FB[b][:, :], ALU.mult, ALU.add))
                dve.scalar_tensor_tensor(OUT[:, b, :], OUT[:, b, :], w1st[:, b:b + 1], XF[:, b, :], ALU.mult, ALU.add).then_inc(out_rdy.sem, 1)

            def body(f, n):
                if n is not None:
                    stats_x(n)
                if f is not None:
                    finish_routing(f)
                for c in range(FC + 1):
                    if f is not None and c >= 1:
                        low_weighted(f, c - 1)
                    if n is not None and c == 3:
                        low_xn(n, 0)
                        low_xn(n, 1)
                    if f is not None and c < FC:
                        weigh_hidden(f, c)
                    if n is None:
                        continue
                    if c == 0:
                        norm_x(n)
                    if c in (5, 7):
                        bias_kv(n, (c - 5) // 2)
                    if c in (9, 11):
                        low_product(n, (c - 9) // 2)
                    if c in (10, 12):
                        make_a(n, (c - 10) // 2)
                    if c in (11, 13):
                        low_qa(n, (c - 11) // 2)
                    if c == 13:
                        make_x1(n, 0)
                        make_query(n, 0)
                    if c == 14:
                        second_keys(n, 0)
                        low_values(n, 0)
                    if c == 15:
                        low_query(n, 0)
                if n is None:
                    read_second_down(f)
                    adapter_out(f)
                    keep_z2(f)
                    for b in range(GB):
                        output(f, b)
                    ff.end()
                    return
                first_queries(n, 0, 0)
                for u in range(KVH):
                    if u == 2 and f is not None:
                        read_second_down(f)
                    if u == 4:
                        make_x1(n, 1)
                    take_max(n, 0, u)
                split_max(n, 0)
                first_queries(n, 0, 1)
                make_query(n, 1)
                for u in range(KVH):
                    split_exp(n, 0, u)
                    if u == 1 and f is not None:
                        adapter_out(f)
                    if u == 3 and f is not None:
                        keep_z2(f)
                    if u == 4:
                        low_query(n, 1)
                    if u == 6:
                        add_attention(n, 0, 0)
                second_keys(n, 1)
                first_queries(n, 1, 0)
                add_attention(n, 0, 1)
                for u in range(KVH):
                    take_max(n, 1, u)
                    if u == 1:
                        stats_x2(n, 0)
                split_max(n, 1)
                first_queries(n, 1, 1)
                low_values(n, 1)
                make_h3(n, 0)
                for u in range(KVH):
                    split_exp(n, 1, u)
                    if u == 1 and f is not None:
                        output(f, 0)
                    if u == 4:
                        low_h3(n, 0)
                    if u == 6:
                        add_attention(n, 1, 0)
                add_attention(n, 1, 1)
                stats_x2(n, 1)
                make_h3(n, 1)
                if f is not None:
                    output(f, 1)
                    dve.wait_ge(out_rdy.sem, out_rdy.count(f))
                    ff.end()
                low_h3(n, 1)
                route(n)
                if f is not None:
                    dve.wait_ge(out_st.sem, out_st.count(f))
                chain.end()

            body(None, 0)
            with dve.Fori(0, NG - 1) as i:
                body(i, i + 1)
            body(NG - 1, None)

        @block.tensor
        def _(pe):
            AHEAD = 4
            W2_BESIDE = (1, 1, (0, 0, 1, 0, 1, 1, 0, 1, 0), 1, 1, 1, (0, 1, 1, 0, 1, 1, 0, 1, 0), 2)
            PASSES = ((0, 0), (0, 1), (1, 0))
            pe.wait_ge(s_const, N_CONST)
            pe.wait_ge(s_pconst, N_PCONST)
            for k in range(KC):
                pe.wait_ge(s_stage[k % 2], stage_count(k))
                for h in range(2):
                    pe.matmul(AB[h][:, :], beta_b[:, k, :], staged(k)[:, (1 + h) * D:(2 + h) * D], start=(k == 0), stop=(k == KC - 1))
                for c in range(KC):
                    last = pe.matmul(AB[2][:, c:c + 1], staged(k)[:, c * P:(c + 1) * P], beta[:, k:k + 1],
                                     start=(k == 0 and c == 0), stop=(k == KC - 1), skip_group_check=True)
                last.then_inc(s_beta, 1)
            pe.wait_ge(s_bias, 3)
            pe.wait_ge(s_lo, len(pieces))

            def mm(*a, **k):
                return pe.matmul(*a, **k)

            def to_width(g, b, src_rdy, done):
                pe.wait_ge(src_rdy.sem, src_rdy.count(g, b + 1))
                for k in range(KC):
                    last = pe.transpose(AB[b][:, k * P:(k + 1) * P], XN[:, b, k * P:(k + 1) * P], idf[:, :])
                last.then_inc(done.sem, 1)

            def project_kv(g, b, half):
                if half == 0:
                    pe.wait_ge(xn_lo.sem, xn_lo.count(g, b + 1))
                    if not (isinstance(g, int) and g == 0):
                        pe.wait_ge(h2_rdy.sem, h2_rdy.count(g - 1, 2 + b))
                bs = slice(b * S, (b + 1) * S)
                out = [AB[(2 + 2 * b + h) % 5] for h in range(2)]
                for k in range(2 * half, 2 * half + 2):
                    for xp in range(2):
                        for h in range(2):
                            for wp in range(2 - xp):
                                last = mm(out[h][:, :], xnT[:, xp, k, bs], w_in[:, wp, k, (1 + h) * D:(2 + h) * D],
                                          start=(k == 0 and xp == 0 and wp == 0), stop=(k == KC - 1 and xp == 1),
                                          skip_group_check=True)
                if half == 1:
                    last.then_inc(kv_ps.sem, 1)

            def project_q(g, c):
                if c == 2:
                    pe.wait_ge(kv_rdy.sem, kv_rdy.count(g, 1))
                for k in range(KC):
                    for xp, wp in PASSES:
                        last = mm(AB[1 + c // 2][:, (c % 2) * T:(c % 2 + 1) * T], w_in[:, wp, k, c * P:(c + 1) * P], xnT[:, xp, k, :],
                                  start=(k == 0 and (xp, wp) == PASSES[0]), stop=(k == KC - 1 and (xp, wp) == PASSES[-1]))
                if c % 2 == 1:
                    last.then_inc(q_ps.sem, 1)

            def sum_tokens(g, b):
                if b == 0:
                    pe.wait_ge(kv_rdy.sem, kv_rdy.count(g, 2))
                else:
                    pe.wait_ge(a_rdy.sem, a_rdy.count(g, b))
                pe.wait_ge(pr_lo.sem, pr_lo.count(g, b + 1))
                pe.wait_ge(pr_hi.sem, pr_hi.count(g, b + 1))
                for c in range(KC):
                    col = b * KC + c
                    for part in range(2):
                        last = mm(AB[3][:, col:col + 1], prs[:, b, part, c * P:(c + 1) * P], ones16[:, :], start=(part == 0), stop=(part == 1))
                last.then_inc(a_ps.sem, 1)

            def project_y(g, b, half):
                if half == 0:
                    pe.wait_ge(kv_rdy.sem, kv_rdy.count(g, 2 * GB))
                    pe.wait_ge(qa_lo.sem, qa_lo.count(g, b + 1))
                for c in range(2 * half, 2 * half + 2):
                    for xp, wp in PASSES:
                        last = mm(AB[(4 + b) % 5][:, :], qas[:, xp, c, b * S:(b + 1) * S], w_out[:, wp, c, :],
                                  start=(c == 0 and (xp, wp) == PASSES[0]), stop=(c == KC - 1 and (xp, wp) == PASSES[-1]))
                if half == 1:
                    last.then_inc(y_ps.sem, 1)

            def turn_queries(g, b, turn):
                if turn == 0:
                    pe.wait_ge(qx_lo.sem, qx_lo.count(g, b + 1))
                    pe.wait_ge(qx_hi.sem, qx_hi.count(g, b + 1))
                    if b == 0:
                        pe.wait_ge(qa_rdy.sem, qa_rdy.count(g))
                    else:
                        pe.wait_ge(ex_rdy.sem, ex_rdy.count(g, KVH * b))
                else:
                    pe.wait_ge(mp_rdy.sem, mp_rdy.count(g, b + 1))
                    pe.wait_ge(qxT_a.sem, qxT_a.count(g, 2 * b + 1))
                    pe.wait_ge(qxT_b.sem, qxT_b.count(g, 2 * b + 1))
                for q in range(PAIRS):
                    dst = AB[1 + q // 8][:, :].bitcast(F16)[:, (q % 8) * P:(q % 8 + 1) * P]
                    last = pe.transpose(dst, Qx[:, 2 * q:2 * q + 2, :].rearrange("p h e -> p (h e)"), idb[:, :])
                    if q % 8 == 7:
                        last.then_inc(qxT_ps.sem, 1)

            def scores_for_max(g, b, u):
                n = KVH * b + u
                if u == 0:
                    pe.wait_ge(qxT_a.sem, qxT_a.count(g, 2 * b + 1))
                    pe.wait_ge(kx_b.sem, kx_b.count(g, b + 1))
                    pe.wait_ge(x1_rdy.sem, x1_rdy.count(g, 1))
                if u % 4 == 0:
                    pe.wait_ge(kx_a.sem, kx_a.count(g, 2 * b + u // 4 + 1))
                if u == 4:
                    pe.wait_ge(qxT_b.sem, qxT_b.count(g, 2 * b + 1))
                if u >= 2:
                    pe.wait_ge(max_done.sem, max_done.count(g, n - 1))
                elif b >= 1:
                    pe.wait_ge(on_rdy.sem, on_rdy.count(g, 2 * b))
                for q in range(2):
                    last = mm(AB[3 + u % 2][:, q * 2 * P:(q + 1) * 2 * P], QxT[:, 2 * u + q, :],
                              kx[:, u, :, :].rearrange("p h t -> p (h t)"), start=True, stop=True)
                last.then_inc(sc_ps.sem, 1)

            def shifted_scores(g, b, u):
                n = KVH * b + u
                if u == 0:
                    pe.wait_ge(qxT_a.sem, qxT_a.count(g, 2 * b + 2))
                if u in (1, 4):
                    pe.wait_ge(qxT_b.sem, qxT_b.count(g, 2 * b + 2))
                if u >= 2:
                    pe.wait_ge(ex_rdy.sem, ex_rdy.count(g, n - 1))
                for a in range(2):
                    last = mm(AB[1 + u % 2][:, a * 2 * P:(a + 1) * 2 * P], kx[:, u, a, :],
                              QxT[:, 2 * u:2 * u + 2, :].rearrange("p q t -> p (q t)"), start=True, stop=True)
                last.then_inc(st_ps.sem, 1)

            def weigh_values(g, b, u):
                n = KVH * b + u
                if u == 0:
                    pe.wait_ge(v_lo.sem, v_lo.count(g, b + 1))
                    pe.wait_ge(max_done.sem, max_done.count(g, KVH * (b + 1)))
                low = ex_lo_p if n % 2 else ex_lo_v
                pe.wait_ge(low.sem, low.count(g, n // 2 + 1))
                pe.wait_ge(ex_hi.sem, ex_hi.count(g, n + 1))
                for a in range(2):
                    for q in range(2):
                        at = (HPG * (u % 4) + 2 * q + a) * (DH + 1)
                        out = AB[3 + u // 4][:, at:at + DH + 1]
                        cols = slice((a * 2 + q) * P, (a * 2 + q + 1) * P)
                        mm(out, exh[:, n % 2, cols], vx[:, u, 0:DH + 1], start=True, stop=False, skip_group_check=True)
                        mm(out[:, 0:DH], exh[:, n % 2, cols], vx[:, u, DH + 1:], start=False, stop=False, skip_group_check=True)
                        last = mm(out, exl[:, n % 2, cols], vx[:, u, 0:DH + 1], start=False, stop=True, skip_group_check=True)
                last.then_inc(pv_done.sem, 1)

            def adapter_and_router(g, b):
                pe.wait_ge(h3_lo.sem, h3_lo.count(g, b + 1))
                at = b * 2 * U1W
                for k in range(KC):
                    bs = slice(b * S, (b + 1) * S)
                    mm(AB[0][:, at:at + 2 * U1W], h3T[:, 0, k, bs], a1r[:, k, :, :].rearrange("p h w -> p (h w)"),
                       start=(k == 0), stop=False, skip_group_check=True)
                    last = mm(AB[0][:, at:at + U1W], h3T[:, 1, k, bs], a1r[:, k, 0, :], start=False, stop=(k == KC - 1), skip_group_check=True)
                last.then_inc(u1_ps.sem, 1)

            def turn_routing(g):
                pe.wait_ge(x2_rdy.sem, x2_rdy.count(g))
                pe.wait_ge(zz_rdy.sem, zz_rdy.count(g))
                for k in range(2):
                    for b in range(GB):
                        dst = AB[0][:, 0:T].bitcast(F16)[:, (k * GB + b) * S:(k * GB + b + 1) * S]
                        last = pe.transpose(dst, zz[:, b, k].rearrange("p h e -> p (h e)"), idb[:, :])
                last.then_inc(zT_ps.sem, 1)
                pe.wait_ge(drho_rdy.sem, drho_rdy.count(g))
                for b in range(GB):
                    last = mm(AB[1][:, b * S:(b + 1) * S], ones[:, :], drho[:, b, :], start=True, stop=True)
                last.then_inc(rho_ps.sem, 1)

            def hidden(g, c):
                if c == 0:
                    pe.wait_ge(h3_lo.sem, h3_lo.count(g))
                if c >= 4:
                    pe.wait_ge(h2_rdy.sem, h2_rdy.count(g, 1 if c == 4 else c - 1))
                elif c in (0, 3) and not (isinstance(g, int) and g == 0):
                    pe.wait_ge(out_rdy.sem, out_rdy.count(g - 1, 1 if c == 0 else 2))
                cs = slice(c * P, (c + 1) * P)
                for k in range(KC):
                    for xp, wp in PASSES:
                        mm(HB[c][:, 0:T], w1[:, wp, k, cs], h3T[:, xp, k, :], start=(k == 0 and (xp, wp) == PASSES[0]), stop=False,
                           skip_group_check=True)

            def first_hidden(g, c):
                if c == 0:
                    pe.wait_ge(zT_rdy.sem, zT_rdy.count(g))
                    pe.wait_ge(rhoB_rdy.sem, rhoB_rdy.count(g))
                adapter_in(c, 0).then_inc(f1_ps.sem, 1)

            def adapter_in(c, k):
                cs = slice(c * P, (c + 1) * P)
                mm(HB[c][:, 0:T], lb1h[:, cs], zT[:, k, :], start=False, stop=False, skip_group_check=True)
                return mm(HB[c][:, 0:T], lb1l[:, cs], zT[0:ER, k, :], start=False, stop=True, skip_group_check=True)

            def second_hidden(g, c):
                pe.wait_ge(h1_rdy.sem, h1_rdy.count(g, c + 1))
                adapter_in(c, 1).then_inc(f2_ps.sem, 1)

            def down(c, at, hi, lo, first):
                mm(UB[:, at:at + 2 * ER], hi, a2[:, c, :, :].rearrange("p h e -> p (h e)"), start=first, stop=False, skip_group_check=True)
                return mm(UB[:, at:at + ER], lo, a2[:, c, 0, :], start=False, stop=(c == FC - 1), skip_group_check=True)

            def second_down(g, c):
                pe.wait_ge(t2_lo.sem, t2_lo.count(g, c + 1))
                pe.wait_ge(t2_hi.sem, t2_hi.count(g, c + 1))
                for b in range(GB):
                    bs = slice(b * S, (b + 1) * S)
                    last = down(c, b * 2 * ER, t2s[:, c % 2, 0, bs], t2s[:, c % 2, 1, bs], c == 0 and b == 0)
                last.then_inc(u2_used.sem, 1)

            def sum_down(g, c0, c1):
                if c0 == 0:
                    pe.wait_ge(u2_ev.sem, u2_ev.count(g))
                    pe.wait_ge(hs_lo.sem, hs_lo.count(g))
                    pe.wait_ge(hs_hi.sem, hs_hi.count(g))
                for c in range(c0, c1):
                    for b in range(GB):
                        bs = slice(b * S, (b + 1) * S)
                        last = down(c, (2 + b) * 2 * ER, hs[:, 0, c, bs], hs[:, 1, c, bs], c == 0 and b == 0)
                if c1 == FC:
                    last.then_inc(us_ps.sem, 1)

            def width_out(g, b, j):
                if j == 0:
                    pe.wait_ge(h2_rdy.sem, h2_rdy.count(g))
                bs = slice(b * S, (b + 1) * S)
                for c in range(2 * j, 2 * j + 2):
                    for xp, wp in PASSES:
                        mm(FB[b][:, :], hs[:, xp, c, bs], w2[:, wp, c, :], start=(c == 0 and (xp, wp) == PASSES[0]), stop=False, skip_group_check=True)

            def turn_z2(g):
                pe.wait_ge(z2_rdy.sem, z2_rdy.count(g))
                for b in range(GB):
                    dst = UB[:, 0:GB * S // 2].bitcast(F16)[:, b * S:(b + 1) * S]
                    last = pe.transpose(dst, z2s[:, b].rearrange("p h e -> p (h e)"), idb[:, :])
                last.then_inc(z2T_ps.sem, 1)

            def adapter_up(g, b):
                pe.wait_ge(z2T_rdy.sem, z2T_rdy.count(g))
                mm(FB[b][:, :], z2T[:, b, :], lb2h[:, :], start=False, stop=False, skip_group_check=True)
                mm(FB[b][:, :], z2T[0:ER, b, :], lb2l[:, :], start=False, stop=True, skip_group_check=True).then_inc(yf_ps.sem, 1)


            def body(f, n):
                for c in range(FC + 2):
                    if f is not None:
                        if AHEAD <= c < FC:
                            hidden(f, c)
                        if c < FC:
                            first_hidden(f, c)
                        if 1 <= c <= FC:
                            second_hidden(f, c - 1)
                    if n is not None:
                        if c == 3:
                            to_width(n, 0, xn_rdy, xnT_ps)
                            to_width(n, 1, xn_rdy, xnT_ps)
                        if 4 <= c < 8:
                            project_kv(n, (c - 4) // 2, c % 2)
                        if 8 <= c < 10:
                            project_q(n, 2 * (c - 8))
                            project_q(n, 2 * (c - 8) + 1)
                        if c in (11, 13):
                            sum_tokens(n, (c - 11) // 2)
                        if c in (13, 14):
                            project_y(n, 0, c - 13)
                    if f is not None and c >= 2:
                        second_down(f, c - 2)
                w2_steps = iter([(b, j) for b in range(GB) for j in range(FC // 2)])

                def w2_next(count):
                    for _ in range(count if f is not None else 0):
                        b, j = next(w2_steps)
                        width_out(f, b, j)
                        if j == FC // 2 - 1:
                            adapter_up(f, b)

                if n is None:
                    sum_down(f, 0, FC)
                    w2_next(2)
                    turn_z2(f)
                    w2_next(FC - 2)
                    return
                turn_queries(n, 0, 0)
                project_y(n, 1, 0)
                project_y(n, 1, 1)
                for u in range(KVH):
                    scores_for_max(n, 0, u)
                    if f is not None and 2 <= u < 6:
                        sum_down(f, 4 * (u - 2), 4 * (u - 1))
                w2_next(W2_BESIDE[0])
                turn_queries(n, 0, 1)
                w2_next(W2_BESIDE[1])
                for u in range(KVH + 1):
                    if u < KVH:
                        shifted_scores(n, 0, u)
                    if u >= 1:
                        weigh_values(n, 0, u - 1)
                    if u == 3 and f is not None:
                        turn_z2(f)
                    w2_next(W2_BESIDE[2][u])
                turn_queries(n, 1, 0)
                w2_next(W2_BESIDE[3])
                for u in range(KVH):
                    scores_for_max(n, 1, u)
                w2_next(W2_BESIDE[4])
                turn_queries(n, 1, 1)
                w2_next(W2_BESIDE[5])
                for u in range(KVH + 1):
                    if u < KVH:
                        shifted_scores(n, 1, u)
                    if u >= 1:
                        weigh_values(n, 1, u - 1)
                    if u == 3:
                        to_width(n, 0, h3_rdy, h3T_ps)
                    if u == 7:
                        adapter_and_router(n, 0)
                    w2_next(W2_BESIDE[6][u])
                w2_next(W2_BESIDE[7])
                to_width(n, 1, h3_rdy, h3T_ps)
                adapter_and_router(n, 1)
                for c in range(AHEAD):
                    hidden(n, c)
                turn_routing(n)

            body(None, 0)
            with pe.Fori(0, NG - 1) as i:
                body(i, i + 1)
            body(NG - 1, None)


N_SMALL = 11
N_PCONST = 8
N_CONST = 6 + NE + 2


def kernel(**inputs):
    import concourse.bacc as _bacc
    from concourse.bass_utils import run_bass_kernel_spmd as _run

    a = {k: np.asarray(v) for k, v in inputs.items()}
    inv = 1.0 / 10000.0 ** (np.arange(0, ROT, 2, dtype=np.float32) / np.float32(ROT))
    freqs = np.repeat(np.arange(S, dtype=np.float32)[:, None] * inv[None, :].astype(np.float32), 2, axis=-1)
    sign = np.where(np.arange(ROT) % 2 == 0, -1.0, 1.0).astype(np.float32)
    rep = (np.arange(P) // DH) % 4
    dim = np.arange(P) % DH
    kform = np.stack([SQ * (rep == 2), SQ * (rep < 3), SM * ((rep == 3) & (dim < 2))], axis=1).astype(np.float32)

    def columns(v):
        return v.reshape(-1, P).T

    feeds = [
        ("x", a["x"]),
        ("ctxT", a["ctx_512"].reshape(BATCH, S, KVH, DH).transpose(0, 3, 2, 1).reshape(BATCH, DH, KVH * S)),
        ("ctx", a["ctx_512"]),
        ("w_in", a["L0_attn_W_in"]), ("b_q", columns(a["L0_attn_b_in"][:D])), ("b_kv", a["L0_attn_b_in"][D:]),
        ("w_out", a["L0_attn_W_out"]), ("b_out", a["L0_attn_b_out"]),
        ("gamma", columns(a["L0_attn_gamma"])), ("beta", columns(a["L0_attn_beta"])),
        ("a1r", np.concatenate([a["L0_ffn_A1"].reshape(ER, D), a["L0_ffn_W_r"]], axis=0).T),
        ("b_r", a["L0_ffn_b_r"]),
        ("w1t", a["L0_ffn_W1"].T), ("b1", columns(a["L0_ffn_b1"])),
        ("w2t", a["L0_ffn_W2"].T), ("b2", a["L0_ffn_b2"]),
        ("b1t", a["L0_ffn_B1"].transpose(0, 2, 1).reshape(ER, F)),
        ("a2t", a["L0_ffn_A2"].reshape(ER, F).T),
        ("b2t", a["L0_ffn_B2"].transpose(0, 2, 1).reshape(ER, D)),
        ("cos", np.cos(freqs).astype(np.float32)), ("sin", (np.sin(freqs) * sign).astype(np.float32)),
        ("kform", kform),
    ]
    nc = _bacc.Bacc("TRN2", target_bir_lowering=False, num_devices=1)
    arrays, args = {}, []
    for name, v in feeds:
        v = np.ascontiguousarray(v)
        arrays[f"in_{name}"] = v
        args.append(nc.dram_tensor(f"in_{name}", v.shape, mybir.dt.from_np(v.dtype), kind="ExternalInput").ap())
    args.append(nc.dram_tensor("out_x", (BATCH, S, D), F32, kind="ExternalOutput").ap())
    build(nc, *args)
    return _run(nc, [arrays], core_ids=[0]).results[0]["out_x"]
```

```python
from contextlib import ExitStack

import numpy as np
import concourse.bass as bass
from concourse import mybir

F32 = mybir.dt.float32
F16 = mybir.dt.float16
ALU = mybir.AluOpType
ACT = mybir.ActivationFunctionType
AX = mybir.AxisListType

P = 128
BATCH, S, D = 32, 128, 512
GB = 2
NG = BATCH // GB
T = GB * S
KC = D // P
F = 2048
FC = F // P
NH, KVH, DH = 32, 8, 16
HPG = NH // KVH
PAIRS = NH // 2
SLOT = 64
NE, R = 8, 8
ER = NE * R
U1W = ER + NE
ROT = D // 2
EPS = 1e-5
SCORE_SCALE = DH ** -0.5
IDENTITY_WEIGHT = 0.5
LORA_SCALE = 2.0
HUGE = 3.0e38
SX = 2.0 ** 6
SW = 2.0 ** 10
SQ = 2.0 ** 4
SA = 2.0 ** 10
SM = 2.0 ** 6
SH = 2.0 ** 4


class Signal:

    def __init__(self, sem, per_group, by=1):
        self.sem, self.per_group, self.by = sem, per_group, by

    def count(self, g, k=None):
        k = self.per_group if k is None else k
        return g * (self.per_group * self.by) + k * self.by


class Chain:

    def __init__(self, eng, sig):
        self.eng, self.sig, self.g, self.n = eng, sig, 0, 0

    def begin(self, g):
        self.g, self.n = g, 0

    def step(self, instruction):
        self.n += 1
        instruction.then_inc(self.sig.sem, 1)

    def link(self, instruction):
        self.step(instruction)
        self.eng.wait_ge(self.sig.sem, self.sig.count(self.g, self.n))

    def end(self):
        assert self.n == self.sig.per_group, (self.sig.sem, self.n)


def build(nc, x_d, ctxT_d, ctx_d, w_in_d, b_q_d, b_kv_d, w_out_d, b_out_d, gamma_d, beta_d,
          a1r_d, b_r_d, w1t_d, b1_d, w2t_d, b2_d, b1t_d, a2t_d, b2t_d, cos_d, sin_d, kform_d,
          out_d):
    ctx = ExitStack()
    with ctx:
        def sb(name, shape, dt=F32):
            return ctx.enter_context(nc.sbuf_tensor(name, shape, dt))

        def sem(name):
            return ctx.enter_context(nc.semaphore(name))

        def sig(name, per_group, by=1):
            return Signal(sem(name), per_group, by)

        w_in = sb("w_in", [P, 2, KC, 3 * D], F16)
        w_out = sb("w_out", [P, 2, KC, D], F16)
        w1 = sb("w1", [P, 2, KC, F], F16)
        w2 = sb("w2", [P, 2, FC, D], F16)
        a1r = sb("a1r", [P, KC, 2, U1W], F16)
        a2 = sb("a2", [P, FC, 2, ER], F16)
        lb1h = sb("lb1h", [P, F], F16)
        lb1l = sb("lb1l", [ER, F], F16)
        lb2h = sb("lb2h", [P, D], F16)
        lb2l = sb("lb2l", [ER, D], F16)
        bkv = sb("bkv", [P, 2 * D])
        bout = sb("bout", [P, D])
        b2b = sb("b2b", [P, D])
        brb = sb("brb", [P, NE])
        bq = sb("bq", [P, KC])
        b1c = sb("b1c", [P, FC])
        gamma = sb("gamma", [P, KC])
        beta = sb("beta", [P, KC])
        cos = sb("cos", [P, ROT])
        sin = sb("sin", [P, ROT])
        kform = sb("kform", [P, 3])
        idf = sb("idf", [P, P])
        idb = sb("idb", [P, P], F16)
        ones = sb("ones", [P, P])
        small = sb("small", [P, 4, GB])
        lnsa = sb("lnsa", [P, 1])
        gammaS = sb("gammaS", [P, KC])
        descend = sb("descend", [P, NE])
        X = sb("X", [P, GB, D])
        XF = sb("XF", [P, GB, D])
        stat = sb("stat", [P, GB, 6])
        mv = sb("mv", [P, 3, GB, 2])
        nrm = sb("nrm", [P, 10, GB])
        XN = sb("XN", [P, GB, D])
        beta_b = XN[:, 0, :].rearrange("p (k n) -> p k n", k=KC)
        junk = XN[:, 1, 0:D // 2].bitcast(F16)
        xnT = sb("xnT", [P, 2, KC, T], F16)
        kst = xnT[:, :, :, :].rearrange("p a k t -> p (a k t)").bitcast(F32)
        KV = sb("KV", [P, GB, 2, D])
        PR = KV[:, :, 0, :]
        QxT = KV[:, 0, :, :].rearrange("p h n -> p (h n)").bitcast(F16).rearrange("p (q t) -> p q t", t=P)
        khi = KV[:, 1, 0, :].bitcast(F16)
        ON = KV[:, 1, 1, :].rearrange("p (h n) -> p h n", h=2)
        kfm = sb("kfm", [P, KVH * P])
        rotc = kfm[:, 0:2 * ROT].rearrange("p (h n) -> p h n", h=2)
        rots = kfm[:, 2 * ROT:4 * ROT].rearrange("p (h n) -> p h n", h=2)
        EX = sb("EX", [P, 2, HPG * P])
        prs = EX[:, :, :].rearrange("p b n -> p (b n)").bitcast(F16).rearrange("p (b h n) -> p b h n", b=GB, h=2)
        ss = sb("ss", [P, GB, 2])
        wn = sb("wn", [P, GB])
        ones16 = sb("ones16", [P, 1], F16)
        asum = sb("asum", [P, GB, KC])
        acol = sb("acol", [P, GB, KC])
        bqa = sb("bqa", [P, GB, KC])
        QA = sb("QA", [P, GB, KC, S])
        Q2 = QA[:, :, :, :].rearrange("p b k t -> p b (k t)")
        qas = sb("qas", [P, 2, KC, T], F16)
        exh, exl = (qas[:, i].rearrange("p k t -> p (k t)").rearrange("p (b n) -> p b n", b=2) for i in range(2))
        kx = sb("kx", [P, KVH, 2, P], F16)
        vst = sb("vst", [P, GB, P])
        vx = sb("vx", [P, KVH, 2 * DH + 1], F16)
        Qx = sb("Qx", [P, NH, SLOT], F16)
        negm = sb("negm", [P, NH])
        fence = sb("fence", [P, 1])
        rl = sb("rl", [P, 2, NH // 2])
        h3T = sb("h3T", [P, 2, KC, T], F16)
        rt = sb("rt", [P, GB, U1W])
        lg = sb("lg", [P, GB, NE])
        top = sb("top", [P, 5, GB])
        sel = sb("sel", [P, 8, GB, NE])
        sume = sb("sume", [P, GB])
        rho = sb("rho", [P, GB])
        w1st = sb("w1st", [P, GB])
        rho1 = sb("rho1", [P, GB])
        both = sb("both", [P, GB])
        zf = kfm[:, 0:2 * GB * ER].rearrange("p (b k e) -> p b k e", b=GB, k=2)
        zz = kfm[:, 2 * GB * ER:4 * GB * ER].bitcast(F16).rearrange("p (b k h e) -> p b k h e", b=GB, k=2, h=2)
        drho = kfm[:, 4 * GB * ER:4 * GB * ER + GB * P].rearrange("p (b n) -> p b n", b=GB)
        zT = sb("zT", [P, 2, T], F16)
        rhoB = sb("rhoB", [P, T])
        OUT = sb("OUT", [P, GB, D])
        H1, H2 = (OUT[:, i, :].rearrange("p (s t) -> p s t", s=2) for i in range(2))
        T2 = sb("T2", [P, 2, T])
        t2s = sb("t2s", [P, 2, 2, T], F16)
        HS = sb("HS", [P, 2, T])
        hs = sb("hs", [P, 2, FC, T], F16)
        u2, us, z2f, z2g = (T2[:, i // 2, (i % 2) * GB * ER:(i % 2 + 1) * GB * ER].rearrange("p (b e) -> p b e", b=GB)
                            for i in range(4))
        z2s = sb("z2s", [P, GB, 2, ER], F16)
        z2T = sb("z2T", [P, GB, P], F16)
        stage = [t.rearrange("p a c t -> p (a c t)").bitcast(F32)[:, i * 2048:(i + 1) * 2048]
                 for t, n in ((hs[:, :, :, :], 2), (w2[:, :, :, :], 4)) for i in range(n)]

        banks = [ctx.enter_context(nc.psum_tensor(f"bank{i}", [P, 512], F32)) for i in range(8)]
        FB, UB, AB = banks[0:2], banks[2], banks[3:8]
        YL = AB[0:2]
        HB = [FB[0], AB[3], AB[4], FB[1]] + [FB[c % 2] for c in range(4, FC)]
        HB_BEFORE = [max([j for j in range(c) if HB[j] is HB[c]], default=None) for c in range(FC)]
        UBv = UB[:, :].rearrange("p (b h e) -> p b h e", b=4, h=2)

        s_small = sem("small_loaded")
        s_const = sem("constants_made")
        s_stage = [sem(f"stage{i}_loaded") for i in range(6)]
        s_hi = sem("weight_high_made")
        s_lo = sem("weight_low_made")
        s_beta = sem("beta_product_done")
        s_bias = sem("bias_folded")
        s_pconst = sem("pool_constants_made")
        x_in = sig("x_loaded", 1, 16)
        k_in = sig("k_loaded", 8 * GB, 16)
        v_in = sig("v_loaded", 1, 16)
        stats1 = sig("stats1_ready", GB)
        norm1 = sig("norm1_ready", 1)
        base1 = sig("base_scales_ready", 1)
        xn_rdy = sig("xn_ready", GB)
        base_rdy = sig("base_ready", GB)
        bo_added = sig("bout_added", GB)
        xnT_ps = sig("xnT_in_psum", GB)
        xn_hi = sig("xnT_high_ready", GB)
        xn_lo = sig("xnT_low_ready", GB)
        kv_ps = sig("kv_in_psum", GB)
        kv_rdy = sig("kv_biased", 2 * GB)
        rot_done = sig("kv_rotated", GB)
        norms = sig("kv_norms_ready", 2 * GB)
        pr_rdy = sig("kv_product_ready", GB)
        pr_hi = sig("kv_product_high", GB)
        pr_lo = sig("kv_product_low", GB)
        wn_rdy = sig("weights_of_tokens_ready", GB)
        a_ps = sig("a_in_psum", GB)
        a_rdy = sig("a_ready", GB)
        q_ps = sig("q_in_psum", 2)
        qa_rdy = sig("qa_ready", KC * GB)
        qa_hi = sig("qa_high", GB)
        qa_lo = sig("qa_low", GB)
        y_ps = sig("y_in_psum", GB)
        x1_rdy = sig("x1_ready", GB)
        stats2 = sig("stats2_ready", GB)
        norm2 = sig("norm2_ready", GB)
        q2_rdy = sig("q_normed", GB)
        qx_hi = sig("qx_high", GB)
        qx_lo = sig("qx_low", GB)
        k_hi = sig("k_high", GB)
        k_fm = sig("k_formed", GB)
        kx_a = sig("kx_even_heads", 2 * GB)
        kx_b0 = sig("kx_odd_heads_row0", 1)
        kx_b1 = sig("kx_odd_heads_row1", 1)
        v_hi = sig("v_high", GB)
        v_lo = sig("v_low", GB)
        qxT_ps = sig("qxT_in_psum", 4 * GB)
        qxT_a = sig("qxT_first_half", 2 * GB)
        qxT_b = sig("qxT_second_half", 2 * GB)
        sc_ps = sig("scores_for_max_in_psum", KVH * GB)
        max_done = sig("max_taken", KVH * GB)
        mp_rdy = sig("max_parts_ready", GB)
        st_ps = sig("shifted_scores_in_psum", KVH * GB)
        ex_rdy = sig("exp_ready", KVH * GB)
        ex_hi = sig("exp_high", KVH * GB)
        ex_lo_v = sig("exp_low_by_vector", KVH * GB // 2)
        ex_lo_p = sig("exp_low_by_pool", KVH * GB // 2)
        pv_done = sig("pv_done", KVH * GB)
        on_rdy = sig("attention_normed", 2 * GB)
        x2_rdy = sig("x2_ready", 2 * GB)
        xf_rdy = sig("x2_kept", GB)
        stats3 = sig("stats3_ready", GB)
        norm3 = sig("norm3_ready", GB)
        h3_rdy = sig("h3_ready", GB)
        h3T_ps = sig("h3T_in_psum", GB)
        h3_hi = sig("h3T_high", GB)
        h3_lo = sig("h3T_low", GB)
        u1_ps = sig("u1_in_psum", GB)
        top_rdy = sig("top_logits_ready", 1)
        rho_rdy = sig("rho_ready", 2 * GB)
        zz_rdy = sig("z_parts_ready", 1)
        zT_ps = sig("zT_in_psum", 1)
        zT_rdy = sig("zT_ready", 1)
        drho_rdy = sig("rho_diagonal_ready", GB)
        rho_ps = sig("rho_rows_in_psum", 1)
        rhoB_rdy = sig("rho_rows_ready", 1)
        dve_at = sig("vector_step_attention", 36)
        pool_at = sig("pool_step_attention", 22)
        f1_ps = sig("hidden1_in_psum", FC)
        h1_rdy = sig("hidden1_ready", FC)
        f2_ps = sig("hidden2_in_psum", FC)
        h2_rdy = sig("hidden2_ready", FC)
        t2_rdy = sig("weighted2_ready", FC)
        t2_hi = sig("weighted2_high", FC)
        t2_lo = sig("weighted2_low", FC)
        hs_rdy = sig("hidden_sum_ready", FC)
        hs_hi = sig("hidden_sum_high", FC)
        hs_lo = sig("hidden_sum_low", FC)
        u2_used = sig("u2_product_done", FC)
        u2_ev = sig("u2_read", 1)
        us_ps = sig("us_in_psum", 1)
        z2_rdy = sig("z2_parts_ready", 1)
        z2T_ps = sig("z2T_in_psum", 1)
        z2T_rdy = sig("z2T_ready", 1)
        yf_ps = sig("ffn_out_in_psum", GB)
        b2_added = sig("b2_added", GB)
        out_rdy = sig("out_ready", GB)
        out_st = sig("out_stored", GB, 16)
        dve_ff = sig("vector_step_ffn", 9)

        w_in_v = w_in_d.rearrange("(k p) n -> p k n", p=P)
        w1_v = w1t_d.rearrange("(k p) n -> p k n", p=P)
        w2_v = w2t_d.rearrange("(k p) n -> p k n", p=P)
        pieces = []
        for k in range(KC):
            pieces.append(([((0, P), w_in_v[:, k, :])], (3 * D,), w_in[:, 0, k, :], w_in[:, 1, k, :], gammaS[:, k:k + 1]))
        pieces.append(([((0, P), w_out_d.rearrange("(k p) n -> p k n", p=P))], (KC, D), w_out[:, 0], w_out[:, 1], SW))
        pieces.append(([((0, P), a1r_d.rearrange("(k p) n -> p k n", p=P))], (KC, U1W), a1r[:, :, 0, :], a1r[:, :, 1, :], SW))
        pieces.append(([((0, ER), b1t_d), ((ER, P), b1t_d)], (F,), lb1h[:, :], lb1l[:, :], LORA_SCALE * SW))
        pieces.append(([((0, ER), b2t_d), ((ER, P), b2t_d)], (D,), lb2h[:, :], lb2l[:, :], LORA_SCALE * SW))
        pieces.append(([((0, P), a2t_d.rearrange("(c p) n -> p c n", p=P))], (FC, ER), a2[:, :, 0, :], a2[:, :, 1, :], SW))
        for k in range(KC):
            pieces.append(([((0, P), w1_v[:, k, :])], (F,), w1[:, 0, k, :], w1[:, 1, k, :], SW))
        for k in range(KC):
            pieces.append(([((0, P), w2_v[:, 4 * k:4 * k + 4, :])], (4, D), w2[:, 0, 4 * k:4 * k + 4, :], w2[:, 1, 4 * k:4 * k + 4, :], SW))

        n_pieces = len(pieces)
        FIRST = KC + 1
        BEFORE_W2 = n_pieces - KC
        slot_of = [i % 6 for i in range(BEFORE_W2)] + [i % 2 for i in range(KC)]

        def staged(i, rows=P):
            shape = pieces[i][1]
            v = stage[slot_of[i]][0:rows, 0:int(np.prod(shape))]
            return v.rearrange("p (a n) -> p a n", a=shape[0]) if len(shape) == 2 else v

        def stage_count(i):
            return 16 * sum(len(pieces[j][0]) for j in range(i + 1) if slot_of[j] == slot_of[i])

        block = ctx.enter_context(nc.Block())

        @block.sync
        def _(sp):
            for dst, src in ((gamma[:, :], gamma_d),
                             (beta[:, :], beta_d),
                             (bq[:, :], b_q_d),
                             (b1c[:, :], b1_d),
                             (bkv[:, :], b_kv_d.partition_broadcast(P)),
                             (bout[:, :], b_out_d.partition_broadcast(P)),
                             (b2b[:, :], b2_d.partition_broadcast(P)),
                             (brb[:, :], b_r_d.partition_broadcast(P)),
                             (cos[:, :], cos_d), (sin[:, :], sin_d), (kform[:, :], kform_d)):
                sp.dma_start(dst, src).then_inc(s_small, 16)

            def load_group(g):
                if not (isinstance(g, int) and g == 0):
                    sp.wait_ge(xf_rdy.sem, xf_rdy.count(g - 1))
                    sp.wait_ge(h3_rdy.sem, h3_rdy.count(g - 1))
                sp.dma_start(X[:, :, :], x_d[bass.ds(g * GB, GB)].rearrange("b s d -> s b d")).then_inc(x_in.sem, 16)
                if not (isinstance(g, int) and g == 0):
                    sp.wait_ge(v_lo.sem, v_lo.count(g - 1))
                sp.dma_start(vst[:, :, :], ctx_d[bass.ds(g * GB, GB)].rearrange("b t n -> t b n")).then_inc(v_in.sem, 16)

            def load_keys(g, b):
                if b == 0:
                    sp.wait_ge(q_ps.sem, q_ps.count(g))
                else:
                    sp.wait_ge(k_fm.sem, k_fm.count(g, b))
                    sp.wait_ge(k_hi.sem, k_hi.count(g, b))
                for r in range(8):
                    sp.dma_start(kst[16 * r:16 * r + 16, :].unsqueeze(1),
                                 ctxT_d[bass.ds(g * GB + b, 1)].rearrange("b d n -> d b n")).then_inc(k_in.sem, 16)

            def attention(g):
                load_group(g)
                for b in range(GB):
                    load_keys(g, b)

            def ffn(g):
                for b in range(GB):
                    sp.wait_ge(out_rdy.sem, out_rdy.count(g, b + 1))
                    sp.dma_start(out_d[bass.ds(g * GB + b, 1)].rearrange("b s d -> s b d"), OUT[:, b:b + 1, :]).then_inc(out_st.sem, 16)

            def load_piece(i):
                before = [j for j in range(i) if slot_of[j] == slot_of[i]]
                if before:
                    sp.wait_ge(s_lo, before[-1] + 1)
                    sp.wait_ge(s_hi, before[-1] + 1)
                    if before[-1] < KC:
                        sp.wait_ge(s_beta, before[-1] + 1)
                for (r0, r1), src in pieces[i][0]:
                    v = staged(i)
                    sp.dma_start(v[r0:r1], src).then_inc(s_stage[slot_of[i]], 16)

            for i in range(6):
                load_piece(i)
            load_group(0)
            for i in range(6, n_pieces):
                load_piece(i)
            for b in range(GB):
                load_keys(0, b)
            with sp.Fori(0, NG - 1) as i:
                attention(i + 1)
                ffn(i)
            ffn(NG - 1)
            sp.wait_ge(out_st.sem, out_st.count(NG - 1))

        @block.gpsimd
        def _(pool):
            pool.memset(idf[:, :], 0.0).then_inc(s_pconst, 1)
            pool.memset(idb[:, :], 0.0).then_inc(s_pconst, 1)
            for i, v in enumerate((EPS, -0.5, -1.0, SA)):
                pool.memset(small[:, i, :], v).then_inc(s_pconst, 1)
            pool.wait_ge(s_pconst, N_PCONST - 2)
            for m in (idf, idb):
                pool.affine_select(out=m[:, :], in_=m[:, :], compare_op=ALU.not_equal, fill=1.0, base=0,
                                   pattern=[[-1, P]], channel_multiplier=1).then_inc(s_pconst, 1)
            pool.wait_ge(s_const, N_CONST)
            pool.wait_ge(s_small, 16 * N_SMALL)
            chain = Chain(pool, pool_at)
            link = chain.link

            def rsqrt(dst, src, n):
                link(pool.tensor_tensor(nrm[:, 7, 0:n], src, small[:, 0, 0:n], ALU.add))
                return pool.tensor_tensor(dst, nrm[:, 7, 0:n], small[:, 1, 0:n], ALU.pow)

            def norm_scales(g):
                chain.begin(g)
                pool.wait_ge(stats1.sem, stats1.count(g))
                mean, var = mv[:, 0, :, 0], mv[:, 0, :, 1]
                link(pool.tensor_tensor(nrm[:, 7, :], var, small[:, 0, :], ALU.add))
                chain.step(pool.tensor_tensor(nrm[:, 0, :], nrm[:, 7, :], small[:, 1, :], ALU.pow))
                link(pool.tensor_tensor(nrm[:, 2, :], nrm[:, 7, :], small[:, 2, :], ALU.pow))
                link(pool.tensor_tensor(nrm[:, 2, :], nrm[:, 2, :], var, ALU.mult))
                link(rsqrt(nrm[:, 3, :], nrm[:, 2, :], GB))
                pool.tensor_tensor(nrm[:, 4, :], nrm[:, 3, :], nrm[:, 0, :], ALU.mult).then_inc(norm1.sem, 1)
                link(pool.tensor_tensor(nrm[:, 1, :], nrm[:, 0, :], mean, ALU.mult))
                chain.step(pool.tensor_tensor(nrm[:, 5, :], nrm[:, 1, :], small[:, 2, :], ALU.mult))
                pool.tensor_tensor(nrm[:, 6, :], nrm[:, 0, :], ones[:, 0:GB], ALU.add).then_inc(base1.sem, 1)

            def add_bout(g, b):
                pool.wait_ge(base_rdy.sem, base_rdy.count(g, b + 1))
                pool.tensor_tensor(X[:, b, :], X[:, b, :], bout[:, :], ALU.add).then_inc(bo_added.sem, 1)

            def rotate(g, b):
                pool.wait_ge(kv_rdy.sem, kv_rdy.count(g, 2 * (b + 1)))
                rot = KV[:, b, :, 0:ROT]
                link(pool.tensor_tensor(rotc[:, :, :], rot, cos[:, :].unsqueeze(1).to_broadcast([P, 2, ROT]), ALU.mult))
                for o in range(2):
                    link(pool.tensor_tensor(rots[:, :, o::2], KV[:, b, :, 1 - o:ROT:2],
                                            sin[:, o::2].unsqueeze(1).to_broadcast([P, 2, ROT // 2]), ALU.mult))
                pool.tensor_tensor(rot, rotc[:, :, :], rots[:, :, :], ALU.add).then_inc(rot_done.sem, 1)
                pool.wait_ge(rot_done.sem, rot_done.count(g, b + 1))
                pool.wait_ge(norms.sem, norms.count(g, 2 * (b + 1)))
                pool.tensor_tensor(PR[:, b, :], KV[:, b, 0, :], KV[:, b, 1, :], ALU.mult).then_inc(pr_rdy.sem, 1)

            def token_weights(g, b):
                pool.wait_ge(norms.sem, norms.count(g, 2 * (b + 1)))
                link(pool.tensor_tensor(wn[:, b:b + 1], ss[:, b, 0:1], ss[:, b, 1:2], ALU.mult))
                link(pool.tensor_tensor(wn[:, b:b + 1], wn[:, b:b + 1], small[:, 1, 0:1], ALU.pow))
                pool.tensor_tensor(wn[:, b:b + 1], wn[:, b:b + 1], small[:, 3, 0:1], ALU.mult).then_inc(wn_rdy.sem, 1)

            def form_even_keys(g, b):
                pool.wait_ge(k_fm.sem, k_fm.count(g, b + 1))
                pool.wait_ge(k_hi.sem, k_hi.count(g, b + 1))
                if b >= 1:
                    pool.wait_ge(st_ps.sem, st_ps.count(g, KVH * b))
                for h in range(2):
                    gs, cs = slice(h * KVH // 2, (h + 1) * KVH // 2), slice(h * KVH * S // 2, (h + 1) * KVH * S // 2)
                    pool.tensor_tensor(kx[0:SLOT, gs, 0, :], kfm[0:SLOT, cs].rearrange("p (g t) -> p g t", t=S),
                                       khi[0:SLOT, cs].rearrange("p (g t) -> p g t", t=S), ALU.subtract).then_inc(kx_a.sem, 1)

            def form_odd_keys(g):
                pool.wait_ge(norm2.sem, norm2.count(g, 1))
                pool.tensor_tensor(kx[SLOT:P, :, 1, :], kfm[SLOT:P, :].rearrange("p (g t) -> p g t", g=KVH),
                                   khi[SLOT:P, :].rearrange("p (g t) -> p g t", g=KVH), ALU.subtract).then_inc(kx_b0.sem, 1)
                pool.wait_ge(kx_b0.sem, kx_b0.count(g))

            def query_norm(g, b):
                pool.wait_ge(stats2.sem, stats2.count(g, b + 1))
                rsqrt(nrm[:, 8, b:b + 1], mv[:, 1, b, 1:2], 1).then_inc(norm2.sem, 1)

            def low_exp(g, b, u):
                n = KVH * b + u
                pool.wait_ge(ex_hi.sem, ex_hi.count(g, n + 1))
                if n >= 2:
                    pool.wait_ge(pv_done.sem, pv_done.count(g, n - 1))
                pool.tensor_tensor(exl[:, n % 2, :], EX[:, n % 2, :], exh[:, n % 2, :], ALU.subtract).then_inc(ex_lo_p.sem, 1)

            def ffn_norm(g, b):
                pool.wait_ge(stats3.sem, stats3.count(g, b + 1))
                rsqrt(nrm[:, 9, b:b + 1], mv[:, 2, b, 1:2], 1).then_inc(norm3.sem, 1)

            def attention(g):
                norm_scales(g)
                for b in range(GB):
                    add_bout(g, b)
                for b in range(GB):
                    rotate(g, b)
                    token_weights(g, b)
                form_even_keys(g, 0)
                query_norm(g, 0)
                form_odd_keys(g)
                query_norm(g, 1)
                for u in range(0, KVH, 2):
                    low_exp(g, 0, u)
                form_even_keys(g, 1)
                ffn_norm(g, 0)
                for u in range(0, KVH, 2):
                    low_exp(g, 1, u)
                ffn_norm(g, 1)
                chain.end()

            attention(0)
            with pool.Fori(0, NG - 1) as i:
                attention(i + 1)

        @block.scalar
        def _(act):
            act.wait_ge(s_small, 16 * N_SMALL)
            act.wait_ge(s_const, N_CONST)
            act.wait_ge(s_pconst, N_PCONST)

            def high_weights(i):
                if i == BEFORE_W2:
                    act.wait_ge(s_lo, BEFORE_W2)
                act.wait_ge(s_stage[slot_of[i]], stage_count(i))
                act.activation(pieces[i][2], staged(i), ACT.Copy, scale=pieces[i][4]).then_inc(s_hi, 1)

            for i in range(FIRST):
                high_weights(i)

            def high_xn(g, b):
                act.wait_ge(xnT_ps.sem, xnT_ps.count(g, b + 1))
                act.activation(xnT[:, 0, :, b * S:(b + 1) * S], AB[b][:, :].rearrange("p (k t) -> p k t", k=KC), ACT.Copy, scale=SX).then_inc(xn_hi.sem, 1)

            def kv_norms(g, b):
                act.wait_ge(rot_done.sem, rot_done.count(g, b + 1))
                for o in range(2):
                    act.activation(junk[:, :], KV[:, b, o, :], ACT.Square, accum_out=ss[:, b, o:o + 1]).then_inc(norms.sem, 1)
                    act.wait_ge(norms.sem, norms.count(g, 2 * b + o + 1))

            def high_product(g, b):
                act.wait_ge(pr_rdy.sem, pr_rdy.count(g, b + 1))
                act.wait_ge(wn_rdy.sem, wn_rdy.count(g, b + 1))
                act.activation(prs[:, b, 0, :], PR[:, b, :], ACT.Copy, scale=wn[:, b:b + 1]).then_inc(pr_hi.sem, 1)

            def scale_q(g, b):
                act.wait_ge(a_rdy.sem, a_rdy.count(g, b + 1))
                act.wait_ge(q_ps.sem, q_ps.count(g))
                for c in range(KC):
                    src = AB[1 + c // 2][:, (c % 2) * T + b * S:(c % 2) * T + (b + 1) * S]
                    act.activation(QA[:, b, c, :], src, ACT.Identity,
                                   scale=acol[:, b, c:c + 1], bias=bqa[:, b, c:c + 1]).then_inc(qa_rdy.sem, 1)

            def high_keys(g, b):
                act.wait_ge(k_in.sem, k_in.count(g, 8 * (b + 1)))
                if b == 0:
                    act.wait_ge(pr_lo.sem, pr_lo.count(g))
                else:
                    act.wait_ge(kx_a.sem, kx_a.count(g, 2 * b))
                    act.wait_ge(kx_b0.sem, kx_b0.count(g))
                act.activation(khi[:, :], kst[:, :], ACT.Copy, scale=kform[:, 0:1]).then_inc(k_hi.sem, 1)

            def full_keys(g, b):
                act.activation(kfm[:, :], kst[:, :], ACT.Identity, scale=kform[:, 1:2], bias=kform[:, 2:3]).then_inc(k_fm.sem, 1)

            def high_values(g, b):
                act.wait_ge(v_in.sem, v_in.count(g))
                if b >= 1:
                    act.wait_ge(pv_done.sem, pv_done.count(g, KVH * b))
                act.activation(vx[:, :, 0:DH], vst[:, b, :].rearrange("p (g e) -> p g e", g=KVH), ACT.Copy, scale=SQ).then_inc(v_hi.sem, 1)

            def high_query(g, b):
                act.wait_ge(q2_rdy.sem, q2_rdy.count(g, b + 1))
                if b >= 1:
                    act.wait_ge(qxT_ps.sem, qxT_ps.count(g, 4 * b))
                act.activation(Qx[:, :, :].rearrange("p h (s e) -> p h s e", e=DH)[:, :, 0:3:2, :],
                                      Q2[:, b, :].rearrange("p (h e) -> p h e", h=NH).unsqueeze(2).to_broadcast([P, NH, 2, DH]), ACT.Copy, scale=SQ).then_inc(qx_hi.sem, 1)

            def second_queries(g, b, turn):
                act.wait_ge(qxT_ps.sem, qxT_ps.count(g, 4 * b + 2 * turn + 2))
                src = AB[2][:, :].bitcast(F16).rearrange("p (q t) -> p q t", t=P)
                act.activation(QxT[:, PAIRS // 2:, :], src, ACT.Copy).then_inc(qxT_b.sem, 1)

            def exps(g, b, u):
                n = KVH * b + u
                act.wait_ge(st_ps.sem, st_ps.count(g, n + 1))
                if n >= 2:
                    low = ex_lo_v if n % 2 else ex_lo_p
                    act.wait_ge(low.sem, low.count(g, n // 2))
                act.activation(EX[:, n % 2, :], AB[1 + u % 2][:, :], ACT.Exp, scale=SCORE_SCALE / (SQ * SQ), bias=lnsa[:, :]).then_inc(ex_rdy.sem, 1)

            def keep_x2(g, b):
                act.wait_ge(x2_rdy.sem, x2_rdy.count(g, 2 * (b + 1)))
                if not (isinstance(g, int) and g == 0):
                    act.wait_ge(out_rdy.sem, out_rdy.count(g - 1, b + 1))
                act.activation(XF[:, b, :], X[:, b, :], ACT.Copy).then_inc(xf_rdy.sem, 1)

            def high_h3(g, b):
                act.wait_ge(h3T_ps.sem, h3T_ps.count(g, b + 1))
                act.activation(h3T[:, 0, :, b * S:(b + 1) * S], AB[b][:, :].rearrange("p (k t) -> p k t", k=KC), ACT.Copy, scale=SX).then_inc(h3_hi.sem, 1)

            def router_exps(g):
                act.wait_ge(top_rdy.sem, top_rdy.count(g))
                for b in range(GB):
                    act.activation(sel[:, 7, b, :], lg[:, b, :], ACT.Exp, bias=top[:, 1, b:b + 1], accum_out=sume[:, b:b + 1]).then_inc(rho_rdy.sem, 1)
                    act.activation(rho[:, b:b + 1], top[:, 2, b:b + 1], ACT.Exp, bias=top[:, 1, b:b + 1]).then_inc(rho_rdy.sem, 1)

            def first_gelu(g, c):
                act.wait_ge(f1_ps.sem, f1_ps.count(g, c + 1))
                if c >= 2:
                    act.wait_ge(hs_rdy.sem, hs_rdy.count(g, c - 1))
                act.activation(H1[:, c % 2, :], HB[c][:, 0:T], ACT.Gelu_apprx_tanh, bias=b1c[:, c:c + 1], scale=1.0 / (SX * SW)).then_inc(h1_rdy.sem, 1)

            def second_gelu(g, c):
                act.wait_ge(f2_ps.sem, f2_ps.count(g, c + 1))
                if c >= 2:
                    act.wait_ge(t2_rdy.sem, t2_rdy.count(g, c - 1))
                act.activation(H2[:, c % 2, :], HB[c][:, 0:T], ACT.Gelu_apprx_tanh, bias=b1c[:, c:c + 1], scale=1.0 / (SX * SW)).then_inc(h2_rdy.sem, 1)

            def high_hidden(g, c):
                act.wait_ge(t2_rdy.sem, t2_rdy.count(g, c + 1))
                if c >= 2:
                    act.wait_ge(u2_used.sem, u2_used.count(g, c - 1))
                act.activation(t2s[:, c % 2, 0, :], T2[:, c % 2, :], ACT.Copy).then_inc(t2_hi.sem, 1)
                act.wait_ge(hs_rdy.sem, hs_rdy.count(g, c + 1))
                act.activation(hs[:, 0, c, :], HS[:, c % 2, :], ACT.Copy).then_inc(hs_hi.sem, 1)

            def body(f, n):
                for c in range(FC + 1):
                    if f is not None:
                        if c < FC:
                            first_gelu(f, c)
                        if c >= 1:
                            high_hidden(f, c - 1)
                    if n is not None:
                        if c == 3:
                            high_xn(n, 0)
                            high_xn(n, 1)
                        if c == 10:
                            high_product(n, 1)
                        if c == 15:
                            second_queries(n, 0, 0)
                    if f is not None and c < FC:
                        second_gelu(f, c)
                    if f is None and c < n_pieces - FIRST:
                        high_weights(FIRST + c)
                    if n is None:
                        continue
                    if c in (6, 8):
                        kv_norms(n, (c - 6) // 2)
                    if c == 7:
                        high_product(n, 0)
                    if c in (9, 11):
                        scale_q(n, (c - 9) // 2)
                    if c == 10:
                        high_keys(n, 0)
                    if c == 12:
                        full_keys(n, 0)
                        high_values(n, 0)
                    if c == 13:
                        high_query(n, 0)
                if n is None:
                    return
                high_keys(n, 1)
                full_keys(n, 1)
                second_queries(n, 0, 1)
                for u in range(KVH):
                    exps(n, 0, u)
                    if u == 3:
                        high_query(n, 1)
                high_values(n, 1)
                second_queries(n, 1, 0)
                second_queries(n, 1, 1)
                for u in range(KVH):
                    exps(n, 1, u)
                    if u == 3:
                        high_h3(n, 0)
                    if u == 6:
                        keep_x2(n, 0)
                high_h3(n, 1)
                keep_x2(n, 1)
                router_exps(n)
                if f is not None:
                    act.wait_ge(out_st.sem, out_st.count(f))

            body(None, 0)
            with act.Fori(0, NG - 1) as i:
                body(i, i + 1)
            body(NG - 1, None)

        @block.vector
        def _(dve):
            dve.memset(ones[:, :], 1.0).then_inc(s_const, 1)
            dve.memset(Qx[:, :, :], 0.0).then_inc(s_const, 1)
            dve.memset(kx[:, :, :, :], 0.0).then_inc(s_const, 1)
            dve.memset(vx[:, :, DH:DH + 1], SQ).then_inc(s_const, 1)
            dve.memset(ones16[:, :], 1.0).then_inc(s_const, 1)
            dve.memset(lnsa[:, :], float(np.log(SA))).then_inc(s_const, 1)
            for e in range(NE):
                dve.memset(descend[:, e:e + 1], float(NE - e)).then_inc(s_const, 1)
            dve.wait_ge(s_small, 16 * N_SMALL)
            dve.tensor_scalar(gammaS[:, :], gamma[:, :], SW, None, ALU.mult).then_inc(s_const, 1)
            dve.tensor_copy(beta_b[:, :, :], beta[:, :].unsqueeze(2).to_broadcast([P, KC, P])).then_inc(s_const, 1)
            dve.wait_ge(s_const, N_CONST)
            dve.wait_ge(s_pconst, N_PCONST)
            def low_weights(i):
                loads, shape, hi, lo, scale = pieces[i]
                rows = lo.shape[0]
                dve.wait_ge(s_hi, i + 1)
                dve.scalar_tensor_tensor(lo, staged(i, rows), scale, hi[0:rows], ALU.mult, ALU.subtract).then_inc(s_lo, 1)

            for i in range(FIRST):
                low_weights(i)
            dve.wait_ge(s_beta, KC)
            for h in range(2):
                dve.tensor_tensor(bkv[:, h * D:(h + 1) * D], AB[h][:, :], bkv[:, h * D:(h + 1) * D], ALU.add).then_inc(s_bias, 1)
            dve.tensor_tensor(bq[:, :], AB[2][:, 0:KC], bq[:, :], ALU.add).then_inc(s_bias, 1)
            dve.wait_ge(s_bias, 3)
            dve.wait_ge(s_lo, FIRST)
            chain = Chain(dve, dve_at)
            link = chain.link

            def stats(src, norm, b, sig_):
                link(dve.bn_stats(stat[:, b, :], src))
                dve.memset(fence[:, 0:1], 0.0)
                dve.bn_aggr(mv[:, norm, b, :], stat[:, b, :]).then_inc(sig_.sem, 1)

            def stats_x(g):
                chain.begin(g)
                dve.wait_ge(x_in.sem, x_in.count(g))
                for b in range(GB):
                    stats(X[:, b, :], 0, b, stats1)

            def norm_x(g):
                dve.wait_ge(norm1.sem, norm1.count(g))
                for b in range(GB):
                    dve.tensor_scalar(XN[:, b, :], X[:, b, :], mv[:, 0, b, 0:1], nrm[:, 4, b:b + 1], ALU.subtract, ALU.mult).then_inc(xn_rdy.sem, 1)
                for b in range(GB):
                    dve.wait_ge(base1.sem, base1.count(g))
                    dve.wait_ge(pool_at.sem, pool_at.count(g, NORM_STEPS))
                    dve.wait_ge(xn_rdy.sem, xn_rdy.count(g, b + 1))
                    dve.tensor_scalar(X[:, b, :], X[:, b, :], nrm[:, 6, b:b + 1], nrm[:, 5, b:b + 1], ALU.mult, ALU.add).then_inc(base_rdy.sem, 1)

            def low_xn(g, b):
                dve.wait_ge(xn_hi.sem, xn_hi.count(g, b + 1))
                bs = slice(b * S, (b + 1) * S)
                dve.scalar_tensor_tensor(xnT[:, 1, :, bs], AB[b][:, :].rearrange("p (k t) -> p k t", k=KC), SX, xnT[:, 0, :, bs], ALU.mult, ALU.subtract).then_inc(xn_lo.sem, 1)

            def bias_kv(g, b):
                dve.wait_ge(kv_ps.sem, kv_ps.count(g, b + 1))
                for h in range(2):
                    bank = AB[(2 + 2 * b + h) % 5]
                    dve.scalar_tensor_tensor(KV[:, b, h, :], bank[:, :], 1.0 / (SX * SW), bkv[:, h * D:(h + 1) * D], ALU.mult, ALU.add).then_inc(kv_rdy.sem, 1)

            def low_product(g, b):
                dve.wait_ge(pr_hi.sem, pr_hi.count(g, b + 1))
                dve.scalar_tensor_tensor(prs[:, b, 1, :], PR[:, b, :], wn[:, b:b + 1], prs[:, b, 0, :], ALU.mult, ALU.subtract).then_inc(pr_lo.sem, 1)

            def make_a(g, b):
                dve.wait_ge(a_ps.sem, a_ps.count(g, b + 1))
                link(dve.tensor_scalar(asum[:, b, :], AB[3][:, b * KC:(b + 1) * KC],
                                       (1.0 - IDENTITY_WEIGHT) / SA, IDENTITY_WEIGHT, ALU.mult, ALU.add))
                link(dve.tensor_scalar(acol[:, b, :], asum[:, b, :], SQ / (SX * SW), None, ALU.mult))
                dve.scalar_tensor_tensor(bqa[:, b, :], asum[:, b, :], SQ, bq[:, :], ALU.mult, ALU.mult).then_inc(a_rdy.sem, 1)

            def split_qa(g, b):
                bs = slice(b * S, (b + 1) * S)
                dve.wait_ge(qa_rdy.sem, qa_rdy.count(g, KC * (b + 1)))
                dve.tensor_copy(qas[:, 0, :, bs], QA[:, b]).then_inc(qa_hi.sem, 1)
                dve.wait_ge(qa_hi.sem, qa_hi.count(g, b + 1))
                dve.tensor_tensor(qas[:, 1, :, bs], QA[:, b], qas[:, 0, :, bs], ALU.subtract).then_inc(qa_lo.sem, 1)

            def make_x1(g, b):
                dve.wait_ge(y_ps.sem, y_ps.count(g, b + 1))
                dve.wait_ge(bo_added.sem, bo_added.count(g, b + 1))
                dve.scalar_tensor_tensor(X[:, b, :], AB[(4 + b) % 5][:, :], 1.0 / (SQ * SW), X[:, b, :], ALU.mult, ALU.add).then_inc(x1_rdy.sem, 1)
                dve.wait_ge(x1_rdy.sem, x1_rdy.count(g, b + 1))
                stats(X[:, b, :], 1, b, stats2)

            def make_query(g, b):
                dve.wait_ge(norm2.sem, norm2.count(g, b + 1))
                dve.tensor_scalar(Q2[:, b, :], X[:, b, :], mv[:, 1, b, 0:1], nrm[:, 8, b:b + 1], ALU.subtract, ALU.mult).then_inc(q2_rdy.sem, 1)

            def form_odd_keys(g):
                dve.wait_ge(k_hi.sem, k_hi.count(g, 2))
                dve.wait_ge(k_fm.sem, k_fm.count(g, 2))
                dve.wait_ge(st_ps.sem, st_ps.count(g, KVH))
                dve.tensor_tensor(kx[SLOT:P, :, 1, :], kfm[SLOT:P, :].rearrange("p (g t) -> p g t", g=KVH),
                                  khi[SLOT:P, :].rearrange("p (g t) -> p g t", g=KVH), ALU.subtract).then_inc(kx_b1.sem, 1)

            def low_values(g, b):
                dve.wait_ge(v_hi.sem, v_hi.count(g, b + 1))
                dve.scalar_tensor_tensor(vx[:, :, DH + 1:], vst[:, b, :].rearrange("p (g e) -> p g e", g=KVH), SQ,
                                                vx[:, :, 0:DH], ALU.mult, ALU.subtract).then_inc(v_lo.sem, 1)

            def low_query(g, b):
                if b >= 1:
                    dve.wait_ge(qxT_ps.sem, qxT_ps.count(g, 4 * b))
                link(dve.memset(Qx[:, :, 3 * DH:3 * DH + 2], 0.0))
                dve.wait_ge(qx_hi.sem, qx_hi.count(g, b + 1))
                dve.scalar_tensor_tensor(Qx[:, :, DH:2 * DH], Q2[:, b, :].rearrange("p (h e) -> p h e", h=NH), SQ, Qx[:, :, 0:DH], ALU.mult, ALU.subtract).then_inc(qx_lo.sem, 1)

            def first_queries(g, b, turn):
                dve.wait_ge(qxT_ps.sem, qxT_ps.count(g, 4 * b + 2 * turn + 1))
                src = AB[1][:, :].bitcast(F16).rearrange("p (q t) -> p q t", t=P)
                dve.tensor_copy(QxT[:, 0:PAIRS // 2, :], src).then_inc(qxT_a.sem, 1)

            def take_max(g, b, u):
                dve.wait_ge(sc_ps.sem, sc_ps.count(g, KVH * b + u + 1))
                dve.tensor_reduce(negm[:, HPG * u:HPG * (u + 1)], AB[3 + u % 2][:, :].rearrange("p (h t) -> p h t", h=HPG),
                                  AX.X, ALU.max, negate=True).then_inc(max_done.sem, 1)

            def split_max(g, b):
                dve.wait_ge(max_done.sem, max_done.count(g, KVH * (b + 1)))
                hi, lo = (Qx[:, :, 3 * DH + i] for i in range(2))
                link(dve.tensor_scalar(hi, negm[:, :], 1.0 / SM, None, ALU.mult))
                dve.scalar_tensor_tensor(lo, negm[:, :], 1.0 / SM, hi, ALU.mult, ALU.subtract).then_inc(mp_rdy.sem, 1)

            def split_exp(g, b, u):
                n = KVH * b + u
                dve.wait_ge(ex_rdy.sem, ex_rdy.count(g, n + 1))
                if n >= 2:
                    dve.wait_ge(pv_done.sem, pv_done.count(g, n - 1))
                dve.tensor_copy(exh[:, n % 2, :], EX[:, n % 2, :]).then_inc(ex_hi.sem, 1)
                if n % 2 == 1:
                    dve.wait_ge(ex_hi.sem, ex_hi.count(g, n + 1))
                    dve.tensor_tensor(exl[:, n % 2, :], EX[:, n % 2, :], exh[:, n % 2, :], ALU.subtract).then_inc(ex_lo_v.sem, 1)

            def divide_values(g, b, h):
                dve.wait_ge(pv_done.sem, pv_done.count(g, KVH * b + HPG * (h + 1)))
                acc = AB[3 + h][:, 0:NH // 2 * (DH + 1)].rearrange("p (h e) -> p h e", e=DH + 1)
                link(dve.reciprocal(rl[:, h, :].unsqueeze(2), acc[:, :, DH:DH + 1]))
                dve.tensor_tensor(ON[:, h, :].rearrange("p (h e) -> p h e", e=DH), acc[:, :, 0:DH],
                                  rl[:, h, :].unsqueeze(2).to_broadcast([P, NH // 2, DH]), ALU.mult).then_inc(on_rdy.sem, 1)

            def add_attention(g, b, h):
                dve.wait_ge(on_rdy.sem, on_rdy.count(g, 2 * b + h + 1))
                half = slice(h * D // 2, (h + 1) * D // 2)
                dve.tensor_tensor(X[:, b, half], X[:, b, half], ON[:, h, :], ALU.add).then_inc(x2_rdy.sem, 1)

            def stats_x2(g, b):
                dve.wait_ge(x2_rdy.sem, x2_rdy.count(g, 2 * (b + 1)))
                stats(X[:, b, :], 2, b, stats3)

            def make_h3(g, b):
                dve.wait_ge(norm3.sem, norm3.count(g, b + 1))
                dve.tensor_scalar(XN[:, b, :], X[:, b, :], mv[:, 2, b, 0:1], nrm[:, 9, b:b + 1], ALU.subtract, ALU.mult).then_inc(h3_rdy.sem, 1)

            def low_h3(g, b):
                dve.wait_ge(h3_hi.sem, h3_hi.count(g, b + 1))
                bs = slice(b * S, (b + 1) * S)
                dve.scalar_tensor_tensor(h3T[:, 1, :, bs], AB[b][:, :].rearrange("p (k t) -> p k t", k=KC), SX, h3T[:, 0, :, bs], ALU.mult, ALU.subtract).then_inc(h3_lo.sem, 1)

            def spread(v):
                return v.unsqueeze(2).to_broadcast([P, GB, NE])

            def first_of(logits, top_, mask):
                link(dve.tensor_tensor(sel[:, 0], logits, spread(top_), ALU.is_equal))
                link(dve.tensor_tensor(sel[:, 1], sel[:, 0], descend[:, :].unsqueeze(1).to_broadcast([P, GB, NE]), ALU.mult))
                link(dve.tensor_reduce(top[:, 3, :].unsqueeze(2), sel[:, 1], AX.X, ALU.max))
                link(dve.tensor_tensor(mask, sel[:, 1], spread(top[:, 3, :]), ALU.is_equal))

            def read_router(g, b):
                dve.wait_ge(u1_ps.sem, u1_ps.count(g, b + 1))
                link(dve.tensor_reduce(rt[:, b, :].unsqueeze(2), AB[0][:, b * 2 * U1W:(b + 1) * 2 * U1W].rearrange("p (h w) -> p w h", h=2), AX.X, ALU.add))

            def route(g):
                link(dve.scalar_tensor_tensor(lg[:, :, :], rt[:, :, ER:U1W], 1.0 / (SX * SW), brb[:, :].unsqueeze(1).to_broadcast([P, GB, NE]), ALU.mult, ALU.add))
                chain.step(dve.tensor_reduce(top[:, 1, :].unsqueeze(2), lg[:, :, :], AX.X, ALU.max, negate=True))
                link(dve.tensor_reduce(top[:, 0, :].unsqueeze(2), lg[:, :, :], AX.X, ALU.max))
                first_of(lg[:, :, :], top[:, 0, :], sel[:, 2])
                link(dve.scalar_tensor_tensor(sel[:, 3], sel[:, 2], -HUGE, lg[:, :, :], ALU.mult, ALU.add))
                dve.tensor_reduce(top[:, 2, :].unsqueeze(2), sel[:, 3], AX.X, ALU.max).then_inc(top_rdy.sem, 1)
                dve.wait_ge(top_rdy.sem, top_rdy.count(g))
                first_of(sel[:, 3], top[:, 2, :], sel[:, 4])
                u1 = rt[:, :, 0:ER].rearrange("p b (e r) -> p b e r", r=R)

                def masked(k, m):
                    return dve.tensor_tensor(zf[:, :, k, :].rearrange("p b (e r) -> p b e r", r=R), u1,
                                             sel[:, m].unsqueeze(3).to_broadcast([P, GB, NE, R]), ALU.mult)
                chain.step(masked(0, 2))
                link(dve.tensor_tensor(sel[:, 5], sel[:, 4], sel[:, 2], ALU.subtract))
                link(masked(1, 5))
                link(dve.tensor_scalar(zz[:, :, :, 0, :], zf[:, :, :, :], 1.0 / SW, None, ALU.mult))
                dve.scalar_tensor_tensor(zz[:, :, :, 1, :].rearrange("p b k e -> p (b k) e"), zf[:, :, :, :].rearrange("p b k e -> p (b k) e"), 1.0 / SW,
                                                zz[:, :, :, 0, :].rearrange("p b k e -> p (b k) e"), ALU.mult, ALU.subtract).then_inc(zz_rdy.sem, 1)
                dve.wait_ge(rho_rdy.sem, rho_rdy.count(g))
                for b in range(GB):
                    dve.tensor_scalar(drho[:, b, :], idf[:, :], rho[:, b:b + 1], None, ALU.mult).then_inc(drho_rdy.sem, 1)

            def finish_routing(g):
                dve.wait_ge(zT_ps.sem, zT_ps.count(g))
                dve.tensor_copy(zT[:, :, :], AB[0][:, 0:T].bitcast(F16).rearrange("p (k t) -> p k t", k=2)).then_inc(zT_rdy.sem, 1)
                dve.wait_ge(rho_ps.sem, rho_ps.count(g))
                dve.tensor_scalar(rhoB[:, :], AB[1][:, 0:T], SH, None, ALU.mult).then_inc(rhoB_rdy.sem, 1)
                dve.wait_ge(rhoB_rdy.sem, rhoB_rdy.count(g))

            def expert_weights(g):
                ff.begin(g)
                ff.step(dve.tensor_scalar(rho1[:, :], rho[:, :], 1.0, None, ALU.add))
                ff.link(dve.reciprocal(w1st[:, :], sume[:, :]))
                ff.link(dve.tensor_tensor(both[:, :], rho1[:, :], w1st[:, :], ALU.mult))
                ff.link(dve.tensor_scalar(w1st[:, :], w1st[:, :], 1.0 / (SH * SW), None, ALU.mult))

            ff = Chain(dve, dve_ff)

            def weigh_hidden(g, c):
                s = c % 2
                dve.wait_ge(h2_rdy.sem, h2_rdy.count(g, c + 1))
                if c >= 2:
                    dve.wait_ge(t2_hi.sem, t2_hi.count(g, c - 1))
                    dve.wait_ge(t2_lo.sem, t2_lo.count(g, c - 1))
                dve.tensor_tensor(T2[:, s, :], H2[:, s, :], rhoB[:, :], ALU.mult).then_inc(t2_rdy.sem, 1)
                dve.wait_ge(t2_rdy.sem, t2_rdy.count(g, c + 1))
                dve.wait_ge(h1_rdy.sem, h1_rdy.count(g, c + 1))
                if c >= 2:
                    dve.wait_ge(hs_lo.sem, hs_lo.count(g, c - 1))
                dve.scalar_tensor_tensor(HS[:, s, :], H1[:, s, :], SH, T2[:, s, :], ALU.mult, ALU.add).then_inc(hs_rdy.sem, 1)

            def low_weighted(g, c):
                s = c % 2
                dve.wait_ge(t2_hi.sem, t2_hi.count(g, c + 1))
                if c >= 2:
                    dve.wait_ge(u2_used.sem, u2_used.count(g, c - 1))
                dve.tensor_tensor(t2s[:, s, 1, :], T2[:, s, :], t2s[:, s, 0, :], ALU.subtract).then_inc(t2_lo.sem, 1)
                dve.wait_ge(hs_hi.sem, hs_hi.count(g, c + 1))
                dve.tensor_tensor(hs[:, 1, c, :], HS[:, s, :], hs[:, 0, c, :], ALU.subtract).then_inc(hs_lo.sem, 1)

            def read_second_down(g):
                dve.wait_ge(u2_used.sem, u2_used.count(g))
                dve.wait_ge(t2_lo.sem, t2_lo.count(g))
                dve.wait_ge(hs_rdy.sem, hs_rdy.count(g))
                dve.tensor_reduce(u2[:, :, :].unsqueeze(3), UBv[:, 0:GB].rearrange("p b h e -> p b e h"), AX.X, ALU.add).then_inc(u2_ev.sem, 1)

            def adapter_out(g):
                dve.wait_ge(us_ps.sem, us_ps.count(g))
                ff.link(dve.tensor_reduce(us[:, :, :].unsqueeze(3), UBv[:, 2:2 + GB].rearrange("p b h e -> p b e h"), AX.X, ALU.add))
                dve.wait_ge(u2_ev.sem, u2_ev.count(g))

                def masked(dst, src, m):
                    return dve.tensor_tensor(dst.rearrange("p b (e r) -> p b e r", r=R), src.rearrange("p b (e r) -> p b e r", r=R),
                                             sel[:, m].unsqueeze(3).to_broadcast([P, GB, NE, R]), ALU.mult)
                ff.link(masked(z2f[:, :, :], us[:, :, :], 2))
                ff.link(masked(z2g[:, :, :], u2[:, :, :], 5))
                ff.link(dve.tensor_tensor(z2f[:, :, :], z2f[:, :, :], z2g[:, :, :], ALU.add))
                ff.link(dve.tensor_scalar(z2s[:, :, 0, :], z2f[:, :, :], 1.0 / SW, None, ALU.mult))
                dve.scalar_tensor_tensor(z2s[:, :, 1, :], z2f[:, :, :], 1.0 / SW, z2s[:, :, 0, :], ALU.mult, ALU.subtract).then_inc(z2_rdy.sem, 1)

            def keep_z2(g):
                dve.wait_ge(z2T_ps.sem, z2T_ps.count(g))
                dve.tensor_copy(z2T[:, :, :], UB[:, 0:GB * S // 2].bitcast(F16).rearrange("p (b t) -> p b t", b=GB)).then_inc(z2T_rdy.sem, 1)

            def add_b2(g, b):
                dve.wait_ge(xf_rdy.sem, xf_rdy.count(g, b + 1))
                dve.scalar_tensor_tensor(XF[:, b, :], b2b[:, :], both[:, b:b + 1], XF[:, b, :], ALU.mult, ALU.add).then_inc(b2_added.sem, 1)

            def output(g, b, bank):
                dve.wait_ge(yf_ps.sem, yf_ps.count(g, b + 1))
                dve.wait_ge(b2_added.sem, b2_added.count(g, b + 1))
                dve.scalar_tensor_tensor(OUT[:, b, :], bank[:, :], w1st[:, b:b + 1], XF[:, b, :], ALU.mult, ALU.add).then_inc(out_rdy.sem, 1)

            def body(f, n):
                if f is not None:
                    finish_routing(f)
                if n is not None:
                    stats_x(n)
                if f is not None:
                    expert_weights(f)
                for c in range(FC + 1):
                    if f is not None and c >= 1:
                        low_weighted(f, c - 1)
                    if n is not None:
                        if c == 3:
                            low_xn(n, 0)
                            low_xn(n, 1)
                        if c in (5, 7):
                            bias_kv(n, (c - 5) // 2)
                        if c == 8:
                            low_product(n, 0)
                        if c == 9:
                            make_a(n, 0)
                        if c == 11:
                            make_a(n, 1)
                        if c in (10, 12):
                            split_qa(n, (c - 10) // 2)
                        if c == 13:
                            make_query(n, 0)
                        if c == 14:
                            low_query(n, 0)
                        if c == 15:
                            first_queries(n, 0, 0)
                        if c == 16:
                            take_max(n, 0, 2)
                    if f is not None:
                        if c < FC:
                            weigh_hidden(f, c)
                        if c in (4, 6):
                            add_b2(f, (c - 4) // 2)
                    elif c < n_pieces - FIRST:
                        low_weights(FIRST + c)
                    if n is None:
                        continue
                    if c == 1:
                        norm_x(n)
                    if c == 10:
                        low_product(n, 1)
                    if c == 12:
                        make_x1(n, 0)
                    if c == 13:
                        low_values(n, 0)
                    if c == 15:
                        take_max(n, 0, 0)
                        take_max(n, 0, 1)
                if n is None:
                    read_second_down(f)
                    adapter_out(f)
                    keep_z2(f)
                    for b in range(GB):
                        output(f, b, YL[b])
                    ff.end()
                    return
                for u in range(3, KVH):
                    take_max(n, 0, u)
                split_max(n, 0)
                first_queries(n, 0, 1)
                if f is not None:
                    read_second_down(f)
                make_x1(n, 1)
                for u in range(KVH):
                    split_exp(n, 0, u)
                    if u == 0:
                        make_query(n, 1)
                    if u == 1 and f is not None:
                        adapter_out(f)
                    if u == 3 and f is not None:
                        keep_z2(f)
                    if u == 4:
                        low_query(n, 1)
                    if u == 6:
                        divide_values(n, 0, 0)
                        add_attention(n, 0, 0)
                form_odd_keys(n)
                first_queries(n, 1, 0)
                divide_values(n, 0, 1)
                for u in range(KVH):
                    take_max(n, 1, u)
                    if u == 0:
                        add_attention(n, 0, 1)
                split_max(n, 1)
                first_queries(n, 1, 1)
                stats_x2(n, 0)
                low_values(n, 1)
                for u in range(KVH):
                    split_exp(n, 1, u)
                    if u == 0:
                        make_h3(n, 0)
                    if u == 2 and f is not None:
                        output(f, 0, FB[0])
                    if u == 4:
                        low_h3(n, 0)
                    if u == 6:
                        divide_values(n, 1, 0)
                        add_attention(n, 1, 0)
                divide_values(n, 1, 1)
                add_attention(n, 1, 1)
                stats_x2(n, 1)
                make_h3(n, 1)
                if f is not None:
                    output(f, 1, FB[1])
                    dve.wait_ge(out_rdy.sem, out_rdy.count(f))
                    ff.end()
                read_router(n, 0)
                low_h3(n, 1)
                read_router(n, 1)
                route(n)
                if f is not None:
                    dve.wait_ge(out_st.sem, out_st.count(f))
                chain.end()

            body(None, 0)
            with dve.Fori(0, NG - 1) as i:
                body(i, i + 1)
            body(NG - 1, None)

        @block.tensor
        def _(pe):
            AHEAD = 4
            W2_BESIDE = (2, 2, (0, 0, 1, 1, 1, 1, 1, 1, 1, 1), 2, (1, 0, 1, 0, 1, 0, 1, 0), 2, (0, 1, 1, 1, 1, 1, 1, 1, 1, 1), 3)
            PASSES = ((0, 0), (0, 1), (1, 0))
            pe.wait_ge(s_const, N_CONST)
            pe.wait_ge(s_pconst, N_PCONST)
            for k in range(KC):
                pe.wait_ge(s_stage[slot_of[k]], stage_count(k))
                for h in range(2):
                    pe.matmul(AB[h][:, :], beta_b[:, k, :], staged(k)[:, (1 + h) * D:(2 + h) * D], start=(k == 0), stop=(k == KC - 1))
                for c in range(KC):
                    last = pe.matmul(AB[2][:, c:c + 1], staged(k)[:, c * P:(c + 1) * P], beta[:, k:k + 1],
                                     start=(k == 0 and c == 0), stop=(k == KC - 1), skip_group_check=True)
                last.then_inc(s_beta, 1)
            pe.wait_ge(s_bias, 3)
            pe.wait_ge(s_lo, FIRST)

            def mm(*a, **k):
                return pe.matmul(*a, **k)

            def to_width(g, b, src_rdy, done):
                pe.wait_ge(src_rdy.sem, src_rdy.count(g, b + 1))
                for k in range(KC):
                    last = pe.transpose(AB[b][:, k * P:(k + 1) * P], XN[:, b, k * P:(k + 1) * P], idf[:, :])
                last.then_inc(done.sem, 1)

            def project_kv(g, b, half):
                if half == 0:
                    pe.wait_ge(xn_lo.sem, xn_lo.count(g, b + 1))
                    if not (isinstance(g, int) and g == 0):
                        pe.wait_ge(h2_rdy.sem, h2_rdy.count(g - 1, 2 + b))
                bs = slice(b * S, (b + 1) * S)
                out = [AB[(2 + 2 * b + h) % 5] for h in range(2)]
                for k in range(2 * half, 2 * half + 2):
                    for xp in range(2):
                        for h in range(2):
                            for wp in range(2 - xp):
                                last = mm(out[h][:, :], xnT[:, xp, k, bs], w_in[:, wp, k, (1 + h) * D:(2 + h) * D],
                                          start=(k == 0 and xp == 0 and wp == 0), stop=(k == KC - 1 and xp == 1),
                                          skip_group_check=True)
                if half == 1:
                    last.then_inc(kv_ps.sem, 1)

            def project_q(g, c):
                if c == 2:
                    pe.wait_ge(kv_rdy.sem, kv_rdy.count(g, 1))
                for k in range(KC):
                    for xp, wp in PASSES:
                        last = mm(AB[1 + c // 2][:, (c % 2) * T:(c % 2 + 1) * T], w_in[:, wp, k, c * P:(c + 1) * P], xnT[:, xp, k, :],
                                  start=(k == 0 and (xp, wp) == PASSES[0]), stop=(k == KC - 1 and (xp, wp) == PASSES[-1]))
                if c % 2 == 1:
                    last.then_inc(q_ps.sem, 1)

            def sum_tokens(g, b):
                if b == 0:
                    pe.wait_ge(kv_rdy.sem, kv_rdy.count(g, 2))
                else:
                    pe.wait_ge(a_rdy.sem, a_rdy.count(g, b))
                pe.wait_ge(pr_lo.sem, pr_lo.count(g, b + 1))
                pe.wait_ge(pr_hi.sem, pr_hi.count(g, b + 1))
                for c in range(KC):
                    col = b * KC + c
                    for part in range(2):
                        last = mm(AB[3][:, col:col + 1], prs[:, b, part, c * P:(c + 1) * P], ones16[:, :], start=(part == 0), stop=(part == 1))
                last.then_inc(a_ps.sem, 1)

            def project_y(g, b, half):
                if half == 0:
                    pe.wait_ge(kv_rdy.sem, kv_rdy.count(g, 2 * GB))
                    pe.wait_ge(qa_lo.sem, qa_lo.count(g, b + 1))
                for c in range(2 * half, 2 * half + 2):
                    for xp, wp in PASSES:
                        last = mm(AB[(4 + b) % 5][:, :], qas[:, xp, c, b * S:(b + 1) * S], w_out[:, wp, c, :],
                                  start=(c == 0 and (xp, wp) == PASSES[0]), stop=(c == KC - 1 and (xp, wp) == PASSES[-1]))
                if half == 1:
                    last.then_inc(y_ps.sem, 1)

            def turn_queries(g, b, turn):
                if turn == 0:
                    pe.wait_ge(qx_lo.sem, qx_lo.count(g, b + 1))
                    pe.wait_ge(qx_hi.sem, qx_hi.count(g, b + 1))
                    if b == 0:
                        pe.wait_ge(qa_rdy.sem, qa_rdy.count(g))
                    else:
                        pe.wait_ge(ex_rdy.sem, ex_rdy.count(g, KVH * b))
                else:
                    pe.wait_ge(mp_rdy.sem, mp_rdy.count(g, b + 1))
                    pe.wait_ge(qxT_a.sem, qxT_a.count(g, 2 * b + 1))
                    pe.wait_ge(qxT_b.sem, qxT_b.count(g, 2 * b + 1))
                for q in range(PAIRS):
                    dst = AB[1 + q // 8][:, :].bitcast(F16)[:, (q % 8) * P:(q % 8 + 1) * P]
                    last = pe.transpose(dst, Qx[:, 2 * q:2 * q + 2, :].rearrange("p h e -> p (h e)"), idb[:, :])
                    if q % 8 == 7:
                        last.then_inc(qxT_ps.sem, 1)

            def scores_for_max(g, b, u):
                n = KVH * b + u
                if u == 0:
                    pe.wait_ge(qxT_a.sem, qxT_a.count(g, 2 * b + 1))
                    odd = kx_b1 if b else kx_b0
                    pe.wait_ge(odd.sem, odd.count(g))
                    pe.wait_ge(x1_rdy.sem, x1_rdy.count(g, 1))
                if u % 4 == 0:
                    pe.wait_ge(kx_a.sem, kx_a.count(g, 2 * b + u // 4 + 1))
                if u == 4:
                    pe.wait_ge(qxT_b.sem, qxT_b.count(g, 2 * b + 1))
                if u >= 2:
                    pe.wait_ge(max_done.sem, max_done.count(g, n - 1))
                elif b >= 1:
                    pe.wait_ge(on_rdy.sem, on_rdy.count(g, 2 * b))
                for q in range(2):
                    last = mm(AB[3 + u % 2][:, q * 2 * P:(q + 1) * 2 * P], QxT[:, 2 * u + q, :],
                              kx[:, u, :, :].rearrange("p h t -> p (h t)"), start=True, stop=True)
                last.then_inc(sc_ps.sem, 1)

            def shifted_scores(g, b, u):
                n = KVH * b + u
                if u == 0:
                    pe.wait_ge(qxT_a.sem, qxT_a.count(g, 2 * b + 2))
                if u in (1, 4):
                    pe.wait_ge(qxT_b.sem, qxT_b.count(g, 2 * b + 2))
                if u >= 2:
                    pe.wait_ge(ex_rdy.sem, ex_rdy.count(g, n - 1))
                for a in range(2):
                    last = mm(AB[1 + u % 2][:, a * 2 * P:(a + 1) * 2 * P], kx[:, u, a, :],
                              QxT[:, 2 * u:2 * u + 2, :].rearrange("p q t -> p (q t)"), start=True, stop=True)
                last.then_inc(st_ps.sem, 1)

            def weigh_values(g, b, u):
                n = KVH * b + u
                if u == 0:
                    pe.wait_ge(v_lo.sem, v_lo.count(g, b + 1))
                    pe.wait_ge(max_done.sem, max_done.count(g, KVH * (b + 1)))
                low = ex_lo_v if n % 2 else ex_lo_p
                pe.wait_ge(low.sem, low.count(g, n // 2 + 1))
                pe.wait_ge(ex_hi.sem, ex_hi.count(g, n + 1))
                for a in range(2):
                    for q in range(2):
                        at = (HPG * (u % 4) + 2 * q + a) * (DH + 1)
                        out = AB[3 + u // 4][:, at:at + DH + 1]
                        cols = slice((a * 2 + q) * P, (a * 2 + q + 1) * P)
                        mm(out, exh[:, n % 2, cols], vx[:, u, 0:DH + 1], start=True, stop=False, skip_group_check=True)
                        mm(out[:, 0:DH], exh[:, n % 2, cols], vx[:, u, DH + 1:], start=False, stop=False, skip_group_check=True)
                        last = mm(out, exl[:, n % 2, cols], vx[:, u, 0:DH + 1], start=False, stop=True, skip_group_check=True)
                last.then_inc(pv_done.sem, 1)

            def adapter_and_router(g, b):
                pe.wait_ge(h3_lo.sem, h3_lo.count(g, b + 1))
                at = b * 2 * U1W
                for k in range(KC):
                    bs = slice(b * S, (b + 1) * S)
                    mm(AB[0][:, at:at + 2 * U1W], h3T[:, 0, k, bs], a1r[:, k, :, :].rearrange("p h w -> p (h w)"),
                       start=(k == 0), stop=False, skip_group_check=True)
                    last = mm(AB[0][:, at:at + U1W], h3T[:, 1, k, bs], a1r[:, k, 0, :], start=False, stop=(k == KC - 1), skip_group_check=True)
                last.then_inc(u1_ps.sem, 1)

            def turn_routing(g):
                pe.wait_ge(x2_rdy.sem, x2_rdy.count(g))
                pe.wait_ge(zz_rdy.sem, zz_rdy.count(g))
                for k in range(2):
                    for b in range(GB):
                        dst = AB[0][:, 0:T].bitcast(F16)[:, (k * GB + b) * S:(k * GB + b + 1) * S]
                        last = pe.transpose(dst, zz[:, b, k].rearrange("p h e -> p (h e)"), idb[:, :])
                last.then_inc(zT_ps.sem, 1)
                pe.wait_ge(drho_rdy.sem, drho_rdy.count(g))
                for b in range(GB):
                    last = mm(AB[1][:, b * S:(b + 1) * S], ones[:, :], drho[:, b, :], start=True, stop=True)
                last.then_inc(rho_ps.sem, 1)

            def hidden(g, c):
                if c == 0:
                    pe.wait_ge(h3_lo.sem, h3_lo.count(g))
                if HB_BEFORE[c] is not None:
                    pe.wait_ge(h2_rdy.sem, h2_rdy.count(g, HB_BEFORE[c] + 1))
                elif c in (0, 3) and not (isinstance(g, int) and g == 0):
                    pe.wait_ge(out_rdy.sem, out_rdy.count(g - 1, 1 if c == 0 else 2))
                cs = slice(c * P, (c + 1) * P)
                for k in range(KC):
                    for xp, wp in PASSES:
                        mm(HB[c][:, 0:T], w1[:, wp, k, cs], h3T[:, xp, k, :], start=(k == 0 and (xp, wp) == PASSES[0]), stop=False,
                           skip_group_check=True)

            def first_hidden(g, c):
                if c == 0:
                    pe.wait_ge(zT_rdy.sem, zT_rdy.count(g))
                    pe.wait_ge(rhoB_rdy.sem, rhoB_rdy.count(g))
                adapter_in(c, 0).then_inc(f1_ps.sem, 1)

            def adapter_in(c, k):
                cs = slice(c * P, (c + 1) * P)
                mm(HB[c][:, 0:T], lb1h[:, cs], zT[:, k, :], start=False, stop=False, skip_group_check=True)
                return mm(HB[c][:, 0:T], lb1l[:, cs], zT[0:ER, k, :], start=False, stop=True, skip_group_check=True)

            def second_hidden(g, c):
                pe.wait_ge(h1_rdy.sem, h1_rdy.count(g, c + 1))
                adapter_in(c, 1).then_inc(f2_ps.sem, 1)

            def down(c, at, hi, lo, first):
                mm(UB[:, at:at + 2 * ER], hi, a2[:, c, :, :].rearrange("p h e -> p (h e)"), start=first, stop=False, skip_group_check=True)
                return mm(UB[:, at:at + ER], lo, a2[:, c, 0, :], start=False, stop=(c == FC - 1), skip_group_check=True)

            def second_down(g, c):
                pe.wait_ge(t2_lo.sem, t2_lo.count(g, c + 1))
                pe.wait_ge(t2_hi.sem, t2_hi.count(g, c + 1))
                for b in range(GB):
                    bs = slice(b * S, (b + 1) * S)
                    last = down(c, b * 2 * ER, t2s[:, c % 2, 0, bs], t2s[:, c % 2, 1, bs], c == 0 and b == 0)
                last.then_inc(u2_used.sem, 1)

            def sum_down(g, c0, c1):
                if c0 == 0:
                    pe.wait_ge(u2_ev.sem, u2_ev.count(g))
                    pe.wait_ge(hs_lo.sem, hs_lo.count(g))
                    pe.wait_ge(hs_hi.sem, hs_hi.count(g))
                for c in range(c0, c1):
                    for b in range(GB):
                        bs = slice(b * S, (b + 1) * S)
                        last = down(c, (2 + b) * 2 * ER, hs[:, 0, c, bs], hs[:, 1, c, bs], c == 0 and b == 0)
                if c1 == FC:
                    last.then_inc(us_ps.sem, 1)

            def width_chunk(b, bank, c):
                for xp, wp in PASSES:
                    mm(bank[:, :], hs[:, xp, c, b * S:(b + 1) * S], w2[:, wp, c, :], start=(c == 0 and (xp, wp) == PASSES[0]), stop=False,
                       skip_group_check=True)

            def width_out(g, b, c):
                if b == 0 and c == 0:
                    pe.wait_ge(h2_rdy.sem, h2_rdy.count(g))
                    pe.wait_ge(hs_hi.sem, hs_hi.count(g))
                    pe.wait_ge(hs_lo.sem, hs_lo.count(g))
                width_chunk(b, FB[b], c)

            def width_out_last(g, c):
                pe.wait_ge(hs_hi.sem, hs_hi.count(g, c + 1))
                pe.wait_ge(hs_lo.sem, hs_lo.count(g, c + 1))
                for b in range(GB):
                    width_chunk(b, YL[b], c)

            def turn_z2(g):
                pe.wait_ge(z2_rdy.sem, z2_rdy.count(g))
                for b in range(GB):
                    dst = UB[:, 0:GB * S // 2].bitcast(F16)[:, b * S:(b + 1) * S]
                    last = pe.transpose(dst, z2s[:, b].rearrange("p h e -> p (h e)"), idb[:, :])
                last.then_inc(z2T_ps.sem, 1)

            def adapter_up(g, b, bank):
                pe.wait_ge(z2T_rdy.sem, z2T_rdy.count(g))
                mm(bank[:, :], z2T[:, b, :], lb2h[:, :], start=False, stop=False, skip_group_check=True)
                mm(bank[:, :], z2T[0:ER, b, :], lb2l[:, :], start=False, stop=True, skip_group_check=True).then_inc(yf_ps.sem, 1)

            def body(f, n):
                for c in range(FC + 2):
                    if f is not None:
                        if AHEAD <= c < FC:
                            hidden(f, c)
                        if c < FC:
                            first_hidden(f, c)
                        if c >= 3:
                            second_down(f, c - 3)
                        if 1 <= c <= FC:
                            second_hidden(f, c - 1)
                        if n is None and 4 <= c:
                            width_out_last(f, c - 4)
                    if n is not None:
                        if c == 3:
                            to_width(n, 0, xn_rdy, xnT_ps)
                            to_width(n, 1, xn_rdy, xnT_ps)
                        if 4 <= c < 8:
                            project_kv(n, (c - 4) // 2, c % 2)
                        if 8 <= c < 10:
                            project_q(n, 2 * (c - 8))
                            project_q(n, 2 * (c - 8) + 1)
                        if c in (11, 12):
                            project_y(n, 0, c - 11)
                        if c in (9, 11):
                            sum_tokens(n, (c - 9) // 2)
                        if c == 14:
                            project_y(n, 1, 0)
                            project_y(n, 1, 1)
                        if c == 15:
                            turn_queries(n, 0, 0)
                        if c >= 16:
                            for u in range(3 * (c - 16), 3 * (c - 15)):
                                scores_for_max(n, 0, u)
                w2_steps = iter([(b, j) for b in range(GB) for j in range(FC)])

                def w2_next(count):
                    for _ in range(count if f is not None else 0):
                        b, j = next(w2_steps)
                        width_out(f, b, j)
                        if j == FC - 1:
                            adapter_up(f, b, FB[b])

                if n is None:
                    second_down(f, FC - 1)
                    width_out_last(f, FC - 2)
                    sum_down(f, 0, FC)
                    width_out_last(f, FC - 1)
                    turn_z2(f)
                    for b in range(GB):
                        adapter_up(f, b, YL[b])
                    return
                if f is not None:
                    second_down(f, FC - 1)
                scores_for_max(n, 0, 6)
                scores_for_max(n, 0, 7)
                w2_next(W2_BESIDE[0])
                turn_queries(n, 0, 1)
                w2_next(W2_BESIDE[1])
                for u in range(KVH + 2):
                    if u < KVH:
                        shifted_scores(n, 0, u)
                    if u >= 2:
                        weigh_values(n, 0, u - 2)
                    if u < 2 and f is not None:
                        sum_down(f, FC // 2 * u, FC // 2 * (u + 1))
                    if u == 3 and f is not None:
                        turn_z2(f)
                    w2_next(W2_BESIDE[2][u])
                turn_queries(n, 1, 0)
                w2_next(W2_BESIDE[3])
                for u in range(KVH):
                    scores_for_max(n, 1, u)
                    w2_next(W2_BESIDE[4][u])
                turn_queries(n, 1, 1)
                w2_next(W2_BESIDE[5])
                for u in range(KVH + 2):
                    if u < KVH:
                        shifted_scores(n, 1, u)
                    if u >= 2:
                        weigh_values(n, 1, u - 2)
                    if u == 3:
                        to_width(n, 0, h3_rdy, h3T_ps)
                    if u == 7:
                        if f is None:
                            pe.wait_ge(s_lo, n_pieces)
                        adapter_and_router(n, 0)
                    w2_next(W2_BESIDE[6][u])
                w2_next(W2_BESIDE[7])
                to_width(n, 1, h3_rdy, h3T_ps)
                adapter_and_router(n, 1)
                for c in range(AHEAD):
                    hidden(n, c)
                turn_routing(n)

            body(None, 0)
            with pe.Fori(0, NG - 1) as i:
                body(i, i + 1)
            body(NG - 1, None)


N_SMALL = 11
NORM_STEPS = 8
N_PCONST = 8
N_CONST = 6 + NE + 2


def kernel(**inputs):
    import concourse.bacc as _bacc
    from concourse.bass_utils import run_bass_kernel_spmd as _run

    a = {k: np.asarray(v) for k, v in inputs.items()}
    inv = 1.0 / 10000.0 ** (np.arange(0, ROT, 2, dtype=np.float32) / np.float32(ROT))
    freqs = np.repeat(np.arange(S, dtype=np.float32)[:, None] * inv[None, :].astype(np.float32), 2, axis=-1)
    sign = np.where(np.arange(ROT) % 2 == 0, -1.0, 1.0).astype(np.float32)
    rep = (np.arange(P) // DH) % 4
    dim = np.arange(P) % DH
    kform = np.stack([SQ * (rep == 2), SQ * (rep < 3), SM * ((rep == 3) & (dim < 2))], axis=1).astype(np.float32)

    def columns(v):
        return v.reshape(-1, P).T

    feeds = [
        ("x", a["x"]),
        ("ctxT", a["ctx_512"].reshape(BATCH, S, KVH, DH).transpose(0, 3, 2, 1).reshape(BATCH, DH, KVH * S)),
        ("ctx", a["ctx_512"]),
        ("w_in", a["L0_attn_W_in"]), ("b_q", columns(a["L0_attn_b_in"][:D])), ("b_kv", a["L0_attn_b_in"][D:]),
        ("w_out", a["L0_attn_W_out"]), ("b_out", a["L0_attn_b_out"]),
        ("gamma", columns(a["L0_attn_gamma"])), ("beta", columns(a["L0_attn_beta"])),
        ("a1r", np.concatenate([a["L0_ffn_A1"].reshape(ER, D), a["L0_ffn_W_r"]], axis=0).T),
        ("b_r", a["L0_ffn_b_r"]),
        ("w1t", a["L0_ffn_W1"].T), ("b1", columns(a["L0_ffn_b1"])),
        ("w2t", a["L0_ffn_W2"].T), ("b2", a["L0_ffn_b2"]),
        ("b1t", a["L0_ffn_B1"].transpose(0, 2, 1).reshape(ER, F)),
        ("a2t", a["L0_ffn_A2"].reshape(ER, F).T),
        ("b2t", a["L0_ffn_B2"].transpose(0, 2, 1).reshape(ER, D)),
        ("cos", np.cos(freqs).astype(np.float32)), ("sin", (np.sin(freqs) * sign).astype(np.float32)),
        ("kform", kform),
    ]
    nc = _bacc.Bacc("TRN2", target_bir_lowering=False, num_devices=1)
    arrays, args = {}, []
    for name, v in feeds:
        v = np.ascontiguousarray(v)
        arrays[f"in_{name}"] = v
        args.append(nc.dram_tensor(f"in_{name}", v.shape, mybir.dt.from_np(v.dtype), kind="ExternalInput").ap())
    args.append(nc.dram_tensor("out_x", (BATCH, S, D), F32, kind="ExternalOutput").ap())
    build(nc, *args)
    return _run(nc, [arrays], core_ids=[0]).results[0]["out_x"]
```
